# Optimizing a Trainium2 kernel written in Bass

```python
import numpy as np
import jax
import jax.numpy as jnp

def _softmax(x, axis=-1):
    return jax.nn.softmax(x, axis=axis)

def _gelu(x):
    return jax.nn.gelu(x, approximate=True)

def _silu(x):
    return jax.nn.silu(x)

def _sigmoid(x):
    return jax.nn.sigmoid(x)

def _layernorm(x, axis=-1, eps=1e-05):
    m = jnp.mean(x, axis=axis, keepdims=True)
    v = jnp.var(x, axis=axis, keepdims=True)
    return (x - m) / jnp.sqrt(v + eps)

def _scatter_add(tgt, idx, src, axis=0):
    return tgt.at[idx].add(src)

def _segment_sum(src, seg, n):
    return jax.ops.segment_sum(src, seg, n)
kernel_name = 'mk_perceiver_d1_seqx_r4_7c4dc3'

def setup_inputs(seed: int=0):
    np.random.seed(seed)
    _w = jnp.asarray

    def _rec_inputs():
        import jax
        import jax.numpy as jnp
        _rk = jax.random.key(seed)
        x = 7.22e-05 + 1 * jax.random.normal(jax.random.fold_in(_rk, 1), (1, 128, 256), jnp.float32)
        _lenS = 128 - jax.random.randint(jax.random.fold_in(_rk, 7), (1,), 0, max(1, 128 // 4) + 1, jnp.int32)
        _lenS2 = 12544 - jax.random.randint(jax.random.fold_in(_rk, 8), (1,), 0, max(1, 12544 // 4) + 1, jnp.int32)
        _ctx_1024P = jax.random.normal(jax.random.fold_in(_rk, 11), (1, 16, 256), jnp.float32)
        _ctx_1024c = jax.random.dirichlet(jax.random.fold_in(_rk, 511), 0.3 * jnp.ones((16,), jnp.float32), (1, 12544))
        _ctx_1024t = jnp.einsum('bsk,bkd->bsd', _ctx_1024c, _ctx_1024P)
        _ctx_1024t = _ctx_1024t * jax.lax.rsqrt(jnp.mean(jnp.square(_ctx_1024t)) + 1e-12) * 0.953939
        ctx_1024 = -1.52775e-05 + 0.999936 * (_ctx_1024t + 0.3 * jax.random.normal(jax.random.fold_in(_rk, 611), (1, 12544, 256), jnp.float32))
        return (x, ctx_1024)
    x, ctx_1024 = _rec_inputs()

    def _L0_xattn_setup():
        import jax, jax.numpy as jnp
        import numpy as np
        HIDDEN = 256
        key = jax.random.key(seed)
        ks = jax.random.split(key, 8)
        s = 1.0 / np.sqrt(HIDDEN)
        return {'query': jax.random.normal(ks[0], (8, 256, HIDDEN), dtype=jnp.float32), 'ref': jax.random.normal(ks[1], (8, 1024, HIDDEN), dtype=jnp.float32), 'Wq': jax.random.normal(ks[2], (HIDDEN, HIDDEN), dtype=jnp.float32) * s, 'bq': jax.random.normal(ks[3], (HIDDEN,), dtype=jnp.float32) * s, 'Wk': jax.random.normal(ks[4], (HIDDEN, HIDDEN), dtype=jnp.float32) * s, 'bk': jax.random.normal(ks[5], (HIDDEN,), dtype=jnp.float32) * s, 'Wv': jax.random.normal(ks[6], (HIDDEN, HIDDEN), dtype=jnp.float32) * s, 'bv': jax.random.normal(ks[7], (HIDDEN,), dtype=jnp.float32) * s}
    _L0_xattn_all = _L0_xattn_setup()
    _L0_xattn_in = {k: v for k, v in _L0_xattn_all.items() if k in ('Wq', 'bq', 'Wk', 'bk', 'Wv', 'bv')}
    del _L0_xattn_all

    def _L0_attn_setup():
        import jax, jax.numpy as jnp
        import numpy as np
        HID = 256
        HK, HV = (4, 8)
        DK, DV = (128, 128)
        KEY_DIM = HK * DK
        VAL_DIM = HV * DV
        CONV_DIM = 2 * KEY_DIM + VAL_DIM
        KCONV = 4
        NEXP, TOPK, INTER = (8, 2, 128)
        EPS = 1e-06

        def zrms(x, w):
            v = jnp.mean(x * x, axis=-1, keepdims=True)
            return x * jax.lax.rsqrt(v + EPS) * (1.0 + w)

        def causal_dwconv(x, w):
            xp = jnp.pad(x, ((0, 0), (KCONV - 1, 0), (0, 0)))
            kern = w.T[:, None, :]
            return jax.lax.conv_general_dilated(xp, kern, (1,), 'VALID', dimension_numbers=('NHC', 'HIO', 'NHC'), feature_group_count=CONV_DIM)

        def gated_delta_rule(q, k, v, g, beta):
            B = q.shape[0]
            S0 = jnp.zeros((B, HV, DK, DV), q.dtype)

            def step(S, inp):
                qt, kt, vt, gt, bt = inp
                S = S * jnp.exp(gt)[..., None, None]
                kv = jnp.einsum('bhk,bhkv->bhv', kt, S)
                delta = (vt - kv) * bt[..., None]
                S = S + jnp.einsum('bhk,bhv->bhkv', kt, delta)
                o = jnp.einsum('bhk,bhkv->bhv', qt, S)
                return (S, o)
            xs = tuple((jnp.moveaxis(a, 1, 0) for a in (q, k, v, g, beta)))
            _, o = jax.lax.scan(step, S0, xs)
            return jnp.moveaxis(o, 0, 1)

        def _reference_tuple_inner(hidden_states, w_ln1, w_ln2, W_qkvz, W_ba, conv_w, dt_bias, A_log, gate_norm_w, W_out, W_router, W_gate_e, W_up_e, W_down_e):
            B, S, _ = hidden_states.shape
            resid = hidden_states
            x = zrms(hidden_states, w_ln1)
            qkvz = x @ W_qkvz
            q, k, v, z = jnp.split(qkvz, [KEY_DIM, 2 * KEY_DIM, 2 * KEY_DIM + VAL_DIM], axis=-1)
            b, a = jnp.split(x @ W_ba, 2, axis=-1)
            beta = jax.nn.sigmoid(b)
            g = -jnp.exp(A_log) * jax.nn.softplus(a + dt_bias)
            mixed = jnp.concatenate([q, k, v], axis=-1)
            mixed = jax.nn.silu(causal_dwconv(mixed, conv_w))
            q, k, v = jnp.split(mixed, [KEY_DIM, 2 * KEY_DIM], axis=-1)
            q = q.reshape(B, S, HK, DK)
            k = k.reshape(B, S, HK, DK)
            v = v.reshape(B, S, HV, DV)
            rep = HV // HK
            q = jnp.repeat(q, rep, axis=2)
            k = jnp.repeat(k, rep, axis=2)
            q = q * jax.lax.rsqrt(jnp.sum(q * q, -1, keepdims=True) + EPS)
            k = k * jax.lax.rsqrt(jnp.sum(k * k, -1, keepdims=True) + EPS)
            q = q * DK ** (-0.5)
            core = gated_delta_rule(q, k, v, g, beta)
            core = core * jax.lax.rsqrt(jnp.mean(core * core, -1, keepdims=True) + EPS) * gate_norm_w
            core = core * jax.nn.silu(z.reshape(B, S, HV, DV))
            h = resid + core.reshape(B, S, VAL_DIM) @ W_out
            resid = h
            x = zrms(h, w_ln2)
            probs = jax.nn.softmax(x @ W_router, axis=-1)
            topv, topi = jax.lax.top_k(probs, TOPK)
            topv = topv / jnp.sum(topv, -1, keepdims=True)
            route = jnp.sum(jax.nn.one_hot(topi, NEXP, dtype=x.dtype) * topv[..., None], axis=-2)
            gate_h = jnp.einsum('bsh,ehi->bsei', x, W_gate_e)
            up_h = jnp.einsum('bsh,ehi->bsei', x, W_up_e)
            exp_out = jnp.einsum('bsei,eih->bseh', jax.nn.silu(gate_h) * up_h, W_down_e)
            moe_out = jnp.einsum('bseh,bse->bsh', exp_out, route)
            return (resid + moe_out, topi)
        key = jax.random.key(seed)
        ks = jax.random.split(key, 12)

        def lin(k, shape, fan_in):
            return jax.random.normal(k, shape, jnp.float32) * fan_in ** (-0.5)
        return {'hidden_states': jax.random.normal(ks[0], (1, 512, HID), jnp.float32), 'w_ln1': jnp.zeros((HID,), jnp.float32), 'w_ln2': jnp.zeros((HID,), jnp.float32), 'W_qkvz': lin(ks[1], (HID, 2 * KEY_DIM + 2 * VAL_DIM), HID), 'W_ba': lin(ks[2], (HID, 2 * HV), HID), 'conv_w': jax.random.normal(ks[3], (CONV_DIM, KCONV), jnp.float32) * KCONV ** (-0.5), 'dt_bias': jax.random.normal(ks[4], (HV,), jnp.float32) * 0.1, 'A_log': jnp.log(jax.random.uniform(ks[5], (HV,), jnp.float32, 1.0, 16.0)), 'gate_norm_w': jnp.ones((DV,), jnp.float32), 'W_out': lin(ks[6], (VAL_DIM, HID), VAL_DIM), 'W_router': lin(ks[7], (HID, NEXP), HID), 'W_gate_e': lin(ks[8], (NEXP, HID, INTER), HID), 'W_up_e': lin(ks[9], (NEXP, HID, INTER), HID), 'W_down_e': lin(ks[10], (NEXP, INTER, HID), INTER)}
    _L0_attn_all = _L0_attn_setup()
    _L0_attn_in = {k: v for k, v in _L0_attn_all.items() if k in ('w_ln1', 'w_ln2', 'W_qkvz', 'W_ba', 'conv_w', 'dt_bias', 'A_log', 'gate_norm_w', 'W_out', 'W_router', 'W_gate_e', 'W_up_e', 'W_down_e')}
    del _L0_attn_all

    def _L0_ffn_setup():
        import jax, jax.numpy as jnp
        import numpy as np
        EMBED = 256
        D_FF = 4 * EMBED
        N_EXPERTS = 8
        TOP_K = 2
        B, S = (2, 256)
        key = jax.random.key(seed)
        ks = jax.random.split(key, 10)
        sc_d = 1.0 / np.sqrt(EMBED)
        sc_h = 1.0 / np.sqrt(D_FF)
        return {'inputs': jax.random.normal(ks[0], (B, S, EMBED), jnp.float32), 'rw1': jax.random.normal(ks[1], (EMBED, D_FF), jnp.float32) * sc_d, 'rb1': jnp.zeros((D_FF,), jnp.float32), 'rw2': jax.random.normal(ks[2], (D_FF, N_EXPERTS), jnp.float32) * sc_h, 'rb2': jnp.zeros((N_EXPERTS,), jnp.float32), 'W1': jax.random.normal(ks[3], (N_EXPERTS, EMBED, D_FF), jnp.float32) * sc_d, 'b1': jnp.zeros((N_EXPERTS, D_FF), jnp.float32), 'W2': jax.random.normal(ks[4], (N_EXPERTS, D_FF, EMBED), jnp.float32) * sc_h, 'b2': jnp.zeros((N_EXPERTS, EMBED), jnp.float32)}
    _L0_ffn_all = _L0_ffn_setup()
    _L0_ffn_in = {k: v for k, v in _L0_ffn_all.items() if k in ('rw1', 'rb1', 'rw2', 'rb2', 'W1', 'b1', 'W2', 'b2')}
    del _L0_ffn_all
    return {'x': x, 'ctx_1024': ctx_1024, 'L0_xattn_Wq': _L0_xattn_in['Wq'], 'L0_xattn_bq': _L0_xattn_in['bq'], 'L0_xattn_Wk': _L0_xattn_in['Wk'], 'L0_xattn_bk': _L0_xattn_in['bk'], 'L0_xattn_Wv': _L0_xattn_in['Wv'], 'L0_xattn_bv': _L0_xattn_in['bv'], 'L0_attn_w_ln1': _L0_attn_in['w_ln1'], 'L0_attn_w_ln2': _L0_attn_in['w_ln2'], 'L0_attn_W_qkvz': _L0_attn_in['W_qkvz'], 'L0_attn_W_ba': _L0_attn_in['W_ba'], 'L0_attn_conv_w': _L0_attn_in['conv_w'], 'L0_attn_dt_bias': _L0_attn_in['dt_bias'], 'L0_attn_A_log': _L0_attn_in['A_log'], 'L0_attn_gate_norm_w': _L0_attn_in['gate_norm_w'], 'L0_attn_W_out': _L0_attn_in['W_out'], 'L0_attn_W_router': _L0_attn_in['W_router'], 'L0_attn_W_gate_e': _L0_attn_in['W_gate_e'], 'L0_attn_W_up_e': _L0_attn_in['W_up_e'], 'L0_attn_W_down_e': _L0_attn_in['W_down_e'], 'L0_ffn_rw1': _L0_ffn_in['rw1'], 'L0_ffn_rb1': _L0_ffn_in['rb1'], 'L0_ffn_rw2': _L0_ffn_in['rw2'], 'L0_ffn_rb2': _L0_ffn_in['rb2'], 'L0_ffn_W1': _L0_ffn_in['W1'], 'L0_ffn_b1': _L0_ffn_in['b1'], 'L0_ffn_W2': _L0_ffn_in['W2'], 'L0_ffn_b2': _L0_ffn_in['b2']}

def reference(x, ctx_1024, L0_xattn_Wq, L0_xattn_bq, L0_xattn_Wk, L0_xattn_bk, L0_xattn_Wv, L0_xattn_bv, L0_attn_w_ln1, L0_attn_w_ln2, L0_attn_W_qkvz, L0_attn_W_ba, L0_attn_conv_w, L0_attn_dt_bias, L0_attn_A_log, L0_attn_gate_norm_w, L0_attn_W_out, L0_attn_W_router, L0_attn_W_gate_e, L0_attn_W_up_e, L0_attn_W_down_e, L0_ffn_rw1, L0_ffn_rb1, L0_ffn_rw2, L0_ffn_rb2, L0_ffn_W1, L0_ffn_b1, L0_ffn_W2, L0_ffn_b2):
    import jax
    import jax.numpy as jnp

    def _L0_xattn_ref(query, ref, Wq, bq, Wk, bk, Wv, bv):
        import jax, jax.numpy as jnp
        import numpy as np
        HIDDEN = 256
        norm_fact = 1.0 / np.sqrt(HIDDEN).astype(np.float32)
        Q = query @ Wq + bq
        K = ref @ Wk + bk
        V = ref @ Wv + bv
        scores = jnp.einsum('bqh,bkh->bqk', Q, K)
        attn = jax.nn.softmax(scores, axis=-1) * norm_fact
        return jnp.einsum('bqk,bkh->bqh', attn, V)

    def _L0_attn_ref(hidden_states, w_ln1, w_ln2, W_qkvz, W_ba, conv_w, dt_bias, A_log, gate_norm_w, W_out, W_router, W_gate_e, W_up_e, W_down_e):
        import jax, jax.numpy as jnp
        import numpy as np
        HID = 256
        HK, HV = (4, 8)
        DK, DV = (128, 128)
        KEY_DIM = HK * DK
        VAL_DIM = HV * DV
        CONV_DIM = 2 * KEY_DIM + VAL_DIM
        KCONV = 4
        NEXP, TOPK, INTER = (8, 2, 128)
        EPS = 1e-06

        def zrms(x, w):
            v = jnp.mean(x * x, axis=-1, keepdims=True)
            return x * jax.lax.rsqrt(v + EPS) * (1.0 + w)

        def causal_dwconv(x, w):
            xp = jnp.pad(x, ((0, 0), (KCONV - 1, 0), (0, 0)))
            kern = w.T[:, None, :]
            return jax.lax.conv_general_dilated(xp, kern, (1,), 'VALID', dimension_numbers=('NHC', 'HIO', 'NHC'), feature_group_count=CONV_DIM)

        def gated_delta_rule(q, k, v, g, beta):
            B = q.shape[0]
            S0 = jnp.zeros((B, HV, DK, DV), q.dtype)

            def step(S, inp):
                qt, kt, vt, gt, bt = inp
                S = S * jnp.exp(gt)[..., None, None]
                kv = jnp.einsum('bhk,bhkv->bhv', kt, S)
                delta = (vt - kv) * bt[..., None]
                S = S + jnp.einsum('bhk,bhv->bhkv', kt, delta)
                o = jnp.einsum('bhk,bhkv->bhv', qt, S)
                return (S, o)
            xs = tuple((jnp.moveaxis(a, 1, 0) for a in (q, k, v, g, beta)))
            _, o = jax.lax.scan(step, S0, xs)
            return jnp.moveaxis(o, 0, 1)

        def _reference_tuple_inner(hidden_states, w_ln1, w_ln2, W_qkvz, W_ba, conv_w, dt_bias, A_log, gate_norm_w, W_out, W_router, W_gate_e, W_up_e, W_down_e):
            B, S, _ = hidden_states.shape
            resid = hidden_states
            x = zrms(hidden_states, w_ln1)
            qkvz = x @ W_qkvz
            q, k, v, z = jnp.split(qkvz, [KEY_DIM, 2 * KEY_DIM, 2 * KEY_DIM + VAL_DIM], axis=-1)
            b, a = jnp.split(x @ W_ba, 2, axis=-1)
            beta = jax.nn.sigmoid(b)
            g = -jnp.exp(A_log) * jax.nn.softplus(a + dt_bias)
            mixed = jnp.concatenate([q, k, v], axis=-1)
            mixed = jax.nn.silu(causal_dwconv(mixed, conv_w))
            q, k, v = jnp.split(mixed, [KEY_DIM, 2 * KEY_DIM], axis=-1)
            q = q.reshape(B, S, HK, DK)
            k = k.reshape(B, S, HK, DK)
            v = v.reshape(B, S, HV, DV)
            rep = HV // HK
            q = jnp.repeat(q, rep, axis=2)
            k = jnp.repeat(k, rep, axis=2)
            q = q * jax.lax.rsqrt(jnp.sum(q * q, -1, keepdims=True) + EPS)
            k = k * jax.lax.rsqrt(jnp.sum(k * k, -1, keepdims=True) + EPS)
            q = q * DK ** (-0.5)
            core = gated_delta_rule(q, k, v, g, beta)
            core = core * jax.lax.rsqrt(jnp.mean(core * core, -1, keepdims=True) + EPS) * gate_norm_w
            core = core * jax.nn.silu(z.reshape(B, S, HV, DV))
            h = resid + core.reshape(B, S, VAL_DIM) @ W_out
            resid = h
            x = zrms(h, w_ln2)
            probs = jax.nn.softmax(x @ W_router, axis=-1)
            topv, topi = jax.lax.top_k(probs, TOPK)
            topv = topv / jnp.sum(topv, -1, keepdims=True)
            route = jnp.sum(jax.nn.one_hot(topi, NEXP, dtype=x.dtype) * topv[..., None], axis=-2)
            gate_h = jnp.einsum('bsh,ehi->bsei', x, W_gate_e)
            up_h = jnp.einsum('bsh,ehi->bsei', x, W_up_e)
            exp_out = jnp.einsum('bsei,eih->bseh', jax.nn.silu(gate_h) * up_h, W_down_e)
            moe_out = jnp.einsum('bseh,bse->bsh', exp_out, route)
            return (resid + moe_out, topi)
        return _reference_tuple_inner(hidden_states, w_ln1, w_ln2, W_qkvz, W_ba, conv_w, dt_bias, A_log, gate_norm_w, W_out, W_router, W_gate_e, W_up_e, W_down_e)[0]

    def _L0_ffn_ref(inputs, rw1, rb1, rw2, rb2, W1, b1, W2, b2):
        import jax, jax.numpy as jnp
        import numpy as np
        EMBED = 256
        D_FF = 4 * EMBED
        N_EXPERTS = 8
        TOP_K = 2
        B, S = (2, 256)
        Bb, Ss, D = inputs.shape
        T = Bb * Ss
        xf = inputs.reshape(T, D)
        score = jax.nn.relu(xf @ rw1 + rb1) @ rw2 + rb2
        _, topi = jax.lax.top_k(score, TOP_K)
        mask = jnp.zeros(score.shape, bool).at[jnp.arange(T)[:, None], topi].set(True)
        gate = jax.nn.softmax(jnp.where(mask, score, -jnp.inf), axis=-1)
        out = jnp.zeros_like(xf)
        for e in range(N_EXPERTS):
            h = jax.nn.relu(xf @ W1[e] + b1[e])
            y = h @ W2[e] + b2[e]
            out = out + gate[:, e:e + 1] * y
        return out.reshape(Bb, Ss, D)
    x = x + _L0_xattn_ref(_layernorm(x, axis=-1), ctx_1024, L0_xattn_Wq, L0_xattn_bq, L0_xattn_Wk, L0_xattn_bk, L0_xattn_Wv, L0_xattn_bv)
    x = x + _L0_attn_ref(_layernorm(x, axis=-1), L0_attn_w_ln1, L0_attn_w_ln2, L0_attn_W_qkvz, L0_attn_W_ba, L0_attn_conv_w, L0_attn_dt_bias, L0_attn_A_log, L0_attn_gate_norm_w, L0_attn_W_out, L0_attn_W_router, L0_attn_W_gate_e, L0_attn_W_up_e, L0_attn_W_down_e)
    x = x + _L0_ffn_ref(_layernorm(x, axis=-1), L0_ffn_rw1, L0_ffn_rb1, L0_ffn_rw2, L0_ffn_rb2, L0_ffn_W1, L0_ffn_b1, L0_ffn_W2, L0_ffn_b2)
    return x

_drawn_inputs = setup_inputs


def setup_inputs(seed=0):
    import zlib

    import numpy as np

    out = dict(_drawn_inputs(seed))
    spreads = {'L0_attn_w_ln1': (0.0, 0.1),
     'L0_attn_w_ln2': (0.0, 0.1),
     'L0_attn_gate_norm_w': (1.0, 0.2),
     'L0_ffn_rb1': (0.0, 0.1),
     'L0_ffn_rb2': (0.0, 0.1),
     'L0_ffn_b1': (0.0, 0.344),
     'L0_ffn_b2': (0.0, 0.1)}
    factors = {'L0_xattn_bk': 64.0, 'L0_xattn_bv': 3.258, 'L0_attn_dt_bias': 2.728}
    for name, (base, spread) in spreads.items():
        noise = np.random.default_rng([zlib.crc32(name.encode()), seed]).standard_normal(out[name].shape)
        drawn = base * np.exp(spread * noise) if base else spread * noise
        out[name] = jnp.asarray(drawn.astype(out[name].dtype))
    for name, factor in factors.items():
        out[name] = (out[name] * factor).astype(out[name].dtype)
    return out
```

```python
from contextlib import ExitStack

import concourse.bass as bass
from concourse import mybir

P = 128
T = 128
D = 256
DC = D // P
S = 12544
GT = 7
NG = S // P // GT
RING = 4
GK = GT * P
HALF = GK // 2
NC = DC * GT
HK, HV = 4, 8
KEY, VAL = HK * P, HV * P
CONV = 2 * KEY + VAL
NCH = CONV // P
E = 8
FF = 1024
FC = FF // P
SLOTS = 4
LEVELS = 7
CTX_BANKS = (0, 1, 7, 0)
LN_EPS, RMS_EPS = 1e-5, 1e-6
NORM = 1.0 / 16.0

F32 = mybir.dt.float32
F32R = mybir.dt.float32r
U32 = mybir.dt.uint32
ALU = mybir.AluOpType
ACT = mybir.ActivationFunctionType
AX = mybir.AxisListType.X


def columns(sizes):
    at, out = 0, {}
    for name, n in sizes:
        out[name] = (at, at + n)
        at += n
    return out, at


EARLY, EARLY_N = columns([
    ("x", D), ("ident", P), ("w_ln1", DC), ("w_ln2", DC), ("bq", DC), ("bk", DC),
    ("wq", DC * D), ("wkT", DC * D), ("wv", DC * D),
    ("tri", P), ("strict", P), ("negmask", P), ("m0", P // 2),
    ("masks", 64 * (LEVELS - 1)), ("iota", E), ("ones", 1),
    ("conv_w", 4 * NCH), ("gate_norm", 1),
    ("rb1", FC), ("b1", E * FC), ("dt_bias", HV), ("A_log", HV), ("rb2", E)])
EARLY_SPLIT = EARLY["wq"][0]
LATE, LATE_USED = columns([
    ("qkvz", DC * (CONV + VAL)), ("ba", DC * 2 * HV), ("out", HV * D), ("gate", DC * E * P),
    ("up", DC * E * P), ("down", E * D), ("router", DC * E), ("rw1", DC * FF), ("rw2", FC * E)])
EXPERT_N = DC * FF + FC * D
LATE_PARTS = NG - RING
EARLY_SLOTS = 2
PART_N = -(-(LATE_USED + EARLY_SLOTS * EXPERT_N) // LATE_PARTS)
LATE_N = PART_N * LATE_PARTS
assert NG * GK == S


def perceiver(nc, early, late, experts, ctx, bv, b2, out):
    with ExitStack() as stack:
        def sb(name, cols, dt=F32, rows=P):
            return stack.enter_context(nc.sbuf_tensor(name, [rows, cols], dt))

        def sem(name):
            return stack.enter_context(nc.semaphore(name))

        E_sb = sb("early_sb", EARLY_N)
        W_sb = sb("late_sb", LATE_N)
        R1 = sb("ring", RING * GT * D)
        def parts(overlay, name, cols):
            return [overlay.enter_context(nc.sbuf_tensor(f"{name}_{part}", [P, cols], F32R)) for part in ("hi", "lo")]

        with ExitStack() as overlay:
            ctxN = parts(overlay, "ctx", 2 * GT * D)
        late_slots = sb("late_slots", (SLOTS - EARLY_SLOTS) * EXPERT_N)
        with ExitStack() as overlay:
            ctxT = parts(overlay, "ctxT", NC * P)
            G = parts(overlay, "G", D)
            PT = parts(overlay, "probsT", GK)
        R2 = sb("work", 8192)
        bv_sb = R2[0:1, 7296:7552]
        sixteenth = R2[0:1, 7552:7552 + P]
        gateT = R2[0:E, 2048:2048 + P]
        b2_sb = sb("b2_sb", D, rows=E)
        psum = stack.enter_context(nc.psum_tensor("psum", [P, 8, 512], F32))
        bank = [psum[:, i, :] for i in range(8)]

        def early_at(name):
            a, b = EARLY[name]
            return E_sb[:, a:b]

        def late_at(name, **kw):
            a, b = LATE[name]
            return W_sb[:, a:b].rearrange("p (c n) -> p c n", **kw)

        x = early_at("x")
        ident = early_at("ident")
        tri = early_at("tri")
        strict = early_at("strict")
        negmask = early_at("negmask")
        m0 = early_at("m0")
        masks = early_at("masks").rearrange("p (l c) -> p l c", c=64)
        ones = early_at("ones")
        conv_w = early_at("conv_w").rearrange("p (c j) -> p c j", j=4)
        wq = early_at("wq").rearrange("p (c n) -> p c n", c=DC)
        wkT = early_at("wkT").rearrange("p (c n) -> p c n", c=DC)
        wv = early_at("wv").rearrange("p (c n) -> p c n", c=DC)
        w_qkvz = late_at("qkvz", c=DC)
        w_ba = late_at("ba", c=DC)
        w_out = late_at("out", c=HV)
        w_gate = late_at("gate", c=DC)
        w_up = late_at("up", c=DC)
        w_down = late_at("down", c=E)
        w_router = late_at("router", c=DC)
        rw1 = late_at("rw1", c=DC)
        rw2 = late_at("rw2", c=FC)
        slots = [W_sb[:, LATE_USED + j * EXPERT_N:LATE_USED + (j + 1) * EXPERT_N] for j in range(EARLY_SLOTS)]
        slots += [late_slots[:, bass.ts(j, EXPERT_N)] for j in range(SLOTS - EARLY_SLOTS)]

        ring = R1[:, :].rearrange("p (r t d) -> p r t d", r=RING, d=D)
        ctxTv = [part[:, :].rearrange("p (c k) -> p c k", c=DC) for part in ctxT]
        probs = R2[:, 5888:5888 + GK]
        ctxNv = [part[:, :].rearrange("p (b t d) -> p b t d", b=2, d=D) for part in ctxN]
        probsT = [part[:, :].rearrange("p (t q) -> p t q", q=T) for part in PT]
        AW = R1[:, 0:2048].rearrange("p (h a t) -> p h a t", h=HV, a=2)
        DT = R1[:, 2048:3072].rearrange("p (h t) -> p h t", h=HV)
        gstrict = R1[:, 3072:4096].rearrange("p (h t) -> p h t", h=HV)
        X = R1[:, 4096:5120].rearrange("p (h t) -> p h t", h=HV)
        Y = R1[:, 5120:6144].rearrange("p (h t) -> p h t", h=HV)
        Bv = R1[:, 6144:7168].rearrange("p (h t) -> p h t", h=HV)
        qkvT = R2[:, 0:2048].rearrange("p (c t) -> p c t", c=NCH)
        squares = R2[:, 2048:3072].rearrange("p (c t) -> p c t", c=2 * HK)
        zs = R2[:, 3072:4096].rearrange("p (h t) -> p h t", h=HV)
        steps = [R2[:, 4096 + 1024 * i:5120 + 1024 * i].rearrange("p (h t) -> p h t", h=HV) for i in range(2)]
        delta = R2[:, 6144:7168].rearrange("p (h t) -> p h t", h=HV)
        core = R2[:, 7168:8192].rearrange("p (h t) -> p h t", h=HV)
        coreT = R1[:, 2048:3072].rearrange("p (h t) -> p h t", h=HV)
        gact = R1[:, 0:1024].rearrange("p (e i) -> p e i", e=E)
        prod = R1[:, 1024:2048].rearrange("p (e i) -> p e i", e=E)
        prodT = R1[:, 3072:4096].rearrange("p (e i) -> p e i", e=E)
        relT = R2[:, 0:1024].rearrange("p (c t) -> p c t", c=FC)
        hT = [R2[:, 4096 + 1024 * i:5120 + 1024 * i].rearrange("p (c t) -> p c t", c=FC) for i in range(2)]

        xn = sb("xn", D)
        xT = sb("xT", D)
        QT = R2[:, 6784:7040]
        OT = R2[:, 7040:7296]
        scratch = R2[:, 7680:7936]
        hh = sb("hh", D)
        O = sb("O", D)
        xb = sb("xb", D)
        x1 = sb("x1", D)
        h0, xh = x, xb
        smalls, SMALL_N = columns([
            ("stats", 6), ("mv", 2), ("sd", 2), ("rs", 2), ("qb", 1), ("M", 2), ("mx", 1), ("nb", 1), ("dm", 2),
            ("al", 2), ("rowsum", 2), ("l", 1), ("rl", 1), ("w1p", DC), ("w2p", DC), ("negA", HV), ("beta", HV),
            ("u", HV), ("au", HV), ("sp", HV), ("g", HV), ("ba", 2 * HV), ("n2", 2 * HK), ("kap", HV), ("ki", HK), ("kn", HK), ("eq", HK),
            ("ms", HV), ("f", HV), ("lg", E), ("top", 8), ("w", 2), ("th", 1), ("idf", 8), ("e1", E), ("e2", E),
            ("route", E), ("gate", E), ("eps", 4), ("dummy", 8)])
        sm = sb("smalls", SMALL_N)
        topi = sb("topi", 8, U32)

        def s_(name, a=0, b=None):
            lo, hi = smalls[name]
            return sm[:, lo + a:(hi if b is None else lo + b)]

        names = """early_in rows_in late_in out_done
            consts_set eps_set
            early2_in dve_chain act_chain steps_zeroed y_free credit mx_done dm_done l_done exp_tab m_done y_ident cleared
            ln_var ln_sd ln_xn ln_T ln_xT q_ready q_done g_ready g_done qb_done bv_ready
            ctx_transposed ctxT_hi ctxT_lo ctx_hi ctx_lo probsT_hi scores_ready max_ready exp_done alpha_done probs_transposed probsT_lo pv_done acc_done
            o_T o_copied att_ready
            var1_done sd1_done xz_done xz_T xz_copied ba_done ba_read softplus_in u_ready eau_done ln1p_done g_done2 gs_done
            proj_bank tap0_done conv_done silu_done z_done zs_done
            beta_done sq_done n2_done n2_read kn_in kn_done decay_done dt_done gram_done aw_done vT_done bv_done
            y_init x_T x_init t_mm t_done xy_mm xy_done delta_mm delta_done o_mm osq_done ms_done f_sd core_done core_T coreT_done
            out_mm h_done hsq_done hsd_done x2_done x2_T x2_copied lg_mm th_in th_done route_done gu_mm gact_done prod_done prod_T prodT_done
            moe_mm x3_done ln3_sd xf_done xf_T xf_copied r1_mm rel_done sc_mm sc_in sc_th gate_done gate_T gateT_done b2_mm acc_init
            h_mm hT_done hT2_done y_mm y_added h0_done""".split()
        s = {n: sem(n) for n in names}
        ctx_in = [sem(f"ctx_in{r}") for r in range(RING)]
        slot_in = [sem(f"slot_in{r}") for r in range(SLOTS)]

        block = stack.enter_context(nc.Block())

        @block.sync
        def _(sp):
            sp.dma_start(E_sb[:, 0:EARLY_SPLIT], early[:, 0:EARLY_SPLIT]).then_inc(s["early_in"], 16)
            sp.dma_start(E_sb[:, EARLY_SPLIT:EARLY_N], early[:, EARLY_SPLIT:EARLY_N]).then_inc(s["early2_in"], 16)
            sp.dma_start(bv_sb[:, :], bv).then_inc(s["rows_in"], 16)
            sp.dma_start(b2_sb[:, :], b2).then_inc(s["rows_in"], 16)

            ctx_g = ctx.rearrange("(p g t) d -> p g (t d)", p=P, g=NG)
            R1g = R1[:, :].rearrange("p (r n) -> p r n", r=RING)

            def group(g, r):
                sp.dma_start(R1g[:, r, :], ctx_g[:, g, :]).then_inc(ctx_in[r], 16)

            def part(i):
                sp.dma_start(W_sb[:, bass.ts(i, PART_N)], late[i, :, :]).then_inc(s["late_in"], 16)

            for r in range(RING):
                group(r, r)
            with sp.Fori(0, 2) as i:
                for r in range(RING):
                    part(i * RING + r)
                    sp.wait_ge(s["ctx_lo"], i * RING + (r + 1))
                    group(i * RING + (RING + r), r)
            for r in range(2):
                part(2 * RING + r)
                sp.wait_ge(s["ctx_lo"], 2 * RING + r + 1)
                group(3 * RING + r, r)
            sp.wait_ge(s["pv_done"], NG)
            for j in range(EARLY_SLOTS, SLOTS):
                sp.dma_start(slots[j], experts[j - EARLY_SLOTS, :, :]).then_inc(slot_in[j], 16)
            for j in range(SLOTS):
                sp.wait_ge(s["y_mm"], j + 3)
                sp.dma_start(slots[j], experts[SLOTS - EARLY_SLOTS + j, :, :]).then_inc(slot_in[j], 16)
            sp.wait_ge(s["m_done"], 1)
            sp.dma_start(out, O[:, :]).then_inc(s["out_done"], 16)
            sp.wait_ge(s["out_done"], 16)

        @block.gpsimd
        def _(pool):
            nc.gpsimd.memset(s_("eps", 0, 1), LN_EPS).then_inc(s["eps_set"], 1)
            nc.gpsimd.memset(s_("eps", 1, 2), LN_EPS * RMS_EPS).then_inc(s["eps_set"], 1)
            nc.gpsimd.memset(s_("eps", 2, 3), RMS_EPS).then_inc(s["eps_set"], 1)
            nc.gpsimd.memset(s_("eps", 3, 4), 1.0).then_inc(s["eps_set"], 1)
            nc.gpsimd.memset(sixteenth[:, :], NORM).then_inc(s["consts_set"], 1)
            nc.gpsimd.memset(O[:, :], 0.0).then_inc(s["consts_set"], 1)
            nc.gpsimd.memset(s_("l"), 0.0).then_inc(s["consts_set"], 1)
            nc.gpsimd.memset(s_("M", 0, 1), -3e38).then_inc(s["consts_set"], 1)
            def ctx_lo_parts(g, r):
                pool.wait_ge(s["ctx_hi"], g + 1)
                nc.gpsimd.tensor_tensor(ctxNv[1][:, r % 2], ring[:, r], ctxNv[0][:, r % 2], ALU.subtract).then_inc(s["ctx_lo"], 1)

            with pool.Fori(0, 3) as i:
                for j in range(RING):
                    ctx_lo_parts(i * RING + j, j)
            for g in range(3 * RING, NG):
                ctx_lo_parts(g, g % RING)
            pool.wait_ge(s["pv_done"], NG)
            pool.wait_ge(s["early_in"], 16)
            nc.gpsimd.tensor_copy(Y, ident.rearrange("p (a t) -> p a t", a=1).to_broadcast([P, HV, P])).then_inc(s["y_ident"], 1)
            for i in range(2):
                nc.gpsimd.memset(steps[i], 0.0).then_inc(s["steps_zeroed"], 1)
            for lv in range(3, LEVELS):
                pool.wait_ge(s["xy_mm"], 2 * (lv - 2))
                nc.gpsimd.memset(steps[lv % 2], 0.0).then_inc(s["steps_zeroed"], 1)

        @block.tensor
        def _(pe):
            def transposes(pairs, done):
                for o, i in pairs:
                    last = nc.tensor.transpose(o, i, ident)
                last.then_inc(done, 1)

            def wide(o, lhs, rhs, n=DC):
                for c in range(n):
                    last = nc.tensor.matmul(o, lhs(c), rhs(c), start=(c == 0), stop=(c == n - 1))
                return last

            def half(t, c):
                return t[:, c * P:(c + 1) * P]

            pe.wait_ge(s["early_in"], 16)
            pe.wait_ge(s["ln_xn"], 1)
            transposes([(half(bank[0], c), half(xn, c)) for c in range(DC)], s["ln_T"])
            pe.wait_ge(s["rows_in"], 32)
            pe.wait_ge(s["early2_in"], 16)
            pe.wait_ge(s["consts_set"], 4)
            nc.tensor.matmul(bank[3][:, 0:D], sixteenth[:, :], bv_sb[:, :], start=True, stop=True).then_inc(s["bv_ready"], 1)
            pe.wait_ge(s["ln_xT"], 1)
            for m in range(DC):
                last = wide(half(bank[1], m), lambda c: wq[:, c, m * P:(m + 1) * P], lambda c: half(xT, c))
            last.then_inc(s["q_ready"], 1)
            pe.wait_ge(s["q_done"], 2)
            for m in range(DC):
                wide(half(bank[2], m), lambda c: wkT[:, c, m * P:(m + 1) * P], lambda c: half(QT, c))
            a = EARLY["bk"][0]
            wide(bank[2][:, D:D + 1], lambda c: half(QT, c), lambda c: E_sb[:, a + c:a + c + 1]).then_inc(s["g_ready"], 1)

            def ctx_transposes(g, r, quads):
                for q in quads:
                    if q == 3:
                        pe.wait_ge(s["ctxT_lo"], g * 4 + 1)
                    blocks = range(4 * q, min(4 * q + 4, NC))
                    transposes([(bank[CTX_BANKS[q]][:, (b % 4) * P:(b % 4 + 1) * P],
                                 ring[:, r, b % GT, (b // GT) * P:(b // GT + 1) * P]) for b in blocks],
                               s["ctx_transposed"])

            def scores(g, first=False):
                if not first:
                    pe.wait_ge(s["exp_done"], g)
                for hf in range(2):
                    pe.wait_ge(s["ctxT_lo"], g * 4 + (3 + hf))
                    terms = [(a, b, c) for a, b in ((0, 0), (1, 0), (0, 1)) for c in range(DC)]
                    for i, (a, b, c) in enumerate(terms):
                        last = nc.tensor.matmul(bank[2 + hf][:, 0:HALF], G[a][:, c * P:(c + 1) * P],
                                                ctxTv[b][:, c, hf * HALF:(hf + 1) * HALF], start=(i == 0), stop=(i == len(terms) - 1))
                last.then_inc(s["scores_ready"], 1)

            def probs_transposes(g, first=False):
                pe.wait_ge(s["exp_done"], g + 1)
                if not first:
                    pe.wait_ge(s["probsT_lo"], g * 2)
                for q, tiles in ((0, range(0, 4)), (1, range(4, 7))):
                    transposes([(bank[4 + q][:, (t % 4) * P:(t % 4 + 1) * P], probs[:, t * P:(t + 1) * P]) for t in tiles],
                               s["probs_transposed"])

            def attend(g, r, first=False):
                if not first:
                    pe.wait_ge(s["acc_done"], g + 1)
                pe.wait_ge(s["probsT_lo"], g * 2 + 2)
                pe.wait_ge(s["ctx_lo"], g + 1)
                terms = [(t, a, b) for a, b in ((0, 0), (1, 0), (0, 1)) for t in range(GT)]
                for i, (t, a, b) in enumerate(terms):
                    last = nc.tensor.matmul(bank[6][:, 0:D], probsT[a][:, t, :], ctxNv[b][:, r % 2, t, :],
                                            start=(i == 0), stop=(i == len(terms) - 1))
                last.then_inc(s["pv_done"], 1)

            pe.wait_ge(ctx_in[0], 16)
            ctx_transposes(0, 0, range(4))
            pe.wait_ge(s["g_done"], 3)
            scores(0, first=True)
            pe.wait_ge(ctx_in[1], 16)
            ctx_transposes(1, 1, range(4))
            probs_transposes(0, first=True)
            with pe.Fori(0, 3) as i:
                for j in range(RING):
                    g = i * RING + (j + 1)
                    scores(g)
                    r = (j + 2) % RING
                    pe.wait_ge(ctx_in[r], i * 16 + (32 if j >= 2 else 16))
                    ctx_transposes(i * RING + (j + 2), r, range(3))
                    attend(i * RING + j, j)
                    ctx_transposes(i * RING + (j + 2), r, [3])
                    probs_transposes(g)
            scores(NG - 1)
            attend(NG - 2, (NG - 2) % RING)
            probs_transposes(NG - 1)
            attend(NG - 1, (NG - 1) % RING)
            pe.wait_ge(s["acc_done"], NG + 1)
            transposes([(half(bank[0], c), half(O, c)) for c in range(DC)], s["o_T"])
            pe.wait_ge(s["o_copied"], 1)
            wide(bank[1][:, 0:D], lambda c: half(OT, c), lambda c: wv[:, c, :]).then_inc(s["att_ready"], 1)

            pe.wait_ge(s["late_in"], 16 * LATE_PARTS)
            pe.wait_ge(s["xz_done"], 1)
            transposes([(half(bank[0], c), half(xn, c)) for c in range(DC)], s["xz_T"])
            pe.wait_ge(s["xz_copied"], 1)
            wide(bank[7][:, 0:2 * HV], lambda c: half(xT, c), lambda c: w_ba[:, c, :]).then_inc(s["ba_done"], 1)
            for b in range(4):
                for k in range(4):
                    n = 4 * b + k
                    last = wide(bank[1 + b][:, k * P:(k + 1) * P], lambda c: w_qkvz[:, c, n * P:(n + 1) * P], lambda c: half(xT, c))
                last.then_inc(s["proj_bank"], 1)
            for b in range(2):
                wide(bank[5 + b][:, :], lambda c: half(xT, c),
                     lambda c: w_qkvz[:, c, CONV + 512 * b:CONV + 512 * (b + 1)]).then_inc(s["z_done"], 1)
            pe.wait_ge(s["gs_done"], 1)
            for b in range(2):
                if b == 1:
                    pe.wait_ge(s["ba_read"], 1)
                o = bank[0 if b == 0 else 7]
                nc.tensor.matmul(o[:, :].rearrange("p (h t) -> p h t", h=4), ident,
                                 negmask.rearrange("p (a t) -> p a t", a=1).to_broadcast([P, 4, P]), start=True, stop=False)
                for k in range(4):
                    last = nc.tensor.matmul(o[:, k * P:(k + 1) * P], gstrict[:, 4 * b + k, :], tri, start=False, stop=(k == 3))
                last.then_inc(s["decay_done"], 1)
            pe.wait_ge(s["sq_done"], 1)
            pe.wait_ge(s["zs_done"], 2)
            for c in range(2 * HK):
                last = nc.tensor.matmul(bank[5][:, c:c + 1], squares[:, c, :], ones[:, 0:1], start=True, stop=True)
            last.then_inc(s["n2_done"], 1)
            pe.wait_ge(s["silu_done"], 2)
            for k in range(HK):
                o = bank[1 + k // 2][:, (k % 2) * 256:(k % 2) * 256 + 256]
                nc.tensor.matmul(o[:, 0:P], qkvT[:, HK + k, :], qkvT[:, HK + k, :], start=True, stop=True)
                last = nc.tensor.matmul(o[:, P:2 * P], qkvT[:, HK + k, :], qkvT[:, k, :], start=True, stop=True)
                if k % 2:
                    last.then_inc(s["gram_done"], 1)
            pe.wait_ge(s["silu_done"], 4)
            for b in range(2):
                transposes([(bank[3 + b][:, k * P:(k + 1) * P], qkvT[:, 2 * HK + 4 * b + k, :]) for k in range(4)], s["vT_done"])
            for b in range(2):
                pe.wait_ge(s["y_init"], b + 1)
                transposes([(bank[5 + b][:, k * P:(k + 1) * P], Y[:, 4 * b + k, :]) for k in range(4)], s["x_T"])
            for lv in range(1, LEVELS):
                bs = 2 ** lv
                for b in range(2):
                    if lv == 1:
                        pe.wait_ge(s["x_init"], b + 1)
                    else:
                        pe.wait_ge(s["xy_done"], 2 * (lv - 2) + b + 1)
                    for k in range(4):
                        h = 4 * b + k
                        last = nc.tensor.matmul(bank[0 if b == 0 else 7][:, k * 64:(k + 1) * 64].rearrange("p (n w) -> p n w", w=bs),
                                                AW[:, h, 0, :], X[:, h, :].rearrange("p (n z w) -> p n z w", z=2, w=bs)[:, :, 0, :],
                                                start=True, stop=True)
                    last.then_inc(s["t_mm"], 1)
                for b in range(2):
                    pe.wait_ge(s["t_done"], 2 * (lv - 1) + b + 1)
                    st = steps[lv % 2]
                    for k in range(4):
                        h = 4 * b + k
                        if lv < LEVELS - 1:
                            nc.tensor.matmul(bank[1 + b][:, k * 64:(k + 1) * 64].rearrange("p (n w) -> p n w", w=bs),
                                             Y[:, h, :], st[:, h, :].rearrange("p (n z w) -> p n z w", z=2, w=bs)[:, :, 0, :],
                                             start=True, stop=True)
                        last = nc.tensor.matmul(bank[1 + b][:, 256 + k * 64:256 + (k + 1) * 64].rearrange("p (n w) -> p n w", w=bs),
                                                st[:, h, :], Y[:, h, :].rearrange("p (n z w) -> p n z w", z=2, w=bs)[:, :, 1, :],
                                                start=True, stop=True)
                    last.then_inc(s["xy_mm"], 1)
            for b in range(2):
                pe.wait_ge(s["xy_done"], 2 * (LEVELS - 2) + b + 1)
                pe.wait_ge(s["bv_done"], 2)
                for k in range(4):
                    last = nc.tensor.matmul(bank[3 + b][:, k * P:(k + 1) * P], Y[:, 4 * b + k, :], Bv[:, 4 * b + k, :], start=True, stop=True)
                last.then_inc(s["delta_mm"], 1)
            for b in range(2):
                pe.wait_ge(s["delta_done"], b + 1)
                for k in range(4):
                    last = nc.tensor.matmul(bank[5 + b][:, k * P:(k + 1) * P], AW[:, 4 * b + k, 1, :], delta[:, 4 * b + k, :], start=True, stop=True)
                last.then_inc(s["o_mm"], 1)
            for b in range(2):
                pe.wait_ge(s["core_done"], 4 * b + 4)
                transposes([(bank[3 + b][:, k * P:(k + 1) * P], core[:, 4 * b + k, :]) for k in range(4)], s["core_T"])
            for h in range(HV):
                if h % 4 == 0:
                    pe.wait_ge(s["coreT_done"], h // 4 + 1)
                last = nc.tensor.matmul(bank[0][:, 0:D], coreT[:, h, :], w_out[:, h, :], start=(h == 0), stop=(h == HV - 1))
            last.then_inc(s["out_mm"], 1)

            pe.wait_ge(s["x2_done"], 1)
            transposes([(half(bank[1], c), half(xn, c)) for c in range(DC)], s["x2_T"])
            pe.wait_ge(s["x2_copied"], 1)
            wide(bank[1][:, D:D + E], lambda c: half(xT, c), lambda c: w_router[:, c, :]).then_inc(s["lg_mm"], 1)
            for b in range(2):
                wide(bank[3 + b][:, :], lambda c: half(xT, c), lambda c: w_gate[:, c, 512 * b:512 * (b + 1)]).then_inc(s["gu_mm"], 1)
                wide(bank[5 + b][:, :], lambda c: half(xT, c), lambda c: w_up[:, c, 512 * b:512 * (b + 1)]).then_inc(s["gu_mm"], 1)
            for b in range(2):
                pe.wait_ge(s["prod_done"], 4 * b + 4)
                transposes([(bank[3 + b][:, k * P:(k + 1) * P], prod[:, 4 * b + k, :]) for k in range(4)], s["prod_T"])
            for e in range(E):
                if e % 4 == 0:
                    pe.wait_ge(s["prodT_done"], e // 4 + 1)
                last = nc.tensor.matmul(bank[0][:, 0:D], prodT[:, e, :], w_down[:, e, :], start=(e == 0), stop=(e == E - 1))
            last.then_inc(s["moe_mm"], 1)

            pe.wait_ge(s["xf_done"], 1)
            transposes([(half(bank[1], c), half(xn, c)) for c in range(DC)], s["xf_T"])
            pe.wait_ge(s["xf_copied"], 1)
            for b in range(2):
                for k in range(4):
                    n = 4 * b + k
                    last = wide(bank[3 + b][:, k * P:(k + 1) * P], lambda c: rw1[:, c, n * P:(n + 1) * P], lambda c: half(xT, c))
                last.then_inc(s["r1_mm"], 1)
            for n in range(FC):
                if n % 4 == 0:
                    pe.wait_ge(s["rel_done"], n + 4)
                last = nc.tensor.matmul(bank[0][:, D:D + E], relT[:, n, :], rw2[:, n, :], start=(n == 0), stop=(n == FC - 1))
            last.then_inc(s["sc_mm"], 1)

            with pe.Fori(0, E // SLOTS) as i:
                for j in range(SLOTS):
                    w1 = slots[j][:, 0:DC * FF].rearrange("p (c n) -> p c n", c=DC)
                    w2 = slots[j][:, DC * FF:EXPERT_N].rearrange("p (c n) -> p c n", c=FC)
                    pe.wait_ge(slot_in[j], i * 16 + (1 if j < EARLY_SLOTS else 16))
                    for b in range(2):
                        for k in range(4):
                            n = 4 * b + k
                            last = wide(bank[3 + 2 * (j % 2) + b][:, k * P:(k + 1) * P], lambda c: w1[:, c, n * P:(n + 1) * P], lambda c: half(xT, c))
                        last.then_inc(s["h_mm"], 1)
                    pe.wait_ge(s["y_free"], i * SLOTS + (j + 1))
                    for n in range(FC):
                        if n == 0:
                            pe.wait_ge(s["hT_done"], i * SLOTS + (j + 1))
                        if n == FC // 2:
                            pe.wait_ge(s["hT2_done"], i * SLOTS + (j + 1))
                        last = nc.tensor.matmul(bank[1 + j % 2][:, 0:D], hT[j % 2][:, n, :], w2[:, n, :], start=(n == 0), stop=(n == FC - 1))
                    last.then_inc(s["y_mm"], 1)
            pe.wait_ge(s["gate_done"], 1)
            nc.tensor.transpose(bank[7][0:E, 0:P], s_("gate"), ident).then_inc(s["gate_T"], 1)
            pe.wait_ge(s["gateT_done"], 1)
            nc.tensor.matmul(bank[0][:, 0:D], gateT[:, :], b2_sb[:, :], start=True, stop=True).then_inc(s["b2_mm"], 1)

        @block.scalar
        def _(act):
            chain = [0]

            def link(ins):
                chain[0] += 1
                ins.then_inc(s["act_chain"], 1)
                act.wait_ge(s["act_chain"], chain[0])

            act.wait_ge(s["eps_set"], 4)
            act.wait_ge(s["ln_var"], 1)
            nc.scalar.activation(s_("sd", 0, 1), s_("mv", 1, 2), ACT.Sqrt, bias=s_("eps", 0, 1)).then_inc(s["ln_sd"], 1)
            act.wait_ge(s["q_ready"], 1)
            a = EARLY["bq"][0]
            for m in range(DC):
                nc.scalar.activation(QT[:, m * P:(m + 1) * P], bank[1][:, m * P:(m + 1) * P], ACT.Identity,
                                     bias=E_sb[:, a + m:a + m + 1]).then_inc(s["q_done"], 1)
            act.wait_ge(s["early2_in"], 16)
            nc.scalar.activation(s_("negA"), early_at("A_log"), ACT.Exp).then_inc(s["exp_tab"], 1)

            def hi_parts(g, quads, first=False):
                if not first:
                    act.wait_ge(s["scores_ready"], g)
                for q in quads:
                    act.wait_ge(s["ctx_transposed"], g * 4 + (q + 1))
                    n = min(512, NC * P - 512 * q)
                    nc.scalar.activation(ctxT[0][:, 512 * q:512 * q + n], bank[CTX_BANKS[q]][:, 0:n], ACT.Copy).then_inc(s["ctxT_hi"], 1)

            def exps(g, b, first=False):
                act.wait_ge(s["max_ready"], g + 1)
                if not first:
                    act.wait_ge(s["probs_transposed"], g * 2)
                    act.wait_ge(s["acc_done"], g)
                nc.scalar.activation(probs[:, :].rearrange("p (z k) -> p z k", z=2), psum[:, 2:4, 0:HALF], ACT.Exp,
                                     bias=s_("nb"), accum_out=s_("rowsum", b, b + 1)).then_inc(s["exp_done"], 1)
                nc.scalar.activation(s_("al", b, b + 1), s_("dm", b, b + 1), ACT.Exp).then_inc(s["alpha_done"], 1)

            def ctx_hi_parts(g, r, first=False):
                if not first:
                    act.wait_ge(s["pv_done"], g - 1)
                nc.scalar.activation(ctxNv[0][:, r % 2], ring[:, r], ACT.Copy).then_inc(s["ctx_hi"], 1)

            def probs_hi_parts(g, first=False):
                if not first:
                    act.wait_ge(s["pv_done"], g)
                for q, tiles in ((0, 4), (1, 3)):
                    act.wait_ge(s["probs_transposed"], g * 2 + (q + 1))
                    nc.scalar.activation(probsT[0][:, 4 * q:4 * q + tiles, :], bank[4 + q][:, 0:tiles * P].rearrange("p (t q) -> p t q", q=T),
                                         ACT.Copy).then_inc(s["probsT_hi"], 1)

            hi_parts(0, range(4), first=True)
            hi_parts(1, range(3))
            exps(0, 0, first=True)
            ctx_hi_parts(0, 0, first=True)
            hi_parts(1, [3])
            probs_hi_parts(0, first=True)
            ctx_hi_parts(1, 1, first=True)
            with act.Fori(0, 3) as i:
                for j in range(RING):
                    g = i * RING + (j + 1)
                    hi_parts(g + 1, range(3))
                    exps(g, (j + 1) % 2)
                    hi_parts(g + 1, [3])
                    probs_hi_parts(g)
                    ctx_hi_parts(g + 1, (j + 2) % RING)
            exps(NG - 1, (NG - 1) % 2)
            probs_hi_parts(NG - 1)

            act.wait_ge(s["o_T"], 1)
            nc.scalar.activation(OT[:, :], bank[0][:, 0:D], ACT.Copy).then_inc(s["o_copied"], 1)
            act.wait_ge(s["var1_done"], 1)
            nc.scalar.activation(s_("sd", 0, 1), s_("mv", 1, 2), ACT.Sqrt, bias=s_("eps", 0, 1)).then_inc(s["sd1_done"], 1)
            nc.scalar.activation(s_("sd", 1, 2), s_("mv", 1, 2), ACT.Sqrt, bias=s_("eps", 1, 2), scale=1.0 + RMS_EPS).then_inc(s["sd1_done"], 1)
            for b in range(4):
                act.wait_ge(s["proj_bank"], b + 1)
                for k in range(4):
                    n = 4 * b + k
                    last = nc.scalar.activation(qkvT[:, n, :], bank[1 + b][:, k * P:(k + 1) * P], ACT.Copy, scale=conv_w[:, n, 3:4])
                last.then_inc(s["tap0_done"], 1)
                if b == 1:
                    act.wait_ge(s["u_ready"], 1)
                    link(nc.scalar.activation(s_("au"), s_("u"), ACT.Abs))
                    link(nc.scalar.activation(s_("sp"), s_("au"), ACT.Exp, scale=-1.0))
                    nc.scalar.activation(s_("au"), s_("sp"), ACT.Ln, bias=s_("eps", 3, 4)).then_inc(s["ln1p_done"], 1)
            nc.scalar.activation(s_("beta"), s_("ba", 0, HV), ACT.Tanh, scale=0.5).then_inc(s["beta_done"], 1)
            for b in range(4):
                act.wait_ge(s["conv_done"], b + 1)
                q = qkvT[:, 4 * b:4 * b + 4, :]
                ins = nc.scalar.activation(q, q, ACT.Silu)
                ins.then_inc(s["silu_done"], 1)
                if b == 1:
                    act.wait_ge(s["silu_done"], 2)
                    nc.scalar.activation(squares, qkvT[:, 0:2 * HK, :], ACT.Square).then_inc(s["sq_done"], 1)
            for b in range(2):
                act.wait_ge(s["z_done"], b + 1)
                nc.scalar.activation(zs[:, 4 * b:4 * b + 4, :], bank[5 + b][:, :].rearrange("p (h t) -> p h t", h=4), ACT.Silu).then_inc(s["zs_done"], 1)
            for b in range(2):
                act.wait_ge(s["decay_done"], b + 1)
                nc.scalar.activation(DT[:, 4 * b:4 * b + 4, :], bank[0 if b == 0 else 7][:, :].rearrange("p (h t) -> p h t", h=4),
                                     ACT.Exp).then_inc(s["dt_done"], 1)
            act.wait_ge(s["kn_in"], 1)
            link(nc.scalar.activation(s_("kn"), s_("n2", HK, 2 * HK), ACT.Sqrt, bias=s_("eps", 2, 3)))
            for b in range(2):
                act.wait_ge(s["vT_done"], b + 1)
                for k in range(4):
                    h = 4 * b + k
                    last = nc.scalar.activation(Bv[:, h, :], bank[3 + b][:, k * P:(k + 1) * P], ACT.Copy, scale=s_("kn", h // 2, h // 2 + 1))
                last.then_inc(s["bv_done"], 1)
            act.wait_ge(s["x_T"], 1)
            nc.scalar.activation(X[:, 0:4, :], bank[5][:, :].rearrange("p (h t) -> p h t", h=4), ACT.Copy).then_inc(s["x_init"], 1)
            act.wait_ge(s["x_T"], 2)
            nc.scalar.activation(X[:, 4:8, :], bank[6][:, :].rearrange("p (h t) -> p h t", h=4), ACT.Copy).then_inc(s["x_init"], 1)
            for b in range(2):
                act.wait_ge(s["delta_mm"], b + 1)
                nc.scalar.activation(delta[:, 4 * b:4 * b + 4, :], bank[3 + b][:, :].rearrange("p (h t) -> p h t", h=4), ACT.Copy).then_inc(s["delta_done"], 1)
            for b in range(2):
                act.wait_ge(s["o_mm"], b + 1)
                nc.scalar.activation(squares[:, 4 * b:4 * b + 4, :], bank[5 + b][:, :].rearrange("p (h t) -> p h t", h=4), ACT.Square).then_inc(s["osq_done"], 1)
            act.wait_ge(s["ms_done"], 1)
            nc.scalar.activation(s_("f"), s_("ms"), ACT.Sqrt).then_inc(s["f_sd"], 1)
            for b in range(2):
                act.wait_ge(s["core_T"], b + 1)
                nc.scalar.activation(coreT[:, 4 * b:4 * b + 4, :], bank[3 + b][:, :].rearrange("p (h t) -> p h t", h=4), ACT.Copy,
                                     scale=early_at("gate_norm")).then_inc(s["coreT_done"], 1)
            act.wait_ge(s["h_done"], 1)
            link(nc.scalar.activation(scratch[:, :], hh[:, :], ACT.Square, accum_out=s_("sd", 0, 1)))
            nc.scalar.activation(s_("sd", 1, 2), s_("sd", 0, 1), ACT.Sqrt, scale=1.0 / D, bias=s_("eps", 2, 3)).then_inc(s["hsd_done"], 1)
            act.wait_ge(s["th_in"], 1)
            nc.scalar.activation(s_("th"), s_("dm", 0, 1), ACT.Tanh, scale=0.5).then_inc(s["th_done"], 1)
            for b in range(2):
                act.wait_ge(s["gu_mm"], 2 * b + 1)
                nc.scalar.activation(gact[:, 4 * b:4 * b + 4, :], bank[3 + b][:, :].rearrange("p (h t) -> p h t", h=4), ACT.Silu).then_inc(s["gact_done"], 1)
            for b in range(2):
                act.wait_ge(s["prod_T"], b + 1)
                nc.scalar.activation(prodT[:, 4 * b:4 * b + 4, :], bank[3 + b][:, :].rearrange("p (h t) -> p h t", h=4), ACT.Copy).then_inc(s["prodT_done"], 1)
            act.wait_ge(s["x3_done"], 1)
            nc.scalar.activation(s_("sd", 0, 1), s_("mv", 1, 2), ACT.Sqrt, bias=s_("eps", 0, 1)).then_inc(s["ln3_sd"], 1)
            act.wait_ge(s["sc_in"], 1)
            nc.scalar.activation(s_("th"), s_("dm", 0, 1), ACT.Tanh, scale=0.5).then_inc(s["sc_th"], 1)
            a = EARLY["b1"][0]
            with act.Fori(0, E // SLOTS) as i:
                for j in range(SLOTS):
                    act.wait_ge(s["h_mm"], i * 8 + (2 * j + 1))
                    act.wait_ge(s["y_mm"], i * SLOTS + (j + 1))
                    for k in range(4):
                        last = nc.scalar.activation(hT[j % 2][:, k, :], bank[3 + 2 * (j % 2)][:, k * P:(k + 1) * P], ACT.Relu,
                                                    bias=E_sb[:, bass.ds(i * (SLOTS * FC) + (a + j * FC + k), 1)])
                    last.then_inc(s["hT_done"], 1)

        @block.vector
        def _(dve):
            V = nc.vector
            chain = [0]

            def link(ins):
                chain[0] += 1
                ins.then_inc(s["dve_chain"], 1)
                dve.wait_ge(s["dve_chain"], chain[0])

            def moments(t):
                link(V.bn_stats(s_("stats"), t))
                return V.bn_aggr(s_("mv"), s_("stats"))

            V.memset(s_("dummy", 0, 1), 0.0).then_inc(s["y_free"], 2)
            V.memset(s_("dummy", 1, 2), 0.0).then_inc(s["y_mm"], 2)
            V.memset(s_("dummy", 2, 3), 0.0).then_inc(s["acc_done"], 1)
            for j in range(EARLY_SLOTS):
                V.memset(s_("dummy", 3 + j, 4 + j), 0.0).then_inc(slot_in[j], 1)
            dve.wait_ge(s["early_in"], 16)
            moments(x).then_inc(s["ln_var"], 1)
            dve.wait_ge(s["ln_sd"], 1)
            link(V.reciprocal(s_("rs", 0, 1), s_("sd", 0, 1)))
            V.tensor_scalar(xn[:, :], x, s_("mv", 0, 1), s_("rs", 0, 1), ALU.subtract, ALU.mult).then_inc(s["ln_xn"], 1)
            V.tensor_scalar(s_("w1p"), early_at("w_ln1"), 1.0, None, ALU.add).then_inc(s["dve_chain"], 1)
            V.tensor_scalar(s_("w2p"), early_at("w_ln2"), 1.0, None, ALU.add).then_inc(s["dve_chain"], 1)
            chain[0] += 2
            dve.wait_ge(s["ln_T"], 1)
            V.tensor_copy(xT[:, :], bank[0][:, 0:D]).then_inc(s["ln_xT"], 1)
            dve.wait_ge(s["bv_ready"], 1)
            V.tensor_tensor(xb[:, :], bank[3][:, 0:D], x, ALU.add).then_inc(s["g_done"], 1)
            dve.wait_ge(s["g_ready"], 1)
            V.tensor_copy(s_("qb"), bank[2][:, D:D + 1]).then_inc(s["g_done"], 1)
            link(V.tensor_copy(G[0][:, :], bank[2][:, 0:D]))
            V.tensor_tensor(G[1][:, :], bank[2][:, 0:D], G[0][:, :], ALU.subtract).then_inc(s["g_done"], 1)
            dve.wait_ge(s["g_done"], 3)
            dve.wait_ge(s["consts_set"], 4)

            def lo_parts(g, quads):
                for q in quads:
                    dve.wait_ge(s["ctxT_hi"], g * 4 + (q + 1))
                    n = min(512, NC * P - 512 * q)
                    at = slice(512 * q, 512 * q + n)
                    V.tensor_tensor(ctxT[1][:, at], bank[CTX_BANKS[q]][:, 0:n], ctxT[0][:, at], ALU.subtract).then_inc(s["ctxT_lo"], 1)

            def maxima(g, b):
                dve.wait_ge(s["scores_ready"], g + 1)
                V.tensor_reduce(s_("mx"), psum[:, 2:4, 0:HALF], mybir.AxisListType.XY, ALU.max).then_inc(s["mx_done"], 1)
                dve.wait_ge(s["mx_done"], g * 2 + 1)
                V.tensor_scalar(s_("M", 1 - b, 2 - b), s_("mx"), s_("qb"), s_("M", b, b + 1), ALU.add, ALU.max).then_inc(s["mx_done"], 1)
                dve.wait_ge(s["mx_done"], g * 2 + 2)
                V.tensor_tensor(s_("dm", b, b + 1), s_("M", b, b + 1), s_("M", 1 - b, 2 - b), ALU.subtract).then_inc(s["dm_done"], 1)
                V.tensor_tensor(s_("nb"), s_("qb"), s_("M", 1 - b, 2 - b), ALU.subtract).then_inc(s["max_ready"], 1)

            def accumulate(g, b):
                dve.wait_ge(s["pv_done"], g + 1)
                dve.wait_ge(s["acc_done"], g + 1)
                V.scalar_tensor_tensor(O[:, :], O[:, :], s_("al", b, b + 1), bank[6][:, 0:D], ALU.mult, ALU.add).then_inc(s["acc_done"], 1)

            def sums(g, b):
                dve.wait_ge(s["exp_done"], g + 1)
                dve.wait_ge(s["alpha_done"], g + 1)
                dve.wait_ge(s["l_done"], g)
                V.scalar_tensor_tensor(s_("l"), s_("l"), s_("al", b, b + 1), s_("rowsum", b, b + 1), ALU.mult, ALU.add).then_inc(s["l_done"], 1)

            def probs_lo_parts(g):
                for q, tiles in ((0, 4), (1, 3)):
                    dve.wait_ge(s["probsT_hi"], g * 2 + (q + 1))
                    V.tensor_tensor(probsT[1][:, 4 * q:4 * q + tiles, :], bank[4 + q][:, 0:tiles * P].rearrange("p (t q) -> p t q", q=T),
                                    probsT[0][:, 4 * q:4 * q + tiles, :], ALU.subtract).then_inc(s["probsT_lo"], 1)

            lo_parts(0, range(4))
            maxima(0, 0)
            lo_parts(1, range(3))
            sums(0, 0)
            lo_parts(1, [3])
            probs_lo_parts(0)
            with dve.Fori(0, 3) as i:
                for j in range(RING):
                    g = i * RING + (j + 1)
                    maxima(g, (j + 1) % 2)
                    lo_parts(g + 1, range(3))
                    sums(g, (j + 1) % 2)
                    accumulate(i * RING + j, j % 2)
                    lo_parts(g + 1, [3])
                    probs_lo_parts(g)
            g = NG - 1
            maxima(g, g % 2)
            accumulate(g - 1, (g - 1) % 2)
            sums(g, g % 2)
            probs_lo_parts(g)
            accumulate(g, g % 2)

            dve.wait_ge(s["l_done"], NG)
            link(V.reciprocal(s_("rl"), s_("l")))
            link(V.tensor_scalar(s_("rl"), s_("rl"), NORM, None, ALU.mult))
            dve.wait_ge(s["att_ready"], 1)
            link(V.scalar_tensor_tensor(x1[:, :], bank[1][:, 0:D], s_("rl"), xb[:, :], ALU.mult, ALU.add))
            moments(x1[:, :]).then_inc(s["var1_done"], 1)
            dve.wait_ge(s["sd1_done"], 2)
            link(V.reciprocal(s_("rs"), s_("sd")))
            V.tensor_scalar(xn[:, :], x1[:, :], s_("mv", 0, 1), s_("rs", 1, 2), ALU.subtract, ALU.mult).then_inc(s["xz_done"], 1)
            V.tensor_scalar(h0[:, :], x1[:, :], s_("mv", 0, 1), s_("rs", 0, 1), ALU.subtract, ALU.mult).then_inc(s["h0_done"], 1)
            dve.wait_ge(s["xz_T"], 1)
            for c in range(DC):
                last = V.tensor_scalar(xT[:, c * P:(c + 1) * P], bank[0][:, c * P:(c + 1) * P], s_("w1p", c, c + 1), None, ALU.mult)
                if c == 0:
                    link(last)
            last.then_inc(s["xz_copied"], 1)
            dve.wait_ge(s["ba_done"], 1)
            V.tensor_copy(s_("ba"), bank[7][:, 0:2 * HV]).then_inc(s["ba_read"], 1)
            dve.wait_ge(s["ba_read"], 1)
            V.tensor_tensor(s_("u"), s_("ba", HV, 2 * HV), early_at("dt_bias"), ALU.add).then_inc(s["u_ready"], 1)

            def taps(b):
                dve.wait_ge(s["tap0_done"], b + 1)
                for d in (1, 2, 3):
                    for k in range(4):
                        n = 4 * b + k
                        last = V.scalar_tensor_tensor(qkvT[:, n, d:T], bank[1 + b][:, k * P:(k + 1) * P - d], conv_w[:, n, 3 - d:4 - d],
                                                      qkvT[:, n, d:T], ALU.mult, ALU.add)
                        last.then_inc(s["conv_done" if d == 3 and k == 3 else "dve_chain"], 1)
                    if d < 3:
                        chain[0] += 4
                        dve.wait_ge(s["dve_chain"], chain[0])
                    else:
                        chain[0] += 3
                        dve.wait_ge(s["dve_chain"], chain[0])

            taps(0)
            taps(1)
            dve.wait_ge(s["ln1p_done"], 1)
            link(V.scalar_tensor_tensor(s_("sp"), s_("u"), 0.0, s_("au"), ALU.max, ALU.add))
            link(V.scalar_tensor_tensor(s_("g"), s_("sp"), -1.0, s_("negA"), ALU.mult, ALU.mult))
            for h in range(HV):
                last = V.tensor_scalar(gstrict[:, h, :], strict, s_("g", h, h + 1), None, ALU.mult)
                if h < HV - 1:
                    last.then_inc(s["dve_chain"], 1)
            last.then_inc(s["gs_done"], 1)
            chain[0] += HV - 1
            taps(2)
            taps(3)
            dve.wait_ge(s["beta_done"], 1)
            link(V.tensor_scalar(s_("beta"), s_("beta"), 0.5, 0.5, ALU.mult, ALU.add))
            dve.wait_ge(s["n2_done"], 1)
            V.tensor_copy(s_("n2"), bank[5][:, 0:2 * HK]).then_inc(s["kn_in"], 1)
            dve.wait_ge(s["kn_in"], 1)
            link(V.tensor_scalar(s_("ki"), s_("n2", HK, 2 * HK), RMS_EPS, None, ALU.add))
            link(V.reciprocal(s_("ki"), s_("ki")))
            link(V.tensor_tensor(s_("kap").rearrange("p (k r) -> p k r", r=2), s_("beta").rearrange("p (k r) -> p k r", r=2),
                                 s_("ki").rearrange("p (k r) -> p k r", r=1).to_broadcast([P, HK, 2]), ALU.mult))
            link(V.tensor_scalar(s_("eq"), s_("n2", 0, HK), P * RMS_EPS, P * RMS_EPS * RMS_EPS, ALU.mult, ALU.add))
            dve.wait_ge(s["y_ident"], 1)
            for b in range(2):
                dve.wait_ge(s["dt_done"], b + 1)
                dve.wait_ge(s["gram_done"], b + 1)
                for k in range(4):
                    h = 4 * b + k
                    kh = h // 2
                    last = V.scalar_tensor_tensor(AW[:, h, :, :],
                                                  bank[1 + kh // 2][:, (kh % 2) * 256:(kh % 2) * 256 + 256].rearrange("p (a t) -> p a t", a=2),
                                                  s_("kap", h, h + 1), DT[:, h:h + 1, :].to_broadcast([P, 2, P]), ALU.mult, ALU.mult)
                    last.then_inc(s["aw_done"], 1)
                dve.wait_ge(s["aw_done"], 4 * b + 4)
                odd = AW[:, 4 * b:4 * b + 4, 0, :].rearrange("p h (n z) -> p h n z", z=2)[:, :, :, 1]
                tmp = delta[:, 4 * b:4 * b + 4, 0:64]
                link(V.scalar_tensor_tensor(tmp, odd, -1.0, m0.rearrange("p (a t) -> p a t", a=1).to_broadcast([P, 4, 64]), ALU.mult, ALU.mult))
                yo = Y[:, 4 * b:4 * b + 4, :].rearrange("p h (n z) -> p h n z", z=2)[:, :, :, 1]
                V.tensor_tensor(yo, yo, tmp, ALU.add).then_inc(s["y_init"], 1)

            dve.wait_ge(s["y_init"], 2)
            dve.wait_ge(s["x_init"], 2)
            for lv in range(1, LEVELS):
                bs = 2 ** lv
                st = steps[lv % 2]

                def first(t, b, z):
                    return t[:, 4 * b:4 * b + 4, :].rearrange("p h (n z w) -> p h n z w", z=2, w=bs)[:, :, :, z, :]

                def four(t):
                    return t.rearrange("p (h n w) -> p h n w", h=4, w=bs)

                for b in range(2):
                    dve.wait_ge(s["t_mm"], 2 * (lv - 1) + b + 1)
                    dve.wait_ge(s["steps_zeroed"], max(2, lv))
                    m = masks[:, lv - 1:lv, :].to_broadcast([P, 4, 64]).rearrange("p h (n w) -> p h n w", w=bs)
                    V.tensor_tensor(first(st, b, 0), four(bank[0 if b == 0 else 7][:, 0:256]), m, ALU.mult).then_inc(s["t_done"], 1)
                for b in range(2):
                    dve.wait_ge(s["xy_mm"], 2 * (lv - 1) + b + 1)
                    if lv < LEVELS - 1:
                        link(V.tensor_tensor(first(X, b, 0), first(X, b, 0), four(bank[1 + b][:, 0:256]), ALU.subtract))
                    V.tensor_tensor(first(Y, b, 1), first(Y, b, 1), four(bank[1 + b][:, 256:512]), ALU.subtract).then_inc(s["xy_done"], 1)
                dve.wait_ge(s["xy_done"], 2 * lv)

            for b in range(2):
                dve.wait_ge(s["osq_done"], b + 1)
                link(V.tensor_reduce(s_("ms", 4 * b, 4 * b + 4), squares[:, 4 * b:4 * b + 4, :], AX, ALU.add))
            V.scalar_tensor_tensor(s_("ms").rearrange("p (k r) -> p k r", r=2), s_("ms").rearrange("p (k r) -> p k r", r=2), 1.0 / P,
                                   s_("eq").rearrange("p (k r) -> p k r", r=1).to_broadcast([P, HK, 2]), ALU.mult, ALU.add).then_inc(s["ms_done"], 1)
            dve.wait_ge(s["f_sd"], 1)
            link(V.reciprocal(s_("f"), s_("f")))
            dve.wait_ge(s["zs_done"], 2)
            for b in range(2):
                for k in range(4):
                    h = 4 * b + k
                    last = V.scalar_tensor_tensor(core[:, h, :], bank[5 + b][:, k * P:(k + 1) * P], s_("f", h, h + 1), zs[:, h, :], ALU.mult, ALU.mult)
                    last.then_inc(s["core_done"], 1)
            dve.wait_ge(s["h0_done"], 1)
            dve.wait_ge(s["out_mm"], 1)
            V.tensor_tensor(hh[:, :], bank[0][:, 0:D], h0[:, :], ALU.add).then_inc(s["h_done"], 1)
            dve.wait_ge(s["h_done"], 1)
            link(V.tensor_tensor(xh[:, :], x1[:, :], hh[:, :], ALU.add))
            dve.wait_ge(s["hsd_done"], 1)
            link(V.reciprocal(s_("rs", 0, 1), s_("sd", 1, 2)))
            V.tensor_scalar(xn[:, :], hh[:, :], s_("rs", 0, 1), None, ALU.mult).then_inc(s["x2_done"], 1)
            dve.wait_ge(s["x2_T"], 1)
            for c in range(DC):
                last = V.tensor_scalar(xT[:, c * P:(c + 1) * P], bank[1][:, c * P:(c + 1) * P], s_("w2p", c, c + 1), None, ALU.mult)
                if c == 0:
                    link(last)
            last.then_inc(s["x2_copied"], 1)

            def gates(out, logits_done, half_tanh, tanh_done):
                link(V.max(s_("top"), s_("lg")))
                link(V.max_index(topi[:, :], s_("top"), s_("lg")))
                V.tensor_tensor(s_("dm", 0, 1), s_("top", 0, 1), s_("top", 1, 2), ALU.subtract).then_inc(s[half_tanh], 1)
                link(V.tensor_copy(s_("idf"), topi[:, :]))
                link(V.tensor_scalar(s_("e1"), early_at("iota"), s_("idf", 0, 1), None, ALU.is_equal))
                link(V.tensor_scalar(s_("e2"), early_at("iota"), s_("idf", 1, 2), None, ALU.is_equal))
                dve.wait_ge(s[tanh_done], 1)
                link(V.tensor_scalar(s_("w", 0, 1), s_("th"), 0.5, 0.5, ALU.mult, ALU.add))
                link(V.tensor_scalar(s_("w", 1, 2), s_("th"), -0.5, 0.5, ALU.mult, ALU.add))
                link(V.tensor_scalar(s_("e1"), s_("e1"), s_("w", 0, 1), None, ALU.mult))
                return V.scalar_tensor_tensor(out, s_("e2"), s_("w", 1, 2), s_("e1"), ALU.mult, ALU.add)

            dve.wait_ge(s["lg_mm"], 1)
            link(V.tensor_copy(s_("lg"), bank[1][:, D:D + E]))
            link(gates(s_("route"), "lg_mm", "th_in", "th_done"))
            for b in range(2):
                dve.wait_ge(s["gact_done"], b + 1)
                dve.wait_ge(s["gu_mm"], 2 * b + 2)
                for k in range(4):
                    e = 4 * b + k
                    V.scalar_tensor_tensor(prod[:, e, :], gact[:, e, :], s_("route", e, e + 1), bank[5 + b][:, k * P:(k + 1) * P], ALU.mult, ALU.mult)\
                        .then_inc(s["prod_done"], 1)
            dve.wait_ge(s["moe_mm"], 1)
            link(V.tensor_tensor(O[:, :], bank[0][:, 0:D], xh[:, :], ALU.add))
            moments(O[:, :]).then_inc(s["x3_done"], 1)
            dve.wait_ge(s["ln3_sd"], 1)
            link(V.reciprocal(s_("rs", 0, 1), s_("sd", 0, 1)))
            V.tensor_scalar(xn[:, :], O[:, :], s_("mv", 0, 1), s_("rs", 0, 1), ALU.subtract, ALU.mult).then_inc(s["xf_done"], 1)
            dve.wait_ge(s["xf_T"], 1)
            V.tensor_copy(xT[:, :], bank[1][:, 0:D]).then_inc(s["xf_copied"], 1)
            a = EARLY["rb1"][0]
            for b in range(2):
                dve.wait_ge(s["r1_mm"], b + 1)
                for k in range(4):
                    n = 4 * b + k
                    V.tensor_scalar(relT[:, n, :], bank[3 + b][:, k * P:(k + 1) * P], E_sb[:, a + n:a + n + 1], 0.0, ALU.add, ALU.max)\
                        .then_inc(s["rel_done"], 1)
            dve.wait_ge(s["sc_mm"], 1)
            link(V.tensor_tensor(s_("lg"), bank[0][:, D:D + E], early_at("rb2"), ALU.add))
            gates(s_("gate"), "sc_mm", "sc_in", "sc_th").then_inc(s["gate_done"], 1)
            dve.wait_ge(s["gate_done"], 1)
            a = EARLY["b1"][0]
            gcol = smalls["gate"][0]
            with dve.Fori(0, E // SLOTS) as i:
                for j in range(SLOTS):
                    dve.wait_ge(s["h_mm"], i * 8 + (2 * j + 2))
                    dve.wait_ge(s["y_mm"], i * SLOTS + (j + 1))
                    for k in range(4):
                        last = V.tensor_scalar(hT[j % 2][:, 4 + k, :], bank[4 + 2 * (j % 2)][:, k * P:(k + 1) * P],
                                               E_sb[:, bass.ds(i * (SLOTS * FC) + (a + j * FC + 4 + k), 1)], 0.0, ALU.add, ALU.max)
                    last.then_inc(s["hT2_done"], 1)
                    dve.wait_ge(s["y_mm"], i * SLOTS + (j + 3))
                    V.scalar_tensor_tensor(O[:, :], bank[1 + j % 2][:, 0:D], sm[:, bass.ds(i * SLOTS + (gcol + j), 1)], O[:, :], ALU.mult, ALU.add)\
                        .then_inc(s["y_free"], 1)
                    dve.wait_ge(s["y_free"], i * SLOTS + (j + 3))
            dve.wait_ge(s["gate_T"], 1)
            V.tensor_copy(gateT[:, :], bank[7][0:E, 0:P]).then_inc(s["gateT_done"], 1)
            dve.wait_ge(s["b2_mm"], 1)
            V.tensor_tensor(O[:, :], bank[0][:, 0:D], O[:, :], ALU.add).then_inc(s["m_done"], 1)


def _chunks(w):
    k, n = w.shape
    return w.reshape(k // P, P, n).transpose(1, 0, 2).reshape(P, -1)


def _constants():
    import numpy as np
    s, t = np.arange(P)[:, None], np.arange(P)[None, :]
    out = {
        "ident": (s == t), "tri": (s <= t), "strict": (s > t),
        "negmask": np.where(t < s, -1e30, 0.0),
        "m0": (s == 2 * np.arange(P // 2)[None, :]),
        "iota": np.broadcast_to(np.arange(E), (P, E)), "ones": np.ones((P, 1)),
    }
    masks = []
    for lv in range(1, LEVELS):
        b = 2 ** lv
        col = np.arange(64)[None, :]
        masks.append((s // (2 * b) == col // b) & (s % (2 * b) >= b))
    out["masks"] = np.concatenate(masks, axis=1)
    return {k: v.astype(np.float32) for k, v in out.items()}


def kernel(**inputs):
    import numpy as np
    import concourse.bacc as bacc
    from concourse.bass_utils import run_bass_kernel_spmd

    a = {k: np.asarray(v) for k, v in inputs.items()}
    c = _constants()

    def rows(v):
        return np.broadcast_to(v[None, :], (P, v.shape[0]))

    def cols(v):
        return v.reshape(-1, P).T

    e = dict(c)
    e.update({
        "x": a["x"][0],
        "conv_w": a["L0_attn_conv_w"].reshape(NCH, P, 4).transpose(1, 0, 2).reshape(P, -1),
        "w_ln1": cols(a["L0_attn_w_ln1"]), "w_ln2": cols(a["L0_attn_w_ln2"]), "gate_norm": cols(a["L0_attn_gate_norm_w"]),
        "bq": cols(a["L0_xattn_bq"]), "bk": cols(a["L0_xattn_bk"]), "rb1": cols(a["L0_ffn_rb1"]),
        "b1": a["L0_ffn_b1"].reshape(E * FC, P).T,
        "dt_bias": rows(a["L0_attn_dt_bias"]), "A_log": rows(a["L0_attn_A_log"]), "rb2": rows(a["L0_ffn_rb2"]),
        "wq": _chunks(a["L0_xattn_Wq"]), "wkT": _chunks(a["L0_xattn_Wk"].T), "wv": _chunks(a["L0_xattn_Wv"]),
    })
    early = np.concatenate([e[name] for name in EARLY], axis=1)

    def by_input(w):
        return w.transpose(1, 0, 2).reshape(w.shape[1], -1)

    w1, w2 = a["L0_ffn_W1"], a["L0_ffn_W2"]
    experts = np.stack([np.concatenate([_chunks(w1[k]), _chunks(w2[k])], axis=1) for k in range(E)])
    late = {
        "qkvz": _chunks(a["L0_attn_W_qkvz"]), "ba": _chunks(a["L0_attn_W_ba"]), "out": _chunks(a["L0_attn_W_out"]),
        "gate": _chunks(by_input(a["L0_attn_W_gate_e"])), "up": _chunks(by_input(a["L0_attn_W_up_e"])),
        "down": a["L0_attn_W_down_e"].transpose(1, 0, 2).reshape(P, -1), "router": _chunks(a["L0_attn_W_router"]),
        "rw1": _chunks(a["L0_ffn_rw1"]), "rw2": _chunks(a["L0_ffn_rw2"]),
    }
    late = np.concatenate([late[name] for name in LATE] + [experts[k] for k in range(EARLY_SLOTS)], axis=1)
    late = np.pad(late, ((0, 0), (0, LATE_N - late.shape[1])))
    late = late.reshape(P, LATE_PARTS, PART_N).transpose(1, 0, 2)

    nc = bacc.Bacc("TRN2", target_bir_lowering=False, num_devices=1)
    arrays = {"early": early, "late": late, "experts": experts[EARLY_SLOTS:], "ctx": a["ctx_1024"][0],
              "bv": a["L0_xattn_bv"].reshape(1, D), "b2": a["L0_ffn_b2"]}
    arrays = {f"in_{k}": np.ascontiguousarray(v) for k, v in arrays.items()}
    args = [nc.dram_tensor(k, v.shape, mybir.dt.from_np(v.dtype), kind="ExternalInput").ap() for k, v in arrays.items()]
    args.append(nc.dram_tensor("out_0", (1, T, D), F32, kind="ExternalOutput").ap().rearrange("b t d -> (b t) d"))
    perceiver(nc, *args)
    r = run_bass_kernel_spmd(nc, [arrays], core_ids=[0])
    return r.results[0]["out_0"]
```

```python
from contextlib import ExitStack

import concourse.bass as bass
from concourse import mybir

P = 128
T = 128
D = 256
DC = D // P
S = 12544
GT = 7
NG = S // P // GT
RING = 4
GK = GT * P
HALF = GK // 2
NC = DC * GT
HK, HV = 4, 8
KEY, VAL = HK * P, HV * P
CONV = 2 * KEY + VAL
NCH = CONV // P
E = 8
FF = 1024
FC = FF // P
SLOTS = 4
LEVELS = 7
CHANNELS = (1, 0, 2, 3)
V_LEVEL = 3
CTX_BANKS = (0, 1, 7, 0)
LN_EPS, RMS_EPS = 1e-5, 1e-6
NORM = 1.0 / 16.0

F32 = mybir.dt.float32
F32R = mybir.dt.float32r
U32 = mybir.dt.uint32
ALU = mybir.AluOpType
ACT = mybir.ActivationFunctionType
AX = mybir.AxisListType.X


def columns(sizes):
    at, out = 0, {}
    for name, n in sizes:
        out[name] = (at, at + n)
        at += n
    return out, at


EARLY, EARLY_N = columns([
    ("x", D), ("ident", P), ("w_ln1", DC), ("w_ln2", DC), ("bq", DC), ("bk", DC), ("A_log", HV),
    ("wq", DC * D), ("wkT", DC * D), ("wv", DC * D),
    ("tri", P), ("strict", P), ("negmask", P), ("m0", P // 2),
    ("masks", 64 * (LEVELS - 1)), ("iota", E), ("ones", 1),
    ("conv_w", 4 * NCH), ("gate_norm", 1),
    ("rb1", FC), ("b1", E * FC), ("dt_bias", HV), ("rb2", E)])
EARLY_CUTS = (0, EARLY["wq"][0], EARLY["wv"][0], EARLY_N)
LATE, LATE_USED = columns([
    ("qkvz", DC * (CONV + VAL)), ("ba", DC * 2 * HV), ("out", HV * D), ("gate", DC * E * P),
    ("up", DC * E * P), ("down", E * D), ("router", DC * E), ("rw1", DC * FF), ("rw2", FC * E)])
EXPERT_N = DC * FF + FC * D
LATE_PARTS = NG - RING
EARLY_SLOTS = 2
PART_N = -(-(LATE_USED + EARLY_SLOTS * EXPERT_N) // LATE_PARTS)
LATE_N = PART_N * LATE_PARTS
assert NG * GK == S


def perceiver(nc, early, late, experts, ctx, bv, b2, out):
    with ExitStack() as stack:
        def sb(name, cols, dt=F32, rows=P):
            return stack.enter_context(nc.sbuf_tensor(name, [rows, cols], dt))

        def sem(name):
            return stack.enter_context(nc.semaphore(name))

        E_sb = sb("early_sb", EARLY_N)
        W_sb = sb("late_sb", LATE_N)
        R1 = sb("ring", RING * GT * D)
        def parts(overlay, name, cols):
            return [overlay.enter_context(nc.sbuf_tensor(f"{name}_{part}", [P, cols], F32R)) for part in ("hi", "lo")]

        with ExitStack() as overlay:
            ctxN = parts(overlay, "ctx", 2 * GT * D)
        late_slots = sb("late_slots", (SLOTS - EARLY_SLOTS) * EXPERT_N)
        with ExitStack() as overlay:
            ctxT = parts(overlay, "ctxT", NC * P)
            G = parts(overlay, "G", D)
            PT = parts(overlay, "probsT", GK)
        R2 = sb("work", 8192)
        bv_sb = R2[0:1, 7296:7552]
        sixteenth = R2[0:1, 7552:7552 + P]
        gateT = R2[0:E, 2048:2048 + P]
        b2_sb = sb("b2_sb", D, rows=E)
        psum = stack.enter_context(nc.psum_tensor("psum", [P, 8, 512], F32))
        bank = [psum[:, i, :] for i in range(8)]

        def early_at(name):
            a, b = EARLY[name]
            return E_sb[:, a:b]

        def late_at(name, **kw):
            a, b = LATE[name]
            return W_sb[:, a:b].rearrange("p (c n) -> p c n", **kw)

        x = early_at("x")
        ident = early_at("ident")
        tri = early_at("tri")
        strict = early_at("strict")
        negmask = early_at("negmask")
        m0 = early_at("m0")
        masks = early_at("masks").rearrange("p (l c) -> p l c", c=64)
        ones = early_at("ones")
        conv_w = early_at("conv_w").rearrange("p (c j) -> p c j", j=4)
        wq = early_at("wq").rearrange("p (c n) -> p c n", c=DC)
        wkT = early_at("wkT").rearrange("p (c n) -> p c n", c=DC)
        wv = early_at("wv").rearrange("p (c n) -> p c n", c=DC)
        w_qkvz = late_at("qkvz", c=DC)
        w_ba = late_at("ba", c=DC)
        w_out = late_at("out", c=HV)
        w_gate = late_at("gate", c=DC)
        w_up = late_at("up", c=DC)
        w_down = late_at("down", c=E)
        w_router = late_at("router", c=DC)
        rw1 = late_at("rw1", c=DC)
        rw2 = late_at("rw2", c=FC)
        slots = [W_sb[:, LATE_USED + j * EXPERT_N:LATE_USED + (j + 1) * EXPERT_N] for j in range(EARLY_SLOTS)]
        slots += [late_slots[:, bass.ts(j, EXPERT_N)] for j in range(SLOTS - EARLY_SLOTS)]

        ring = R1[:, :].rearrange("p (r t d) -> p r t d", r=RING, d=D)
        ctxTv = [part[:, :].rearrange("p (c k) -> p c k", c=DC) for part in ctxT]
        probs = R2[:, 5888:5888 + GK]
        ctxNv = [part[:, :].rearrange("p (b t d) -> p b t d", b=2, d=D) for part in ctxN]
        probsT = [part[:, :].rearrange("p (t q) -> p t q", q=T) for part in PT]
        AW = R1[:, 0:2048].rearrange("p (h a t) -> p h a t", h=HV, a=2)
        DT = R1[:, 2048:3072].rearrange("p (h t) -> p h t", h=HV)
        gstrict = R1[:, 3072:4096].rearrange("p (h t) -> p h t", h=HV)
        X = R1[:, 4096:5120].rearrange("p (h t) -> p h t", h=HV)
        Y = R1[:, 5120:6144].rearrange("p (h t) -> p h t", h=HV)
        Bv = R1[:, 6144:7168].rearrange("p (h t) -> p h t", h=HV)
        qkvT = R2[:, 0:2048].rearrange("p (c t) -> p c t", c=NCH)
        squares = R2[:, 2048:3072].rearrange("p (c t) -> p c t", c=2 * HK)
        zs = R2[:, 3072:4096].rearrange("p (h t) -> p h t", h=HV)
        steps = [R2[:, 4096 + 1024 * i:5120 + 1024 * i].rearrange("p (h t) -> p h t", h=HV) for i in range(2)]
        delta = R2[:, 6144:7168].rearrange("p (h t) -> p h t", h=HV)
        core = R2[:, 7168:8192].rearrange("p (h t) -> p h t", h=HV)
        rawv = core
        tap = gstrict
        coreT = R1[:, 2048:3072].rearrange("p (h t) -> p h t", h=HV)
        gact = R1[:, 0:1024].rearrange("p (e i) -> p e i", e=E)
        prod = R1[:, 1024:2048].rearrange("p (e i) -> p e i", e=E)
        prodT = R1[:, 3072:4096].rearrange("p (e i) -> p e i", e=E)
        relT = R2[:, 0:1024].rearrange("p (c t) -> p c t", c=FC)
        hT = [R2[:, 4096 + 1024 * i:5120 + 1024 * i].rearrange("p (c t) -> p c t", c=FC) for i in range(2)]

        xn = sb("xn", D)
        xT = sb("xT", D)
        QT = R2[:, 6784:7040]
        OT = R2[:, 7040:7296]
        scratch = R2[:, 7680:7936]
        hh = sb("hh", D)
        O = sb("O", D)
        xb = sb("xb", D)
        x1 = sb("x1", D)
        h0, xh = x, xb
        smalls, SMALL_N = columns([
            ("stats", 6), ("mv", 2), ("sd", 2), ("rs", 2), ("qb", 1), ("M", 2), ("mx", 1), ("nb", 1), ("dm", 2),
            ("al", 2), ("rowsum", 2), ("l", 1), ("rl", 1), ("w1p", DC), ("w2p", DC), ("negA", HV), ("beta", HV),
            ("u", HV), ("au", HV), ("sp", HV), ("g", HV), ("ba", 2 * HV), ("n2", 2 * HK), ("kap", HV), ("ki", HK), ("kn", HK), ("eq", HK),
            ("ms", HV), ("f", HV), ("lg", E), ("top", 8), ("w", 2), ("th", 1), ("idf", 8), ("e1", E), ("e2", E),
            ("route", E), ("gate", E), ("eps", 4), ("dummy", 8), ("spare", 2)])
        sm = sb("smalls", SMALL_N)
        topi = sb("topi", 8, U32)

        def s_(name, a=0, b=None):
            lo, hi = smalls[name]
            return sm[:, lo + a:(hi if b is None else lo + b)]

        names = """early_in early3_in rows_in late_in out_done
            consts_set eps_set
            early2_in dve_chain act_chain pool_chain conv_v steps_zeroed y_free credit mx_done dm_done l_done exp_tab m_done y_ident cleared
            ln_var ln_sd ln_xn ln_T ln_xT q_ready q_done g_ready g_done qb_done bv_ready
            ctx_transposed ctxT_hi ctxT_lo ctx_hi ctx_lo probsT_hi scores_ready max_ready exp_done alpha_done probs_transposed probsT_lo pv_done acc_done
            o_T o_copied att_ready
            var1_done sd1_done xz_done xz_T xz_copied ba_done ba_read softplus_in u_ready eau_done ln1p_done g_done2 gs_done
            proj_bank tap0_done conv_done silu_done z_done zs_done
            beta_done sq_done n2_done n2_read kn_in kn_done decay_done dt_done gram_done aw_done vT_done bv_done
            y_init x_T x_init x_done t_mm t_done y_step y_done delta_mm delta_done o_mm osq_done ms_done f_sd f_done core_done core_done2 zo_done raw_v core_T coreT_done
            out_mm h_done hsq_done hsd_done x2_done x2_T x2_copied lg_mm th_in th_done route_done gu_mm gact_done prod_done prod_T prodT_done
            moe_mm x3_done ln3_sd xf_done xf_T xf_copied r1_mm rel_done rel_done2 sc_mm sc_in sc_th gate_done gate_T gateT_done b2_mm acc_init
            h_mm hT_done hT2_done y_mm y_added h0_done""".split()
        s = {n: sem(n) for n in names}
        ctx_in = [sem(f"ctx_in{r}") for r in range(RING)]
        slot_in = [sem(f"slot_in{r}") for r in range(SLOTS)]

        def half(t, c):
            return t[:, c * P:(c + 1) * P]

        block = stack.enter_context(nc.Block())

        @block.sync
        def _(sp):
            def early_part(i, done):
                at = slice(EARLY_CUTS[i], EARLY_CUTS[i + 1])
                sp.dma_start(E_sb[:, at], early[:, at]).then_inc(s[done], 16)

            early_part(0, "early_in")
            early_part(1, "early2_in")
            sp.dma_start(bv_sb[:, :], bv).then_inc(s["rows_in"], 16)
            sp.dma_start(b2_sb[:, :], b2).then_inc(s["rows_in"], 16)

            ctx_g = ctx.rearrange("(p g t) d -> p g (t d)", p=P, g=NG)
            R1g = R1[:, :].rearrange("p (r n) -> p r n", r=RING)

            def group(g, r):
                sp.dma_start(R1g[:, r, :], ctx_g[:, g, :]).then_inc(ctx_in[r], 16)

            def part(i):
                sp.dma_start(W_sb[:, bass.ts(i, PART_N)], late[i, :, :]).then_inc(s["late_in"], 16)

            group(0, 0)
            early_part(2, "early3_in")
            for r in range(1, RING):
                group(r, r)
            with sp.Fori(0, 2) as i:
                for r in range(RING):
                    part(i * RING + r)
                    sp.wait_ge(s["ctx_lo"], i * RING + (r + 1))
                    group(i * RING + (RING + r), r)
            for r in range(2):
                part(2 * RING + r)
                sp.wait_ge(s["ctx_lo"], 2 * RING + r + 1)
                group(3 * RING + r, r)
            sp.wait_ge(s["pv_done"], NG)
            for j in range(EARLY_SLOTS, SLOTS):
                sp.dma_start(slots[j], experts[j - EARLY_SLOTS, :, :]).then_inc(slot_in[j], 16)
            for j in range(SLOTS):
                sp.wait_ge(s["y_mm"], j + 3)
                sp.dma_start(slots[j], experts[SLOTS - EARLY_SLOTS + j, :, :]).then_inc(slot_in[j], 16)
            sp.wait_ge(s["m_done"], 1)
            sp.dma_start(out, O[:, :]).then_inc(s["out_done"], 16)
            sp.wait_ge(s["out_done"], 16)

        @block.gpsimd
        def _(pool):
            nc.gpsimd.memset(s_("eps", 0, 1), LN_EPS).then_inc(s["eps_set"], 1)
            nc.gpsimd.memset(s_("eps", 1, 2), LN_EPS * RMS_EPS).then_inc(s["eps_set"], 1)
            nc.gpsimd.memset(s_("eps", 2, 3), RMS_EPS).then_inc(s["eps_set"], 1)
            nc.gpsimd.memset(s_("eps", 3, 4), 1.0).then_inc(s["eps_set"], 1)
            nc.gpsimd.memset(sixteenth[:, :], NORM).then_inc(s["consts_set"], 1)
            nc.gpsimd.memset(O[:, :], 0.0).then_inc(s["consts_set"], 1)
            nc.gpsimd.memset(s_("l"), 0.0).then_inc(s["consts_set"], 1)
            nc.gpsimd.memset(s_("M", 0, 1), -3e38).then_inc(s["consts_set"], 1)
            def ctx_lo_parts(g, r):
                pool.wait_ge(s["ctx_hi"], g + 1)
                nc.gpsimd.tensor_tensor(ctxNv[1][:, r % 2], ring[:, r], ctxNv[0][:, r % 2], ALU.subtract).then_inc(s["ctx_lo"], 1)

            with pool.Fori(0, 3) as i:
                for j in range(RING):
                    ctx_lo_parts(i * RING + j, j)
            for g in range(3 * RING, NG):
                ctx_lo_parts(g, g % RING)
            pool.wait_ge(s["pv_done"], NG)
            pool.wait_ge(s["early_in"], 16)
            nc.gpsimd.tensor_copy(Y, ident.rearrange("p (a t) -> p a t", a=1).to_broadcast([P, HV, P])).then_inc(s["y_ident"], 1)
            for i in range(2):
                nc.gpsimd.memset(steps[i], 0.0).then_inc(s["steps_zeroed"], 1)
            for b in range(2):
                pool.wait_ge(s["raw_v"], b + 1)
                chunks = slice(2 * HK + 4 * b, 2 * HK + 4 * b + 4)
                for d in range(4):
                    w = conv_w[:, chunks, 3 - d:4 - d].to_broadcast([P, 4, T - d])
                    product = qkvT[:, chunks, :] if d == 0 else tap[:, 4 * b:4 * b + 4, d:T]
                    nc.gpsimd.tensor_tensor(product, rawv[:, 4 * b:4 * b + 4, 0:T - d], w, ALU.mult).then_inc(s["pool_chain"], 1)
                    pool.wait_ge(s["pool_chain"], 6 * b + max(1, 2 * d))
                    if d > 0:
                        nc.gpsimd.tensor_tensor(qkvT[:, chunks, d:T], qkvT[:, chunks, d:T], product, ALU.add)\
                            .then_inc(s["conv_v" if d == 3 else "pool_chain"], 1)
                        pool.wait_ge(s["conv_v"] if d == 3 else s["pool_chain"], b + 1 if d == 3 else 6 * b + 2 * d + 1)
            for lv in range(3, LEVELS):
                pool.wait_ge(s["y_step"], 2 * (lv - 2))
                nc.gpsimd.memset(steps[lv % 2], 0.0).then_inc(s["steps_zeroed"], 1)

        @block.tensor
        def _(pe):
            def transposes(pairs, done):
                for o, i in pairs:
                    last = nc.tensor.transpose(o, i, ident)
                last.then_inc(done, 1)

            def wide(o, lhs, rhs, n=DC):
                for c in range(n):
                    last = nc.tensor.matmul(o, lhs(c), rhs(c), start=(c == 0), stop=(c == n - 1))
                return last

            def ctx_transposes(g, r, quads):
                for q in quads:
                    if q == 3:
                        pe.wait_ge(s["ctxT_lo"], g * 4 + 1)
                    blocks = range(4 * q, min(4 * q + 4, NC))
                    transposes([(bank[CTX_BANKS[q]][:, (b % 4) * P:(b % 4 + 1) * P],
                                 ring[:, r, b % GT, (b // GT) * P:(b // GT + 1) * P]) for b in blocks],
                               s["ctx_transposed"])

            pe.wait_ge(s["early_in"], 16)
            pe.wait_ge(s["ln_xn"], 1)
            transposes([(half(bank[4], c), half(xn, c)) for c in range(DC)], s["ln_T"])
            pe.wait_ge(s["rows_in"], 32)
            pe.wait_ge(s["early2_in"], 16)
            pe.wait_ge(s["consts_set"], 4)
            nc.tensor.matmul(bank[3][:, 0:D], sixteenth[:, :], bv_sb[:, :], start=True, stop=True).then_inc(s["bv_ready"], 1)
            pe.wait_ge(s["ln_xT"], 1)
            for m in range(DC):
                last = wide(half(bank[5], m), lambda c: wq[:, c, m * P:(m + 1) * P], lambda c: half(xT, c))
            last.then_inc(s["q_ready"], 1)
            pe.wait_ge(ctx_in[0], 16)
            ctx_transposes(0, 0, range(2))
            pe.wait_ge(s["q_done"], 2)
            for m in range(DC):
                wide(half(bank[6], m), lambda c: wkT[:, c, m * P:(m + 1) * P], lambda c: half(QT, c))
            a = EARLY["bk"][0]
            wide(bank[6][:, D:D + 1], lambda c: half(QT, c), lambda c: E_sb[:, a + c:a + c + 1]).then_inc(s["g_ready"], 1)

            def scores(g, first=False):
                if not first:
                    pe.wait_ge(s["exp_done"], g)
                for hf in range(2):
                    pe.wait_ge(s["ctxT_lo"], g * 4 + (3 + hf))
                    terms = [(a, b, c) for a, b in ((0, 0), (1, 0), (0, 1)) for c in range(DC)]
                    for i, (a, b, c) in enumerate(terms):
                        last = nc.tensor.matmul(bank[2 + hf][:, 0:HALF], G[a][:, c * P:(c + 1) * P],
                                                ctxTv[b][:, c, hf * HALF:(hf + 1) * HALF], start=(i == 0), stop=(i == len(terms) - 1))
                last.then_inc(s["scores_ready"], 1)

            def probs_transposes(g, first=False):
                pe.wait_ge(s["exp_done"], g + 1)
                if not first:
                    pe.wait_ge(s["probsT_lo"], g * 2)
                for q, tiles in ((0, range(0, 4)), (1, range(4, 7))):
                    transposes([(bank[4 + q][:, (t % 4) * P:(t % 4 + 1) * P], probs[:, t * P:(t + 1) * P]) for t in tiles],
                               s["probs_transposed"])

            def attend(g, r, first=False):
                if not first:
                    pe.wait_ge(s["acc_done"], g + 1)
                pe.wait_ge(s["ctx_lo"], g + 1)
                terms = [(t, a, b) for tiles in (range(4), range(4, GT)) for a, b in ((0, 0), (1, 0), (0, 1)) for t in tiles]
                for i, (t, a, b) in enumerate(terms):
                    if i == 0:
                        pe.wait_ge(s["probsT_lo"], g * 2 + 1)
                    if i == 4 * 3:
                        pe.wait_ge(s["probsT_lo"], g * 2 + 2)
                    last = nc.tensor.matmul(bank[6][:, 0:D], probsT[a][:, t, :], ctxNv[b][:, r % 2, t, :],
                                            start=(i == 0), stop=(i == len(terms) - 1))
                last.then_inc(s["pv_done"], 1)

            ctx_transposes(0, 0, [2, 3])
            pe.wait_ge(s["g_done"], 3)
            scores(0, first=True)
            pe.wait_ge(ctx_in[1], 16)
            ctx_transposes(1, 1, range(4))
            probs_transposes(0, first=True)
            with pe.Fori(0, 3) as i:
                for j in range(RING):
                    g = i * RING + (j + 1)
                    scores(g)
                    r = (j + 2) % RING
                    pe.wait_ge(ctx_in[r], i * 16 + (32 if j >= 2 else 16))
                    ctx_transposes(i * RING + (j + 2), r, range(3))
                    attend(i * RING + j, j)
                    ctx_transposes(i * RING + (j + 2), r, [3])
                    probs_transposes(g)
            scores(NG - 1)
            attend(NG - 2, (NG - 2) % RING)
            probs_transposes(NG - 1)
            attend(NG - 1, (NG - 1) % RING)
            pe.wait_ge(s["acc_done"], NG + 1)
            transposes([(half(bank[0], c), half(O, c)) for c in range(DC)], s["o_T"])
            pe.wait_ge(s["o_copied"], 1)
            wide(bank[1][:, 0:D], lambda c: half(OT, c), lambda c: wv[:, c, :]).then_inc(s["att_ready"], 1)

            pe.wait_ge(s["late_in"], 16 * LATE_PARTS)
            pe.wait_ge(s["xz_done"], 1)
            transposes([(half(bank[0], c), half(xn, c)) for c in range(DC)], s["xz_T"])
            pe.wait_ge(s["xz_copied"], 1)
            wide(bank[7][:, 0:2 * HV], lambda c: half(xT, c), lambda c: w_ba[:, c, :]).then_inc(s["ba_done"], 1)

            def project(i):
                for k in range(4):
                    n = 4 * CHANNELS[i] + k
                    last = wide(bank[1 + i][:, k * P:(k + 1) * P], lambda c: w_qkvz[:, c, n * P:(n + 1) * P], lambda c: half(xT, c))
                last.then_inc(s["proj_bank"], 1)

            def project_z(b):
                wide(bank[5 + b][:, :], lambda c: half(xT, c),
                     lambda c: w_qkvz[:, c, CONV + 512 * b:CONV + 512 * (b + 1)]).then_inc(s["z_done"], 1)

            project(0)
            project(1)
            pe.wait_ge(s["gs_done"], 1)
            pe.wait_ge(s["ba_read"], 1)
            for b in range(2):
                o = bank[0 if b == 0 else 7]
                nc.tensor.matmul(o[:, :].rearrange("p (h t) -> p h t", h=4), ident,
                                 negmask.rearrange("p (a t) -> p a t", a=1).to_broadcast([P, 4, P]), start=True, stop=False)
                for k in range(4):
                    last = nc.tensor.matmul(o[:, k * P:(k + 1) * P], gstrict[:, 4 * b + k, :], tri, start=False, stop=(k == 3))
                last.then_inc(s["decay_done"], 1)
            project(2)
            project(3)
            pe.wait_ge(s["dt_done"], 1)
            pe.wait_ge(s["sq_done"], 1)

            def lengths(first):
                for c in range(first, first + HK):
                    last = nc.tensor.matmul(bank[0][:, c:c + 1], squares[:, c, :], ones[:, 0:1], start=True, stop=True)
                last.then_inc(s["n2_done"], 1)

            def gram(k, other):
                o = bank[1 + k // 2][:, (k % 2) * 256 + other * P:(k % 2) * 256 + (other + 1) * P]
                return nc.tensor.matmul(o, qkvT[:, HK + k, :], qkvT[:, HK + k if other == 0 else k, :], start=True, stop=True)

            lengths(HK)
            for k in range(2):
                gram(k, 0)
            pe.wait_ge(s["silu_done"], 2)
            for k in range(2):
                last = gram(k, 1)
            last.then_inc(s["gram_done"], 1)
            for k in range(2, HK):
                gram(k, 0)
                last = gram(k, 1)
            last.then_inc(s["gram_done"], 1)
            pe.wait_ge(s["sq_done"], 2)
            pe.wait_ge(s["kn_in"], 1)
            lengths(0)
            project_z(0)
            pe.wait_ge(s["raw_v"], 2)
            for b in range(2):
                pe.wait_ge(s["y_init"], b + 1)
                transposes([(bank[3 + b][:, k * P:(k + 1) * P], Y[:, 4 * b + k, :]) for k in range(4)], s["x_T"])
                if b == 0:
                    project_z(1)
            pe.wait_ge(s["n2_read"], 1)
            for lv in range(1, LEVELS):
                bs = 2 ** lv
                for b in range(2):
                    if lv == 1:
                        pe.wait_ge(s["x_init"], b + 1)
                    else:
                        pe.wait_ge(s["x_done"], 2 * (lv - 2) + b + 1)
                    for k in range(4):
                        h = 4 * b + k
                        last = nc.tensor.matmul(bank[0 if b == 0 else 7][:, k * 64:(k + 1) * 64].rearrange("p (n w) -> p n w", w=bs),
                                                AW[:, h, 0, :], X[:, h, :].rearrange("p (n z w) -> p n z w", z=2, w=bs)[:, :, 0, :],
                                                start=True, stop=True)
                    last.then_inc(s["t_mm"], 1)
                for b in range(2):
                    pe.wait_ge(s["t_done"], 2 * (lv - 1) + b + 1)
                    st = steps[lv % 2]
                    for k in range(4):
                        h = 4 * b + k
                        last = nc.tensor.matmul(bank[1 + b][:, k * 64:(k + 1) * 64].rearrange("p (n w) -> p n w", w=bs),
                                                st[:, h, :], Y[:, h, :].rearrange("p (n z w) -> p n z w", z=2, w=bs)[:, :, 1, :],
                                                start=True, stop=True)
                    last.then_inc(s["y_step"], 1)
                if lv < LEVELS - 1:
                    for b in range(2):
                        pe.wait_ge(s["y_done"], 2 * (lv - 1) + b + 1)
                        transposes([(bank[3 + b][:, k * P:(k + 1) * P], Y[:, 4 * b + k, :]) for k in range(4)], s["x_T"])
                if lv == V_LEVEL:
                    pe.wait_ge(s["zs_done"], 2)
                    pe.wait_ge(s["silu_done"], 4)
                    for b in range(2):
                        transposes([(bank[5 + b][:, k * P:(k + 1) * P], qkvT[:, 2 * HK + 4 * b + k, :]) for k in range(4)], s["vT_done"])
            for b in range(2):
                pe.wait_ge(s["y_done"], 2 * (LEVELS - 2) + b + 1)
                pe.wait_ge(s["bv_done"], 2)
                for k in range(4):
                    last = nc.tensor.matmul(bank[3 + b][:, k * P:(k + 1) * P], Y[:, 4 * b + k, :], Bv[:, 4 * b + k, :], start=True, stop=True)
                last.then_inc(s["delta_mm"], 1)
            for b in range(2):
                pe.wait_ge(s["delta_done"], b + 1)
                for k in range(4):
                    last = nc.tensor.matmul(bank[5 + b][:, k * P:(k + 1) * P], AW[:, 4 * b + k, 1, :], delta[:, 4 * b + k, :], start=True, stop=True)
                last.then_inc(s["o_mm"], 1)
            for b in range(2):
                pe.wait_ge(s["core_done"], b + 1)
                pe.wait_ge(s["core_done2"], b + 1)
                transposes([(bank[3 + b][:, k * P:(k + 1) * P], core[:, 4 * b + k, :]) for k in range(4)], s["core_T"])
            for h in range(HV):
                if h % 4 == 0:
                    pe.wait_ge(s["coreT_done"], h // 4 + 1)
                last = nc.tensor.matmul(bank[0][:, 0:D], coreT[:, h, :], w_out[:, h, :], start=(h == 0), stop=(h == HV - 1))
            last.then_inc(s["out_mm"], 1)

            pe.wait_ge(s["h_done"], 1)
            transposes([(half(bank[1], c), half(hh, c)) for c in range(DC)], s["x2_T"])
            pe.wait_ge(s["x2_copied"], 1)
            wide(bank[1][:, D:D + E], lambda c: half(xT, c), lambda c: w_router[:, c, :]).then_inc(s["lg_mm"], 1)
            def gate_up(b, o, w):
                wide(bank[o + b][:, :], lambda c: half(xT, c), lambda c: w[:, c, 512 * b:512 * (b + 1)]).then_inc(s["gu_mm"], 1)

            def products(b):
                pe.wait_ge(s["prod_done"], 4 * b + 4)
                transposes([(bank[3 + b][:, k * P:(k + 1) * P], prod[:, 4 * b + k, :]) for k in range(4)], s["prod_T"])

            def downs(b):
                pe.wait_ge(s["prodT_done"], b + 1)
                for e in range(4 * b, 4 * b + 4):
                    last = nc.tensor.matmul(bank[0][:, 0:D], prodT[:, e, :], w_down[:, e, :], start=(e == 0), stop=(e == E - 1))
                return last

            gate_up(0, 3, w_gate)
            gate_up(0, 5, w_up)
            gate_up(1, 3, w_gate)
            products(0)
            gate_up(1, 5, w_up)
            downs(0)
            products(1)
            last = downs(1)
            last.then_inc(s["moe_mm"], 1)

            pe.wait_ge(s["xf_done"], 1)
            transposes([(half(bank[1], c), half(xn, c)) for c in range(DC)], s["xf_T"])
            pe.wait_ge(s["xf_copied"], 1)
            for n in range(FC):
                last = wide(half(bank[3 + n // 2], n % 2), lambda c: rw1[:, c, n * P:(n + 1) * P], lambda c: half(xT, c))
                if n % 2:
                    last.then_inc(s["r1_mm"], 1)
            for n in range(FC):
                if n % 4 == 0:
                    pe.wait_ge(s["rel_done"], n // 4 + 1)
                if n % 4 == 2:
                    pe.wait_ge(s["rel_done2"], n // 4 + 1)
                last = nc.tensor.matmul(bank[0][:, D:D + E], relT[:, n, :], rw2[:, n, :], start=(n == 0), stop=(n == FC - 1))
            last.then_inc(s["sc_mm"], 1)

            with pe.Fori(0, E // SLOTS) as i:
                for j in range(SLOTS):
                    w1 = slots[j][:, 0:DC * FF].rearrange("p (c n) -> p c n", c=DC)
                    w2 = slots[j][:, DC * FF:EXPERT_N].rearrange("p (c n) -> p c n", c=FC)
                    pe.wait_ge(slot_in[j], i * 16 + (1 if j < EARLY_SLOTS else 16))
                    for b in range(2):
                        for k in range(4):
                            n = 4 * b + k
                            last = wide(bank[3 + 2 * (j % 2) + b][:, k * P:(k + 1) * P], lambda c: w1[:, c, n * P:(n + 1) * P], lambda c: half(xT, c))
                        last.then_inc(s["h_mm"], 1)
                    pe.wait_ge(s["y_free"], i * SLOTS + (j + 1))
                    for n in range(FC):
                        if n == 0:
                            pe.wait_ge(s["hT_done"], i * SLOTS + (j + 1))
                        if n == FC // 2:
                            pe.wait_ge(s["hT2_done"], i * SLOTS + (j + 1))
                        last = nc.tensor.matmul(bank[1 + j % 2][:, 0:D], hT[j % 2][:, n, :], w2[:, n, :], start=(n == 0), stop=(n == FC - 1))
                    last.then_inc(s["y_mm"], 1)
            pe.wait_ge(s["gate_done"], 1)
            nc.tensor.transpose(bank[7][0:E, 0:P], s_("gate"), ident).then_inc(s["gate_T"], 1)
            pe.wait_ge(s["gateT_done"], 1)
            nc.tensor.matmul(bank[0][:, 0:D], gateT[:, :], b2_sb[:, :], start=True, stop=True).then_inc(s["b2_mm"], 1)

        @block.scalar
        def _(act):
            chain = [0]

            def link(ins):
                chain[0] += 1
                ins.then_inc(s["act_chain"], 1)
                act.wait_ge(s["act_chain"], chain[0])

            act.wait_ge(s["eps_set"], 4)
            nc.scalar.activation(s_("spare", 0, 1), s_("eps", 3, 4), ACT.Sqrt).then_inc(s["act_chain"], 1)
            chain[0] += 1
            act.wait_ge(s["early_in"], 16)
            act.wait_ge(s["ln_var"], 1)
            nc.scalar.activation(s_("sd", 0, 1), s_("mv", 1, 2), ACT.Sqrt, bias=s_("eps", 0, 1)).then_inc(s["ln_sd"], 1)
            nc.scalar.activation(s_("negA"), early_at("A_log"), ACT.Exp).then_inc(s["exp_tab"], 1)
            act.wait_ge(s["q_ready"], 1)
            a = EARLY["bq"][0]
            for m in range(DC):
                nc.scalar.activation(QT[:, m * P:(m + 1) * P], bank[5][:, m * P:(m + 1) * P], ACT.Identity,
                                     bias=E_sb[:, a + m:a + m + 1]).then_inc(s["q_done"], 1)
            def hi_parts(g, quads, first=False):
                if not first:
                    act.wait_ge(s["scores_ready"], g)
                for q in quads:
                    act.wait_ge(s["ctx_transposed"], g * 4 + (q + 1))
                    n = min(512, NC * P - 512 * q)
                    nc.scalar.activation(ctxT[0][:, 512 * q:512 * q + n], bank[CTX_BANKS[q]][:, 0:n], ACT.Copy).then_inc(s["ctxT_hi"], 1)

            def exps(g, b, first=False):
                act.wait_ge(s["max_ready"], g + 1)
                if not first:
                    act.wait_ge(s["probs_transposed"], g * 2)
                    act.wait_ge(s["acc_done"], g)
                nc.scalar.activation(probs[:, :].rearrange("p (z k) -> p z k", z=2), psum[:, 2:4, 0:HALF], ACT.Exp,
                                     bias=s_("nb"), accum_out=s_("rowsum", b, b + 1)).then_inc(s["exp_done"], 1)
                nc.scalar.activation(s_("al", b, b + 1), s_("dm", b, b + 1), ACT.Exp).then_inc(s["alpha_done"], 1)

            def ctx_hi_parts(g, r, first=False):
                if not first:
                    act.wait_ge(s["pv_done"], g - 1)
                nc.scalar.activation(ctxNv[0][:, r % 2], ring[:, r], ACT.Copy).then_inc(s["ctx_hi"], 1)

            def probs_hi_parts(g, first=False):
                if not first:
                    act.wait_ge(s["pv_done"], g)
                for q, tiles in ((0, 4), (1, 3)):
                    act.wait_ge(s["probs_transposed"], g * 2 + (q + 1))
                    nc.scalar.activation(probsT[0][:, 4 * q:4 * q + tiles, :], bank[4 + q][:, 0:tiles * P].rearrange("p (t q) -> p t q", q=T),
                                         ACT.Copy).then_inc(s["probsT_hi"], 1)

            hi_parts(0, range(4), first=True)
            hi_parts(1, range(3))
            exps(0, 0, first=True)
            ctx_hi_parts(0, 0, first=True)
            hi_parts(1, [3])
            probs_hi_parts(0, first=True)
            ctx_hi_parts(1, 1, first=True)
            with act.Fori(0, 3) as i:
                for j in range(RING):
                    g = i * RING + (j + 1)
                    hi_parts(g + 1, range(3))
                    exps(g, (j + 1) % 2)
                    hi_parts(g + 1, [3])
                    probs_hi_parts(g)
                    ctx_hi_parts(g + 1, (j + 2) % RING)
            exps(NG - 1, (NG - 1) % 2)
            probs_hi_parts(NG - 1)

            act.wait_ge(s["o_T"], 1)
            nc.scalar.activation(OT[:, :], bank[0][:, 0:D], ACT.Copy).then_inc(s["o_copied"], 1)
            act.wait_ge(s["var1_done"], 1)
            nc.scalar.activation(s_("sd", 0, 1), s_("mv", 1, 2), ACT.Sqrt, bias=s_("eps", 0, 1)).then_inc(s["sd1_done"], 1)
            nc.scalar.activation(s_("sd", 1, 2), s_("mv", 1, 2), ACT.Sqrt, bias=s_("eps", 1, 2), scale=1.0 + RMS_EPS).then_inc(s["sd1_done"], 1)
            link(nc.scalar.activation(s_("spare", 1, 2), s_("eps", 3, 4), ACT.Exp))
            act.wait_ge(s["u_ready"], 1)
            link(nc.scalar.activation(s_("au"), s_("u"), ACT.Abs))
            link(nc.scalar.activation(s_("sp"), s_("au"), ACT.Exp, scale=-1.0))
            nc.scalar.activation(s_("au"), s_("sp"), ACT.Ln, bias=s_("eps", 3, 4)).then_inc(s["ln1p_done"], 1)
            for i in range(2):
                act.wait_ge(s["proj_bank"], i + 1)
                for k in range(4):
                    n = 4 * CHANNELS[i] + k
                    last = nc.scalar.activation(qkvT[:, n, :], bank[1 + i][:, k * P:(k + 1) * P], ACT.Copy, scale=conv_w[:, n, 3:4])
                last.then_inc(s["tap0_done"], 1)
            for b in range(2):
                act.wait_ge(s["decay_done"], b + 1)
                nc.scalar.activation(DT[:, 4 * b:4 * b + 4, :], bank[0 if b == 0 else 7][:, :].rearrange("p (h t) -> p h t", h=4),
                                     ACT.Exp).then_inc(s["dt_done"], 1)
            for i in range(2):
                act.wait_ge(s["conv_done"], i + 1)
                at = slice(4 * CHANNELS[i], 4 * CHANNELS[i] + 4)
                nc.scalar.activation(qkvT[:, at, :], qkvT[:, at, :], ACT.Silu).then_inc(s["silu_done"], 1)
                act.wait_ge(s["silu_done"], i + 1)
                nc.scalar.activation(squares[:, at, :], qkvT[:, at, :], ACT.Square).then_inc(s["sq_done"], 1)
                if i == 0:
                    nc.scalar.activation(s_("beta"), s_("ba", 0, HV), ACT.Tanh, scale=0.5).then_inc(s["beta_done"], 1)
                act.wait_ge(s["proj_bank"], 3 + i)
                nc.scalar.activation(rawv[:, 4 * i:4 * i + 4, :], bank[3 + i][:, :].rearrange("p (h t) -> p h t", h=4), ACT.Copy).then_inc(s["raw_v"], 1)
            for b in range(2):
                act.wait_ge(s["x_T"], b + 1)
                nc.scalar.activation(X[:, 4 * b:4 * b + 4, :], bank[3 + b][:, :].rearrange("p (h t) -> p h t", h=4), ACT.Copy).then_inc(s["x_init"], 1)
            for b in range(2):
                act.wait_ge(s["z_done"], b + 1)
                nc.scalar.activation(zs[:, 4 * b:4 * b + 4, :], bank[5 + b][:, :].rearrange("p (h t) -> p h t", h=4), ACT.Silu).then_inc(s["zs_done"], 1)
            for b in range(2):
                act.wait_ge(s["conv_v"], b + 1)
                at = slice(2 * HK + 4 * b, 2 * HK + 4 * b + 4)
                nc.scalar.activation(qkvT[:, at, :], qkvT[:, at, :], ACT.Silu).then_inc(s["silu_done"], 1)
            act.wait_ge(s["kn_in"], 1)
            link(nc.scalar.activation(s_("kn"), s_("n2", HK, 2 * HK), ACT.Sqrt, bias=s_("eps", 2, 3)))
            for b in range(2):
                act.wait_ge(s["vT_done"], b + 1)
                for k in range(4):
                    h = 4 * b + k
                    last = nc.scalar.activation(Bv[:, h, :], bank[5 + b][:, k * P:(k + 1) * P], ACT.Copy, scale=s_("kn", h // 2, h // 2 + 1))
                last.then_inc(s["bv_done"], 1)
            for b in range(2):
                act.wait_ge(s["delta_mm"], b + 1)
                nc.scalar.activation(delta[:, 4 * b:4 * b + 4, :], bank[3 + b][:, :].rearrange("p (h t) -> p h t", h=4), ACT.Copy).then_inc(s["delta_done"], 1)
            act.wait_ge(s["o_mm"], 1)
            nc.scalar.activation(squares[:, 0:4, :], bank[5][:, :].rearrange("p (h t) -> p h t", h=4), ACT.Square).then_inc(s["osq_done"], 1)
            act.wait_ge(s["o_mm"], 2)
            for k in range(4):
                last = nc.scalar.activation(squares[:, 4 + k, :], bank[6][:, k * P:(k + 1) * P], ACT.Square, accum_out=s_("ms", 4 + k, 5 + k))
            last.then_inc(s["osq_done"], 1)
            for b in range(2):
                act.wait_ge(s["ms_done"], b + 1)
                nc.scalar.activation(s_("f", 4 * b, 4 * b + 4), s_("ms", 4 * b, 4 * b + 4), ACT.Sqrt).then_inc(s["f_sd"], 1)
                act.wait_ge(s["f_done"], b + 1)
                for k in (2, 3):
                    h = 4 * b + k
                    last = nc.scalar.activation(core[:, h, :], core[:, h, :], ACT.Copy, scale=s_("f", h, h + 1))
                last.then_inc(s["core_done2"], 1)
            for b in range(2):
                act.wait_ge(s["core_T"], b + 1)
                nc.scalar.activation(coreT[:, 4 * b:4 * b + 4, :], bank[3 + b][:, :].rearrange("p (h t) -> p h t", h=4), ACT.Copy,
                                     scale=early_at("gate_norm")).then_inc(s["coreT_done"], 1)
            act.wait_ge(s["h_done"], 1)
            link(nc.scalar.activation(scratch[:, :], hh[:, :], ACT.Square, accum_out=s_("sd", 0, 1)))
            nc.scalar.activation(s_("sd", 1, 2), s_("sd", 0, 1), ACT.Sqrt, scale=1.0 / D, bias=s_("eps", 2, 3)).then_inc(s["hsd_done"], 1)
            act.wait_ge(s["th_in"], 1)
            nc.scalar.activation(s_("th"), s_("dm", 0, 1), ACT.Tanh, scale=0.5).then_inc(s["th_done"], 1)
            for b in range(2):
                act.wait_ge(s["x2_done"], 1)
                act.wait_ge(s["gu_mm"], 2 * b + 1)
                nc.scalar.activation(gact[:, 4 * b:4 * b + 4, :], bank[3 + b][:, :].rearrange("p (h t) -> p h t", h=4), ACT.Silu,
                                     scale=s_("rs", 0, 1)).then_inc(s["gact_done"], 1)
            for b in range(2):
                act.wait_ge(s["prod_T"], b + 1)
                nc.scalar.activation(prodT[:, 4 * b:4 * b + 4, :], bank[3 + b][:, :].rearrange("p (h t) -> p h t", h=4), ACT.Copy).then_inc(s["prodT_done"], 1)
            act.wait_ge(s["x3_done"], 1)
            nc.scalar.activation(s_("sd", 0, 1), s_("mv", 1, 2), ACT.Sqrt, bias=s_("eps", 0, 1)).then_inc(s["ln3_sd"], 1)
            a = EARLY["rb1"][0]
            for i in (1, 3):
                act.wait_ge(s["r1_mm"], i + 1)
                for n in (2 * i, 2 * i + 1):
                    last = nc.scalar.activation(relT[:, n, :], half(bank[3 + i], n % 2), ACT.Relu, bias=E_sb[:, a + n:a + n + 1])
                last.then_inc(s["rel_done2"], 1)
            act.wait_ge(s["sc_in"], 1)
            nc.scalar.activation(s_("th"), s_("dm", 0, 1), ACT.Tanh, scale=0.5).then_inc(s["sc_th"], 1)
            a = EARLY["b1"][0]
            with act.Fori(0, E // SLOTS) as i:
                for j in range(SLOTS):
                    act.wait_ge(s["h_mm"], i * 8 + (2 * j + 1))
                    act.wait_ge(s["y_mm"], i * SLOTS + (j + 1))
                    for k in range(4):
                        last = nc.scalar.activation(hT[j % 2][:, k, :], bank[3 + 2 * (j % 2)][:, k * P:(k + 1) * P], ACT.Relu,
                                                    bias=E_sb[:, bass.ds(i * (SLOTS * FC) + (a + j * FC + k), 1)])
                    last.then_inc(s["hT_done"], 1)

            act.wait_ge(s["gate_T"], 1)
            nc.scalar.activation(gateT[:, :], bank[7][0:E, 0:P], ACT.Copy).then_inc(s["gateT_done"], 1)

        @block.vector
        def _(dve):
            V = nc.vector
            chain = [0]

            def link(ins):
                chain[0] += 1
                ins.then_inc(s["dve_chain"], 1)
                dve.wait_ge(s["dve_chain"], chain[0])

            def moments(t):
                link(V.bn_stats(s_("stats"), t))
                return V.bn_aggr(s_("mv"), s_("stats"))

            def lo_parts(g, quads):
                for q in quads:
                    dve.wait_ge(s["ctxT_hi"], g * 4 + (q + 1))
                    n = min(512, NC * P - 512 * q)
                    at = slice(512 * q, 512 * q + n)
                    V.tensor_tensor(ctxT[1][:, at], bank[CTX_BANKS[q]][:, 0:n], ctxT[0][:, at], ALU.subtract).then_inc(s["ctxT_lo"], 1)

            V.memset(s_("dummy", 0, 1), 0.0).then_inc(s["y_free"], 2)
            V.memset(s_("dummy", 1, 2), 0.0).then_inc(s["y_mm"], 2)
            V.memset(s_("dummy", 2, 3), 0.0).then_inc(s["acc_done"], 1)
            for j in range(EARLY_SLOTS):
                V.memset(s_("dummy", 3 + j, 4 + j), 0.0).then_inc(slot_in[j], 1)
            dve.wait_ge(s["early_in"], 16)
            moments(x).then_inc(s["ln_var"], 1)
            dve.wait_ge(s["ln_sd"], 1)
            link(V.reciprocal(s_("rs", 0, 1), s_("sd", 0, 1)))
            V.tensor_scalar(xn[:, :], x, s_("mv", 0, 1), s_("rs", 0, 1), ALU.subtract, ALU.mult).then_inc(s["ln_xn"], 1)
            V.tensor_scalar(s_("w1p"), early_at("w_ln1"), 1.0, None, ALU.add).then_inc(s["dve_chain"], 1)
            V.tensor_scalar(s_("w2p"), early_at("w_ln2"), 1.0, None, ALU.add).then_inc(s["dve_chain"], 1)
            chain[0] += 2
            dve.wait_ge(s["ln_T"], 1)
            V.tensor_copy(xT[:, :], bank[4][:, 0:D]).then_inc(s["ln_xT"], 1)
            dve.wait_ge(s["bv_ready"], 1)
            V.tensor_tensor(xb[:, :], bank[3][:, 0:D], x, ALU.add).then_inc(s["g_done"], 1)
            lo_parts(0, range(2))
            dve.wait_ge(s["g_ready"], 1)
            V.tensor_copy(s_("qb"), bank[6][:, D:D + 1]).then_inc(s["g_done"], 1)
            link(V.tensor_copy(G[0][:, :], bank[6][:, 0:D]))
            V.tensor_tensor(G[1][:, :], bank[6][:, 0:D], G[0][:, :], ALU.subtract).then_inc(s["g_done"], 1)
            dve.wait_ge(s["g_done"], 3)
            dve.wait_ge(s["consts_set"], 4)

            def maxima(g, b):
                dve.wait_ge(s["scores_ready"], g + 1)
                V.tensor_reduce(s_("mx"), psum[:, 2:4, 0:HALF], mybir.AxisListType.XY, ALU.max).then_inc(s["mx_done"], 1)
                dve.wait_ge(s["mx_done"], g * 2 + 1)
                V.tensor_scalar(s_("M", 1 - b, 2 - b), s_("mx"), s_("qb"), s_("M", b, b + 1), ALU.add, ALU.max).then_inc(s["mx_done"], 1)
                dve.wait_ge(s["mx_done"], g * 2 + 2)
                V.tensor_tensor(s_("dm", b, b + 1), s_("M", b, b + 1), s_("M", 1 - b, 2 - b), ALU.subtract).then_inc(s["dm_done"], 1)
                V.tensor_tensor(s_("nb"), s_("qb"), s_("M", 1 - b, 2 - b), ALU.subtract).then_inc(s["max_ready"], 1)

            def accumulate(g, b):
                dve.wait_ge(s["pv_done"], g + 1)
                dve.wait_ge(s["acc_done"], g + 1)
                V.scalar_tensor_tensor(O[:, :], O[:, :], s_("al", b, b + 1), bank[6][:, 0:D], ALU.mult, ALU.add).then_inc(s["acc_done"], 1)

            def sums(g, b):
                dve.wait_ge(s["exp_done"], g + 1)
                dve.wait_ge(s["alpha_done"], g + 1)
                dve.wait_ge(s["l_done"], g)
                V.scalar_tensor_tensor(s_("l"), s_("l"), s_("al", b, b + 1), s_("rowsum", b, b + 1), ALU.mult, ALU.add).then_inc(s["l_done"], 1)

            def probs_lo_parts(g):
                for q, tiles in ((0, 4), (1, 3)):
                    dve.wait_ge(s["probsT_hi"], g * 2 + (q + 1))
                    V.tensor_tensor(probsT[1][:, 4 * q:4 * q + tiles, :], bank[4 + q][:, 0:tiles * P].rearrange("p (t q) -> p t q", q=T),
                                    probsT[0][:, 4 * q:4 * q + tiles, :], ALU.subtract).then_inc(s["probsT_lo"], 1)

            lo_parts(0, [2, 3])
            maxima(0, 0)
            lo_parts(1, range(3))
            sums(0, 0)
            lo_parts(1, [3])
            probs_lo_parts(0)
            with dve.Fori(0, 3) as i:
                for j in range(RING):
                    g = i * RING + (j + 1)
                    maxima(g, (j + 1) % 2)
                    lo_parts(g + 1, range(3))
                    sums(g, (j + 1) % 2)
                    accumulate(i * RING + j, j % 2)
                    lo_parts(g + 1, [3])
                    probs_lo_parts(g)
            g = NG - 1
            maxima(g, g % 2)
            accumulate(g - 1, (g - 1) % 2)
            sums(g, g % 2)
            probs_lo_parts(g)
            accumulate(g, g % 2)

            dve.wait_ge(s["l_done"], NG)
            link(V.reciprocal(s_("rl"), s_("l")))
            link(V.tensor_scalar(s_("rl"), s_("rl"), NORM, None, ALU.mult))
            dve.wait_ge(s["att_ready"], 1)
            link(V.scalar_tensor_tensor(x1[:, :], bank[1][:, 0:D], s_("rl"), xb[:, :], ALU.mult, ALU.add))
            moments(x1[:, :]).then_inc(s["var1_done"], 1)
            dve.wait_ge(s["sd1_done"], 2)
            link(V.reciprocal(s_("rs"), s_("sd")))
            V.tensor_scalar(xn[:, :], x1[:, :], s_("mv", 0, 1), s_("rs", 1, 2), ALU.subtract, ALU.mult).then_inc(s["xz_done"], 1)
            V.tensor_scalar(h0[:, :], x1[:, :], s_("mv", 0, 1), s_("rs", 0, 1), ALU.subtract, ALU.mult).then_inc(s["h0_done"], 1)
            dve.wait_ge(s["xz_T"], 1)
            for c in range(DC):
                last = V.tensor_scalar(xT[:, c * P:(c + 1) * P], bank[0][:, c * P:(c + 1) * P], s_("w1p", c, c + 1), None, ALU.mult)
                if c == 0:
                    link(last)
            last.then_inc(s["xz_copied"], 1)
            dve.wait_ge(s["ba_done"], 1)
            V.tensor_copy(s_("ba"), bank[7][:, 0:2 * HV]).then_inc(s["ba_read"], 1)
            dve.wait_ge(s["ba_read"], 1)
            V.tensor_tensor(s_("u"), s_("ba", HV, 2 * HV), early_at("dt_bias"), ALU.add).then_inc(s["u_ready"], 1)

            dve.wait_ge(s["ln1p_done"], 1)
            link(V.scalar_tensor_tensor(s_("sp"), s_("u"), 0.0, s_("au"), ALU.max, ALU.add))
            link(V.scalar_tensor_tensor(s_("g"), s_("sp"), -1.0, s_("negA"), ALU.mult, ALU.mult))
            for h in range(HV):
                last = V.tensor_scalar(gstrict[:, h, :], strict, s_("g", h, h + 1), None, ALU.mult)
                if h < HV - 1:
                    last.then_inc(s["dve_chain"], 1)
            last.then_inc(s["gs_done"], 1)
            chain[0] += HV - 1

            def taps(i):
                dve.wait_ge(s["tap0_done"], i + 1)
                for d in (1, 2, 3):
                    for k in range(4):
                        n = 4 * CHANNELS[i] + k
                        last = V.scalar_tensor_tensor(qkvT[:, n, d:T], bank[1 + i][:, k * P:(k + 1) * P - d], conv_w[:, n, 3 - d:4 - d],
                                                      qkvT[:, n, d:T], ALU.mult, ALU.add)
                        last.then_inc(s["conv_done" if d == 3 and k == 3 else "dve_chain"], 1)
                    chain[0] += 4 if d < 3 else 3
                    dve.wait_ge(s["dve_chain"], chain[0])

            taps(0)
            taps(1)
            dve.wait_ge(s["beta_done"], 1)
            link(V.tensor_scalar(s_("beta"), s_("beta"), 0.5, 0.5, ALU.mult, ALU.add))
            dve.wait_ge(s["n2_done"], 1)
            V.tensor_copy(s_("n2", HK, 2 * HK), bank[0][:, HK:2 * HK]).then_inc(s["kn_in"], 1)
            dve.wait_ge(s["kn_in"], 1)
            link(V.tensor_scalar(s_("ki"), s_("n2", HK, 2 * HK), RMS_EPS, None, ALU.add))
            link(V.reciprocal(s_("ki"), s_("ki")))
            link(V.tensor_tensor(s_("kap").rearrange("p (k r) -> p k r", r=2), s_("beta").rearrange("p (k r) -> p k r", r=2),
                                 s_("ki").rearrange("p (k r) -> p k r", r=1).to_broadcast([P, HK, 2]), ALU.mult))
            dve.wait_ge(s["y_ident"], 1)
            for b in range(2):
                dve.wait_ge(s["dt_done"], b + 1)
                dve.wait_ge(s["gram_done"], b + 1)
                for k in range(4):
                    h = 4 * b + k
                    kh = h // 2
                    last = V.scalar_tensor_tensor(AW[:, h, :, :],
                                                  bank[1 + kh // 2][:, (kh % 2) * 256:(kh % 2) * 256 + 256].rearrange("p (a t) -> p a t", a=2),
                                                  s_("kap", h, h + 1), DT[:, h:h + 1, :].to_broadcast([P, 2, P]), ALU.mult, ALU.mult)
                    last.then_inc(s["aw_done"], 1)
                dve.wait_ge(s["aw_done"], 4 * b + 4)
                odd = AW[:, 4 * b:4 * b + 4, 0, :].rearrange("p h (n z) -> p h n z", z=2)[:, :, :, 1]
                tmp = delta[:, 4 * b:4 * b + 4, 0:64]
                link(V.scalar_tensor_tensor(tmp, odd, -1.0, m0.rearrange("p (a t) -> p a t", a=1).to_broadcast([P, 4, 64]), ALU.mult, ALU.mult))
                yo = Y[:, 4 * b:4 * b + 4, :].rearrange("p h (n z) -> p h n z", z=2)[:, :, :, 1]
                V.tensor_tensor(yo, yo, tmp, ALU.add).then_inc(s["y_init"], 1)

            dve.wait_ge(s["n2_done"], 2)
            V.tensor_scalar(s_("eq"), bank[0][:, 0:HK], P * RMS_EPS, P * RMS_EPS * RMS_EPS, ALU.mult, ALU.add).then_inc(s["n2_read"], 1)
            dve.wait_ge(s["n2_read"], 1)
            dve.wait_ge(s["y_init"], 2)
            dve.wait_ge(s["x_init"], 2)
            for lv in range(1, LEVELS):
                bs = 2 ** lv
                st = steps[lv % 2]

                def first(t, b, z):
                    return t[:, 4 * b:4 * b + 4, :].rearrange("p h (n z w) -> p h n z w", z=2, w=bs)[:, :, :, z, :]

                def four(t):
                    return t.rearrange("p (h n w) -> p h n w", h=4, w=bs)

                for b in range(2):
                    dve.wait_ge(s["t_mm"], 2 * (lv - 1) + b + 1)
                    dve.wait_ge(s["steps_zeroed"], max(2, lv))
                    m = masks[:, lv - 1:lv, :].to_broadcast([P, 4, 64]).rearrange("p h (n w) -> p h n w", w=bs)
                    V.tensor_tensor(first(st, b, 0), four(bank[0 if b == 0 else 7][:, 0:256]), m, ALU.mult).then_inc(s["t_done"], 1)
                for b in range(2):
                    dve.wait_ge(s["y_step"], 2 * (lv - 1) + b + 1)
                    V.tensor_tensor(first(Y, b, 1), first(Y, b, 1), four(bank[1 + b][:, 0:256]), ALU.subtract).then_inc(s["y_done"], 1)
                if lv < LEVELS - 1:
                    for b in range(2):
                        dve.wait_ge(s["x_T"], 2 * lv + b + 1)
                        V.tensor_copy(X[:, 4 * b:4 * b + 4, :], bank[3 + b][:, :].rearrange("p (h t) -> p h t", h=4)).then_inc(s["x_done"], 1)

            dve.wait_ge(s["zs_done"], 2)
            for b in range(2):
                dve.wait_ge(s["osq_done"], b + 1)
                if b == 0:
                    link(V.tensor_reduce(s_("ms", 0, 4), squares[:, 0:4, :], AX, ALU.add))
                ms = s_("ms", 4 * b, 4 * b + 4).rearrange("p (k r) -> p k r", r=2)
                V.scalar_tensor_tensor(ms, ms, 1.0 / P, s_("eq", 2 * b, 2 * b + 2).rearrange("p (k r) -> p k r", r=1).to_broadcast([P, 2, 2]),
                                       ALU.mult, ALU.add).then_inc(s["ms_done"], 1)
                V.tensor_tensor(core[:, 4 * b:4 * b + 4, :], bank[5 + b][:, :].rearrange("p (h t) -> p h t", h=4), zs[:, 4 * b:4 * b + 4, :],
                                ALU.mult).then_inc(s["zo_done"], 1)
                dve.wait_ge(s["f_sd"], b + 1)
                dve.wait_ge(s["zo_done"], b + 1)
                V.reciprocal(s_("f", 4 * b, 4 * b + 4), s_("f", 4 * b, 4 * b + 4)).then_inc(s["f_done"], 1)
                dve.wait_ge(s["f_done"], b + 1)
                for k in range(2):
                    h = 4 * b + k
                    last = V.tensor_scalar(core[:, h, :], core[:, h, :], s_("f", h, h + 1), None, ALU.mult)
                    if k == 0:
                        last.then_inc(s["dve_chain"], 1)
                last.then_inc(s["core_done"], 1)
                chain[0] += 1
            dve.wait_ge(s["h0_done"], 1)
            dve.wait_ge(s["out_mm"], 1)
            V.tensor_tensor(hh[:, :], bank[0][:, 0:D], h0[:, :], ALU.add).then_inc(s["h_done"], 1)
            dve.wait_ge(s["h_done"], 1)
            dve.wait_ge(s["x2_T"], 1)
            for c in range(DC):
                last = V.tensor_scalar(xT[:, c * P:(c + 1) * P], bank[1][:, c * P:(c + 1) * P], s_("w2p", c, c + 1), None, ALU.mult)
                if c == 0:
                    link(last)
            last.then_inc(s["x2_copied"], 1)
            dve.wait_ge(s["hsd_done"], 1)
            V.reciprocal(s_("rs", 0, 1), s_("sd", 1, 2)).then_inc(s["x2_done"], 1)
            dve.wait_ge(s["x2_done"], 1)
            link(V.tensor_tensor(xh[:, :], x1[:, :], hh[:, :], ALU.add))

            def gates(out, half_tanh, tanh_done, scale):
                link(V.max(s_("top"), s_("lg")))
                link(V.max_index(topi[:, :], s_("top"), s_("lg")))
                V.tensor_scalar(s_("dm", 0, 1), s_("top", 0, 1), s_("top", 1, 2), scale, ALU.subtract, ALU.mult).then_inc(s[half_tanh], 1)
                link(V.tensor_copy(s_("idf"), topi[:, :]))
                link(V.tensor_scalar(s_("e1"), early_at("iota"), s_("idf", 0, 1), None, ALU.is_equal))
                link(V.tensor_scalar(s_("e2"), early_at("iota"), s_("idf", 1, 2), None, ALU.is_equal))
                dve.wait_ge(s[tanh_done], 1)
                link(V.tensor_scalar(s_("w", 0, 1), s_("th"), 0.5, 0.5, ALU.mult, ALU.add))
                link(V.tensor_scalar(s_("w", 1, 2), s_("th"), -0.5, 0.5, ALU.mult, ALU.add))
                link(V.tensor_scalar(s_("e1"), s_("e1"), s_("w", 0, 1), None, ALU.mult))
                return V.scalar_tensor_tensor(out, s_("e2"), s_("w", 1, 2), s_("e1"), ALU.mult, ALU.add)

            dve.wait_ge(s["lg_mm"], 1)
            link(V.tensor_copy(s_("lg"), bank[1][:, D:D + E]))
            link(gates(s_("route"), "th_in", "th_done", s_("rs", 0, 1)))
            link(V.tensor_scalar(s_("route"), s_("route"), s_("rs", 0, 1), None, ALU.mult))
            for b in range(2):
                dve.wait_ge(s["gact_done"], b + 1)
                dve.wait_ge(s["gu_mm"], 2 * b + 2)
                for k in range(4):
                    e = 4 * b + k
                    V.scalar_tensor_tensor(prod[:, e, :], gact[:, e, :], s_("route", e, e + 1), bank[5 + b][:, k * P:(k + 1) * P], ALU.mult, ALU.mult)\
                        .then_inc(s["prod_done"], 1)
            dve.wait_ge(s["moe_mm"], 1)
            link(V.tensor_tensor(O[:, :], bank[0][:, 0:D], xh[:, :], ALU.add))
            moments(O[:, :]).then_inc(s["x3_done"], 1)
            dve.wait_ge(s["ln3_sd"], 1)
            link(V.reciprocal(s_("rs", 0, 1), s_("sd", 0, 1)))
            V.tensor_scalar(xn[:, :], O[:, :], s_("mv", 0, 1), s_("rs", 0, 1), ALU.subtract, ALU.mult).then_inc(s["xf_done"], 1)
            dve.wait_ge(s["xf_T"], 1)
            V.tensor_copy(xT[:, :], bank[1][:, 0:D]).then_inc(s["xf_copied"], 1)
            a = EARLY["rb1"][0]
            for i in (0, 2):
                dve.wait_ge(s["r1_mm"], i + 1)
                for n in (2 * i, 2 * i + 1):
                    last = V.tensor_scalar(relT[:, n, :], half(bank[3 + i], n % 2), E_sb[:, a + n:a + n + 1], 0.0, ALU.add, ALU.max)
                last.then_inc(s["rel_done"], 1)
            dve.wait_ge(s["sc_mm"], 1)
            link(V.tensor_tensor(s_("lg"), bank[0][:, D:D + E], early_at("rb2"), ALU.add))
            gates(s_("gate"), "sc_in", "sc_th", 1.0).then_inc(s["gate_done"], 1)
            dve.wait_ge(s["gate_done"], 1)
            a = EARLY["b1"][0]
            gcol = smalls["gate"][0]
            with dve.Fori(0, E // SLOTS) as i:
                for j in range(SLOTS):
                    dve.wait_ge(s["h_mm"], i * 8 + (2 * j + 2))
                    dve.wait_ge(s["y_mm"], i * SLOTS + (j + 1))
                    for k in range(4):
                        last = V.tensor_scalar(hT[j % 2][:, 4 + k, :], bank[4 + 2 * (j % 2)][:, k * P:(k + 1) * P],
                                               E_sb[:, bass.ds(i * (SLOTS * FC) + (a + j * FC + 4 + k), 1)], 0.0, ALU.add, ALU.max)
                    last.then_inc(s["hT2_done"], 1)
                    dve.wait_ge(s["y_mm"], i * SLOTS + (j + 3))
                    V.scalar_tensor_tensor(O[:, :], bank[1 + j % 2][:, 0:D], sm[:, bass.ds(i * SLOTS + (gcol + j), 1)], O[:, :], ALU.mult, ALU.add)\
                        .then_inc(s["y_free"], 1)
                    dve.wait_ge(s["y_free"], i * SLOTS + (j + 3))
            dve.wait_ge(s["b2_mm"], 1)
            V.tensor_tensor(O[:, :], bank[0][:, 0:D], O[:, :], ALU.add).then_inc(s["m_done"], 1)


def _chunks(w):
    k, n = w.shape
    return w.reshape(k // P, P, n).transpose(1, 0, 2).reshape(P, -1)


def _constants():
    import numpy as np
    s, t = np.arange(P)[:, None], np.arange(P)[None, :]
    out = {
        "ident": (s == t), "tri": (s <= t), "strict": (s > t),
        "negmask": np.where(t < s, -1e30, 0.0),
        "m0": (s == 2 * np.arange(P // 2)[None, :]),
        "iota": np.broadcast_to(np.arange(E), (P, E)), "ones": np.ones((P, 1)),
    }
    masks = []
    for lv in range(1, LEVELS):
        b = 2 ** lv
        col = np.arange(64)[None, :]
        masks.append((s // (2 * b) == col // b) & (s % (2 * b) >= b))
    out["masks"] = np.concatenate(masks, axis=1)
    return {k: v.astype(np.float32) for k, v in out.items()}


def kernel(**inputs):
    import numpy as np
    import concourse.bacc as bacc
    from concourse.bass_utils import run_bass_kernel_spmd

    a = {k: np.asarray(v) for k, v in inputs.items()}
    c = _constants()

    def rows(v):
        return np.broadcast_to(v[None, :], (P, v.shape[0]))

    def cols(v):
        return v.reshape(-1, P).T

    e = dict(c)
    e.update({
        "x": a["x"][0],
        "conv_w": a["L0_attn_conv_w"].reshape(NCH, P, 4).transpose(1, 0, 2).reshape(P, -1),
        "w_ln1": cols(a["L0_attn_w_ln1"]), "w_ln2": cols(a["L0_attn_w_ln2"]), "gate_norm": cols(a["L0_attn_gate_norm_w"]),
        "bq": cols(a["L0_xattn_bq"]), "bk": cols(a["L0_xattn_bk"]), "rb1": cols(a["L0_ffn_rb1"]),
        "b1": a["L0_ffn_b1"].reshape(E * FC, P).T,
        "dt_bias": rows(a["L0_attn_dt_bias"]), "A_log": rows(a["L0_attn_A_log"]), "rb2": rows(a["L0_ffn_rb2"]),
        "wq": _chunks(a["L0_xattn_Wq"]), "wkT": _chunks(a["L0_xattn_Wk"].T), "wv": _chunks(a["L0_xattn_Wv"]),
    })
    early = np.concatenate([e[name] for name in EARLY], axis=1)

    def by_input(w):
        return w.transpose(1, 0, 2).reshape(w.shape[1], -1)

    w1, w2 = a["L0_ffn_W1"], a["L0_ffn_W2"]
    experts = np.stack([np.concatenate([_chunks(w1[k]), _chunks(w2[k])], axis=1) for k in range(E)])
    late = {
        "qkvz": _chunks(a["L0_attn_W_qkvz"]), "ba": _chunks(a["L0_attn_W_ba"]), "out": _chunks(a["L0_attn_W_out"]),
        "gate": _chunks(by_input(a["L0_attn_W_gate_e"])), "up": _chunks(by_input(a["L0_attn_W_up_e"])),
        "down": a["L0_attn_W_down_e"].transpose(1, 0, 2).reshape(P, -1), "router": _chunks(a["L0_attn_W_router"]),
        "rw1": _chunks(a["L0_ffn_rw1"]), "rw2": _chunks(a["L0_ffn_rw2"]),
    }
    late = np.concatenate([late[name] for name in LATE] + [experts[k] for k in range(EARLY_SLOTS)], axis=1)
    late = np.pad(late, ((0, 0), (0, LATE_N - late.shape[1])))
    late = late.reshape(P, LATE_PARTS, PART_N).transpose(1, 0, 2)

    nc = bacc.Bacc("TRN2", target_bir_lowering=False, num_devices=1)
    arrays = {"early": early, "late": late, "experts": experts[EARLY_SLOTS:], "ctx": a["ctx_1024"][0],
              "bv": a["L0_xattn_bv"].reshape(1, D), "b2": a["L0_ffn_b2"]}
    arrays = {f"in_{k}": np.ascontiguousarray(v) for k, v in arrays.items()}
    args = [nc.dram_tensor(k, v.shape, mybir.dt.from_np(v.dtype), kind="ExternalInput").ap() for k, v in arrays.items()]
    args.append(nc.dram_tensor("out_0", (1, T, D), F32, kind="ExternalOutput").ap().rearrange("b t d -> (b t) d"))
    perceiver(nc, *args)
    r = run_bass_kernel_spmd(nc, [arrays], core_ids=[0])
    return r.results[0]["out_0"]
```

```python
from contextlib import ExitStack

import concourse.bass as bass
from concourse import mybir

P = 128
T = 128
D = 256
DC = D // P
S = 12544
GT = 7
NG = S // P // GT
RING = 4
GK = GT * P
HALF = GK // 2
NC = DC * GT
HK, HV = 4, 8
KEY, VAL = HK * P, HV * P
CONV = 2 * KEY + VAL
NCH = CONV // P
E = 8
FF = 1024
FC = FF // P
SLOTS = 4
LEVELS = 7
CHANNELS = (1, 0, 2, 3)
POOL_CHUNKS = 5
BLOCK_LEVEL = 5
V_LEVELS = (4, 5)
CTX_BANKS = (0, 1, 7, 0)
LN_EPS, RMS_EPS = 1e-5, 1e-6
NORM = 1.0 / 16.0

F32 = mybir.dt.float32
F32R = mybir.dt.float32r
U32 = mybir.dt.uint32
ALU = mybir.AluOpType
ACT = mybir.ActivationFunctionType
AX = mybir.AxisListType.X


def columns(sizes):
    at, out = 0, {}
    for name, n in sizes:
        out[name] = (at, at + n)
        at += n
    return out, at


EARLY, EARLY_N = columns([
    ("x", D), ("ident", P), ("w_ln1", DC), ("w_ln2", DC), ("bq", DC), ("bk", DC), ("A_log", HV),
    ("wq", DC * D), ("wkT", DC * D), ("wv", DC * D),
    ("tri", P), ("strict", P), ("m0", P // 2),
    ("masks", 64 * (BLOCK_LEVEL - 1)), ("iota", E), ("ones", 1),
    ("conv_w", 4 * NCH), ("gate_norm", 1),
    ("rb1", FC), ("b1", E * FC), ("dt_bias", HV), ("rb2", E)])
EARLY_CUTS = (0, EARLY["wq"][0], EARLY["wv"][0], EARLY_N)
LATE, LATE_USED = columns([
    ("qkvz", DC * (CONV + VAL)), ("ba", DC * 2 * HV), ("out", HV * D), ("gate", DC * E * P),
    ("up", DC * E * P), ("down", E * D), ("router", DC * E), ("rw1", DC * FF), ("rw2", FC * E)])
EXPERT_N = DC * FF + FC * D
LATE_PARTS = NG - RING
EARLY_SLOTS = 2
PART_N = -(-(LATE_USED + EARLY_SLOTS * EXPERT_N) // LATE_PARTS)
LATE_N = PART_N * LATE_PARTS
assert NG * GK == S


def perceiver(nc, early, late, experts, ctx, bv, b2, out):
    with ExitStack() as stack:
        def sb(name, cols, dt=F32, rows=P):
            return stack.enter_context(nc.sbuf_tensor(name, [rows, cols], dt))

        def sem(name):
            return stack.enter_context(nc.semaphore(name))

        E_sb = sb("early_sb", EARLY_N)
        W_sb = sb("late_sb", LATE_N)
        with ExitStack() as overlay:
            w2_hi, h_hi = [overlay.enter_context(nc.sbuf_tensor(name, [P, cols], F32R)) for name, cols in
                           (("w2_hi", 2 * FC * D), ("h_hi", 2 * FF))]
        R1 = sb("ring", RING * GT * D)
        def parts(overlay, name, cols):
            return [overlay.enter_context(nc.sbuf_tensor(f"{name}_{part}", [P, cols], F32R)) for part in ("hi", "lo")]

        with ExitStack() as overlay:
            ctxN = parts(overlay, "ctx", 2 * GT * D)
        late_slots = sb("late_slots", (SLOTS - EARLY_SLOTS) * EXPERT_N)
        with ExitStack() as overlay:
            ctxT = parts(overlay, "ctxT", NC * P)
            G = parts(overlay, "G", D)
            PT = parts(overlay, "probsT", GK)
        with ExitStack() as overlay:
            w2_lo, h_lo = [overlay.enter_context(nc.sbuf_tensor(name, [P, cols], F32R)) for name, cols in
                           (("w2_lo", 2 * FC * D), ("h_lo", 2 * FF))]
        R2 = sb("work", 8192)
        bv_sb = R2[0:1, 7296:7552]
        sixteenth = R2[0:1, 7552:7552 + P]
        gateT = R2[0:E, 7168:7168 + P]
        b2_sb = sb("b2_sb", D, rows=E)
        psum = stack.enter_context(nc.psum_tensor("psum", [P, 8, 512], F32))
        bank = [psum[:, i, :] for i in range(8)]

        def early_at(name):
            a, b = EARLY[name]
            return E_sb[:, a:b]

        def late_at(name, **kw):
            a, b = LATE[name]
            return W_sb[:, a:b].rearrange("p (c n) -> p c n", **kw)

        x = early_at("x")
        ident = early_at("ident")
        tri = early_at("tri")
        strict = early_at("strict")
        m0 = early_at("m0")
        masks = early_at("masks").rearrange("p (l c) -> p l c", c=64)
        ones = early_at("ones")
        conv_w = early_at("conv_w").rearrange("p (c j) -> p c j", j=4)
        wq = early_at("wq").rearrange("p (c n) -> p c n", c=DC)
        wkT = early_at("wkT").rearrange("p (c n) -> p c n", c=DC)
        wv = early_at("wv").rearrange("p (c n) -> p c n", c=DC)
        w_qkvz = late_at("qkvz", c=DC)
        w_ba = late_at("ba", c=DC)
        w_out = late_at("out", c=HV)
        w_gate = late_at("gate", c=DC)
        w_up = late_at("up", c=DC)
        w_down = late_at("down", c=E)
        w_router = late_at("router", c=DC)
        rw1 = late_at("rw1", c=DC)
        rw2 = late_at("rw2", c=FC)
        slots = [W_sb[:, LATE_USED + j * EXPERT_N:LATE_USED + (j + 1) * EXPERT_N] for j in range(EARLY_SLOTS)]
        slots += [late_slots[:, bass.ts(j, EXPERT_N)] for j in range(SLOTS - EARLY_SLOTS)]

        ring = R1[:, :].rearrange("p (r t d) -> p r t d", r=RING, d=D)
        ctxTv = [part[:, :].rearrange("p (c k) -> p c k", c=DC) for part in ctxT]
        probs = R2[:, 5888:5888 + GK]
        ctxNv = [part[:, :].rearrange("p (b t d) -> p b t d", b=2, d=D) for part in ctxN]
        probsT = [part[:, :].rearrange("p (t q) -> p t q", q=T) for part in PT]
        AW = R1[:, 0:2048].rearrange("p (h a t) -> p h a t", h=HV, a=2)
        DT = R1[:, 2048:3072].rearrange("p (h t) -> p h t", h=HV)
        gstrict = R1[:, 3072:4096].rearrange("p (h t) -> p h t", h=HV)
        X = R1[:, 4096:5120].rearrange("p (h t) -> p h t", h=HV)
        Y = R1[:, 5120:6144].rearrange("p (h t) -> p h t", h=HV)
        Bv = R1[:, 6144:7168].rearrange("p (h t) -> p h t", h=HV)
        qkvT = R2[:, 0:2048].rearrange("p (c t) -> p c t", c=NCH)
        squares = R2[:, 2048:3072].rearrange("p (c t) -> p c t", c=2 * HK)
        zs = R2[:, 3072:4096].rearrange("p (h t) -> p h t", h=HV)
        steps = [R2[:, 4096 + 1024 * i:5120 + 1024 * i].rearrange("p (h t) -> p h t", h=HV) for i in range(2)]
        delta = R2[:, 6144:7168].rearrange("p (h t) -> p h t", h=HV)
        core = R2[:, 7168:8192].rearrange("p (h t) -> p h t", h=HV)
        rawv = core
        tap = gstrict
        coreT = R1[:, 2048:3072].rearrange("p (h t) -> p h t", h=HV)
        gact = R1[:, 0:1024].rearrange("p (e i) -> p e i", e=E)
        prod = R1[:, 1024:2048].rearrange("p (e i) -> p e i", e=E)
        prodT = R1[:, 3072:4096].rearrange("p (e i) -> p e i", e=E)
        relT = R2[:, 6144:7168].rearrange("p (c t) -> p c t", c=FC)
        h32 = R1[:, 6144:7168].rearrange("p (c t) -> p c t", c=FC)
        hT = [part[:, :].rearrange("p (z c t) -> p z c t", z=2, c=FC) for part in (h_hi, h_lo)]
        w2 = [part[:, :].rearrange("p (z c n) -> p z c n", z=2, c=FC) for part in (w2_hi, w2_lo)]

        warm = sb("warm", P)
        xn = sb("xn", D)
        xT = sb("xT", D)
        QT = R2[:, 6784:7040]
        OT = R2[:, 7040:7296]
        scratch = R2[:, 7680:7936]
        hh = sb("hh", D)
        O = sb("O", D)
        xb = sb("xb", D)
        x1 = sb("x1", D)
        h0, xh = x, xb
        smalls, SMALL_N = columns([
            ("stats", 6), ("mv", 2), ("sd", 2), ("rs", 2), ("qb", 1), ("M", 2), ("mx", 1), ("nb", 1), ("dm", 2),
            ("al", 2), ("rowsum", 2), ("l", 1), ("rl", 1), ("w1p", DC), ("w2p", DC), ("negA", HV), ("beta", HV),
            ("u", HV), ("au", HV), ("sp", HV), ("g", HV), ("ba", 2 * HV), ("n2", 2 * HK), ("kap", HV), ("ki", HK), ("kn", HK), ("eq", HK),
            ("ms", HV), ("f", HV), ("lg", E), ("top", 8), ("w", 2), ("th", 1), ("idf", 8), ("e1", E), ("e2", E),
            ("route", E), ("gate", E), ("eps", 4), ("marks", 8), ("spare", 2)])
        sm = sb("smalls", SMALL_N)
        topi = sb("topi", 8, U32)

        def s_(name, a=0, b=None):
            lo, hi = smalls[name]
            return sm[:, lo + a:(hi if b is None else lo + b)]

        names = """early_in tables_in rows_in late_in out_done
            consts_set warm_set eps_set
            wqk_in dve_chain act_chain pool_chain conv_v steps_zeroed y_free mx_done l_done out_ready y_ident
            ln_var ln_sd ln_xn ln_T ln_xT q_ready q_done g_ready g_done bv_ready
            ctx_transposed ctxT_hi ctxT_lo ctx_hi ctx_lo probsT_hi scores_ready max_ready exp_done alpha_done probs_transposed probsT_lo pv_done acc_done
            o_T o_copied att_ready
            var1_done sd1_done xz_done xz_T xz_copied_dve xz_copied_act x2_copied_act ba_done ba_read u_ready ln1p_done rates_done gs_done
            proj_bank tap0_done conv_done silu_done z_done zs_done
            beta_done sq_done n2_done n2_read kn_in decay_done exp_decay dt_done gram_done aw_done vT_done bv_done
            y_init x_T x_init t_mm t_done ty_mm y_done delta_mm delta_done o_mm osq_done ms_done f_sd f_done core_dve core_act zo_done raw_v core_T coreT_done
            out_mm h_done hsd_done x2_done x2_T x2_copied_dve lg_mm th_in th_done gu_mm gact_done prod_done prod_T prodT_done
            moe_mm x3_done ln3_sd xf_done xf_T xf_copied r1_mm rel_dve rel_act sc_mm sc_in sc_th gate_done gate_T gateT_done b2_mm
            h_mm w2_hi_done w2_lo_pool w2_lo_dve h_act h_dve h_hi_done h_lo_done y_mm h0_done""".split()
        s = {n: sem(n) for n in names}
        ctx_in = [sem(f"ctx_in{r}") for r in range(RING)]
        x_done = [sem(f"x_done{r}") for r in range(2)]
        slot_in = [sem(f"slot_in{r}") for r in range(SLOTS)]

        def half(t, c):
            return t[:, c * P:(c + 1) * P]

        def block_pairs(bs):
            return [(slice(r, r + bs), slice(r + bs, r + 2 * bs)) for r in range(0, P, 2 * bs)]

        def slot_full(i, j):
            return i * 16 + (1 if j < EARLY_SLOTS else 16)

        def slot_w2(j):
            return slots[j][:, DC * FF:EXPERT_N].rearrange("p (c n) -> p c n", c=FC)

        block = stack.enter_context(nc.Block())

        @block.sync
        def _(sp):
            def early_part(i, done):
                at = slice(EARLY_CUTS[i], EARLY_CUTS[i + 1])
                sp.dma_start(E_sb[:, at], early[:, at]).then_inc(s[done], 16)

            early_part(0, "early_in")
            early_part(1, "wqk_in")
            sp.dma_start(bv_sb[:, :], bv).then_inc(s["rows_in"], 16)
            sp.dma_start(b2_sb[:, :], b2).then_inc(s["rows_in"], 16)

            ctx_g = ctx.rearrange("(p g t) d -> p g (t d)", p=P, g=NG)
            R1g = R1[:, :].rearrange("p (r n) -> p r n", r=RING)

            def group(g, r):
                sp.dma_start(R1g[:, r, :], ctx_g[:, g, :]).then_inc(ctx_in[r], 16)

            def part(i):
                sp.dma_start(W_sb[:, bass.ts(i, PART_N)], late[i, :, :]).then_inc(s["late_in"], 16)

            group(0, 0)
            early_part(2, "tables_in")
            for r in range(1, RING):
                group(r, r)
            with sp.Fori(0, 2) as i:
                for r in range(RING):
                    part(i * RING + r)
                    sp.wait_ge(s["ctx_lo"], i * RING + (r + 1))
                    group(i * RING + (RING + r), r)
            for r in range(2):
                part(2 * RING + r)
                sp.wait_ge(s["ctx_lo"], 2 * RING + r + 1)
                group(3 * RING + r, r)
            sp.wait_ge(s["pv_done"], NG)
            for j in range(EARLY_SLOTS, SLOTS):
                sp.dma_start(slots[j], experts[j - EARLY_SLOTS, :, :]).then_inc(slot_in[j], 16)
            for j in range(SLOTS):
                sp.wait_ge(s["y_mm"], j + 3)
                sp.dma_start(slots[j], experts[SLOTS - EARLY_SLOTS + j, :, :]).then_inc(slot_in[j], 16)
            sp.wait_ge(s["out_ready"], 1)
            sp.dma_start(out, O[:, :]).then_inc(s["out_done"], 16)
            sp.wait_ge(s["out_done"], 16)

        @block.gpsimd
        def _(pool):
            nc.gpsimd.memset(warm[:, :], 1.0).then_inc(s["warm_set"], 1)
            nc.gpsimd.memset(s_("eps", 0, 1), LN_EPS).then_inc(s["eps_set"], 1)
            nc.gpsimd.memset(s_("eps", 1, 2), LN_EPS * RMS_EPS).then_inc(s["eps_set"], 1)
            nc.gpsimd.memset(s_("eps", 2, 3), RMS_EPS).then_inc(s["eps_set"], 1)
            nc.gpsimd.memset(s_("eps", 3, 4), 1.0).then_inc(s["eps_set"], 1)
            nc.gpsimd.memset(sixteenth[:, :], NORM).then_inc(s["consts_set"], 1)
            nc.gpsimd.memset(O[:, :], 0.0).then_inc(s["consts_set"], 1)
            nc.gpsimd.memset(s_("l"), 0.0).then_inc(s["consts_set"], 1)
            nc.gpsimd.memset(s_("M", 0, 1), -3e38).then_inc(s["consts_set"], 1)

            def ctx_lo_parts(g, r):
                pool.wait_ge(s["ctx_hi"], g + 1)
                nc.gpsimd.tensor_tensor(ctxNv[1][:, r % 2], ring[:, r], ctxNv[0][:, r % 2], ALU.subtract).then_inc(s["ctx_lo"], 1)

            with pool.Fori(0, 3) as i:
                for j in range(RING):
                    ctx_lo_parts(i * RING + j, j)
            for g in range(3 * RING, NG):
                ctx_lo_parts(g, g % RING)
            pool.wait_ge(s["pv_done"], NG)
            pool.wait_ge(s["early_in"], 16)
            nc.gpsimd.tensor_copy(Y, ident.rearrange("p (a t) -> p a t", a=1).to_broadcast([P, HV, P])).then_inc(s["y_ident"], 1)
            for i in range(2):
                nc.gpsimd.memset(steps[i], 0.0).then_inc(s["steps_zeroed"], 1)
            pool.wait_ge(s["tables_in"], 16)
            pool.wait_ge(s["rates_done"], 1)
            nc.gpsimd.tensor_tensor(gstrict, strict.rearrange("p (a t) -> p a t", a=1).to_broadcast([P, HV, T]),
                                    s_("g").rearrange("p (h t) -> p h t", t=1).to_broadcast([P, HV, T]), ALU.mult).then_inc(s["gs_done"], 1)
            for b in range(2):
                pool.wait_ge(s["exp_decay"], b + 1)
                d = DT[:, 4 * b:4 * b + 4, :]
                nc.gpsimd.tensor_tensor(d, d, tri.rearrange("p (a t) -> p a t", a=1).to_broadcast([P, 4, T]), ALU.mult).then_inc(s["dt_done"], 1)
            for b in range(2):
                pool.wait_ge(s["raw_v"], b + 1)
                chunks = slice(2 * HK + 4 * b, 2 * HK + 4 * b + 4)
                for d in range(4):
                    w = conv_w[:, chunks, 3 - d:4 - d].to_broadcast([P, 4, T - d])
                    product = qkvT[:, chunks, :] if d == 0 else tap[:, 4 * b:4 * b + 4, d:T]
                    nc.gpsimd.tensor_tensor(product, rawv[:, 4 * b:4 * b + 4, 0:T - d], w, ALU.mult).then_inc(s["pool_chain"], 1)
                    pool.wait_ge(s["pool_chain"], 6 * b + max(1, 2 * d))
                    if d > 0:
                        nc.gpsimd.tensor_tensor(qkvT[:, chunks, d:T], qkvT[:, chunks, d:T], product, ALU.add)\
                            .then_inc(s["conv_v" if d == 3 else "pool_chain"], 1)
                        pool.wait_ge(s["conv_v"] if d == 3 else s["pool_chain"], b + 1 if d == 3 else 6 * b + 2 * d + 1)
            for lv in range(3, LEVELS):
                pool.wait_ge(s["ty_mm"], 2 * (lv - 2))
                nc.gpsimd.memset(steps[lv % 2], 0.0).then_inc(s["steps_zeroed"], 1)

            with pool.Fori(0, E // SLOTS) as i:
                for j in range(SLOTS):
                    e = i * SLOTS + j
                    pool.wait_ge(s["w2_hi_done"], e + 1)
                    at = slice(0, POOL_CHUNKS)
                    nc.gpsimd.tensor_tensor(w2[1][:, j % 2, at], slot_w2(j)[:, at], w2[0][:, j % 2, at], ALU.subtract).then_inc(s["w2_lo_pool"], 1)

        @block.tensor
        def _(pe):
            def keep_warm(n):
                for _ in range(n):
                    nc.tensor.matmul(bank[7][:, 0:P], warm[:, :], warm[:, :], start=True, stop=True)

            def transposes(pairs, done):
                for o, i in pairs:
                    last = nc.tensor.transpose(o, i, ident)
                last.then_inc(done, 1)

            def wide(o, lhs, rhs, n=DC):
                for c in range(n):
                    last = nc.tensor.matmul(o, lhs(c), rhs(c), start=(c == 0), stop=(c == n - 1))
                return last

            def ctx_transposes(g, r, quads):
                for q in quads:
                    if q == 3:
                        pe.wait_ge(s["ctxT_lo"], g * 4 + 1)
                    blocks = range(4 * q, min(4 * q + 4, NC))
                    transposes([(bank[CTX_BANKS[q]][:, (b % 4) * P:(b % 4 + 1) * P],
                                 ring[:, r, b % GT, (b // GT) * P:(b // GT + 1) * P]) for b in blocks],
                               s["ctx_transposed"])

            pe.wait_ge(s["warm_set"], 1)
            keep_warm(8)
            pe.wait_ge(s["early_in"], 16)
            pe.wait_ge(s["ln_xn"], 1)
            transposes([(half(bank[4], c), half(xn, c)) for c in range(DC)], s["ln_T"])
            pe.wait_ge(s["rows_in"], 32)
            pe.wait_ge(s["wqk_in"], 16)
            pe.wait_ge(s["consts_set"], 4)
            nc.tensor.matmul(bank[3][:, 0:D], sixteenth[:, :], bv_sb[:, :], start=True, stop=True).then_inc(s["bv_ready"], 1)
            pe.wait_ge(s["ln_xT"], 1)
            for m in range(DC):
                last = wide(half(bank[5], m), lambda c: wq[:, c, m * P:(m + 1) * P], lambda c: half(xT, c))
            last.then_inc(s["q_ready"], 1)
            pe.wait_ge(ctx_in[0], 16)
            ctx_transposes(0, 0, range(2))
            pe.wait_ge(s["q_done"], 2)
            for m in range(DC):
                wide(half(bank[6], m), lambda c: wkT[:, c, m * P:(m + 1) * P], lambda c: half(QT, c))
            a = EARLY["bk"][0]
            wide(bank[6][:, D:D + 1], lambda c: half(QT, c), lambda c: E_sb[:, a + c:a + c + 1]).then_inc(s["g_ready"], 1)

            def scores(g, first=False):
                if not first:
                    pe.wait_ge(s["exp_done"], g)
                for hf in range(2):
                    pe.wait_ge(s["ctxT_lo"], g * 4 + (3 + hf))
                    terms = [(a, b, c) for a, b in ((0, 0), (1, 0), (0, 1)) for c in range(DC)]
                    for i, (a, b, c) in enumerate(terms):
                        last = nc.tensor.matmul(bank[2 + hf][:, 0:HALF], G[a][:, c * P:(c + 1) * P],
                                                ctxTv[b][:, c, hf * HALF:(hf + 1) * HALF], start=(i == 0), stop=(i == len(terms) - 1))
                last.then_inc(s["scores_ready"], 1)

            def probs_transposes(g, first=False):
                pe.wait_ge(s["exp_done"], g + 1)
                if not first:
                    pe.wait_ge(s["probsT_lo"], g * 2)
                for q, tiles in ((0, range(0, 4)), (1, range(4, 7))):
                    transposes([(bank[4 + q][:, (t % 4) * P:(t % 4 + 1) * P], probs[:, t * P:(t + 1) * P]) for t in tiles],
                               s["probs_transposed"])

            def attend(g, r, first=False):
                if not first:
                    pe.wait_ge(s["acc_done"], g + 1)
                pe.wait_ge(s["ctx_lo"], g + 1)
                terms = [(t, a, b) for tiles in (range(4), range(4, GT)) for a, b in ((0, 0), (1, 0), (0, 1)) for t in tiles]
                for i, (t, a, b) in enumerate(terms):
                    if i == 0:
                        pe.wait_ge(s["probsT_lo"], g * 2 + 1)
                    if i == 4 * 3:
                        pe.wait_ge(s["probsT_lo"], g * 2 + 2)
                    last = nc.tensor.matmul(bank[6][:, 0:D], probsT[a][:, t, :], ctxNv[b][:, r % 2, t, :],
                                            start=(i == 0), stop=(i == len(terms) - 1))
                last.then_inc(s["pv_done"], 1)

            ctx_transposes(0, 0, [2, 3])
            pe.wait_ge(s["g_done"], 3)
            scores(0, first=True)
            pe.wait_ge(ctx_in[1], 16)
            ctx_transposes(1, 1, range(4))
            probs_transposes(0, first=True)
            with pe.Fori(0, 3) as i:
                for j in range(RING):
                    g = i * RING + (j + 1)
                    scores(g)
                    r = (j + 2) % RING
                    pe.wait_ge(ctx_in[r], i * 16 + (32 if j >= 2 else 16))
                    ctx_transposes(i * RING + (j + 2), r, range(3))
                    attend(i * RING + j, j)
                    ctx_transposes(i * RING + (j + 2), r, [3])
                    probs_transposes(g)
            scores(NG - 1)
            attend(NG - 2, (NG - 2) % RING)
            probs_transposes(NG - 1)
            attend(NG - 1, (NG - 1) % RING)
            pe.wait_ge(s["tables_in"], 16)
            pe.wait_ge(s["acc_done"], NG + 1)
            transposes([(half(bank[0], c), half(O, c)) for c in range(DC)], s["o_T"])
            pe.wait_ge(s["o_copied"], 1)
            wide(bank[1][:, 0:D], lambda c: half(OT, c), lambda c: wv[:, c, :]).then_inc(s["att_ready"], 1)

            keep_warm(11)
            pe.wait_ge(s["late_in"], 16 * LATE_PARTS)
            pe.wait_ge(s["xz_done"], 1)
            transposes([(bank[5 + c][:, 0:P], half(xn, c)) for c in range(DC)], s["xz_T"])
            keep_warm(3)
            pe.wait_ge(s["xz_copied_dve"], 1)
            pe.wait_ge(s["xz_copied_act"], 1)
            wide(bank[7][:, 0:2 * HV], lambda c: half(xT, c), lambda c: w_ba[:, c, :]).then_inc(s["ba_done"], 1)

            def project(i):
                for k in range(4):
                    n = 4 * CHANNELS[i] + k
                    last = wide(bank[1 + i][:, k * P:(k + 1) * P], lambda c: w_qkvz[:, c, n * P:(n + 1) * P], lambda c: half(xT, c))
                last.then_inc(s["proj_bank"], 1)

            def project_z(b):
                wide(bank[5 + b][:, :], lambda c: half(xT, c),
                     lambda c: w_qkvz[:, c, CONV + 512 * b:CONV + 512 * (b + 1)]).then_inc(s["z_done"], 1)

            project(0)
            project(1)
            project(2)
            pe.wait_ge(s["gs_done"], 1)
            pe.wait_ge(s["ba_read"], 1)
            for b in range(2):
                for k in range(4):
                    last = nc.tensor.matmul(bank[0 if b == 0 else 7][:, k * P:(k + 1) * P], gstrict[:, 4 * b + k, :], tri, start=True, stop=True)
                last.then_inc(s["decay_done"], 1)
            project(3)
            project_z(0)
            pe.wait_ge(s["exp_decay"], 1)
            pe.wait_ge(s["sq_done"], 1)

            def lengths(first):
                for c in range(first, first + HK):
                    last = nc.tensor.matmul(bank[0][:, c:c + 1], squares[:, c, :], ones[:, 0:1], start=True, stop=True)
                last.then_inc(s["n2_done"], 1)

            def gram(k, other):
                o = bank[1 + k // 2][:, (k % 2) * 256 + other * P:(k % 2) * 256 + (other + 1) * P]
                return nc.tensor.matmul(o, qkvT[:, HK + k, :], qkvT[:, HK + k if other == 0 else k, :], start=True, stop=True)

            lengths(HK)
            for k in range(2):
                gram(k, 0)
            pe.wait_ge(s["silu_done"], 2)
            for k in range(2):
                last = gram(k, 1)
            last.then_inc(s["gram_done"], 1)
            for k in range(2, HK):
                gram(k, 0)
                last = gram(k, 1)
            last.then_inc(s["gram_done"], 1)
            pe.wait_ge(s["sq_done"], 2)
            pe.wait_ge(s["kn_in"], 1)
            lengths(0)
            pe.wait_ge(s["raw_v"], 2)
            for b in range(2):
                pe.wait_ge(s["y_init"], b + 1)
                transposes([(bank[3 + b][:, k * P:(k + 1) * P], Y[:, 4 * b + k, :]) for k in range(4)], s["x_T"])
                if b == 0:
                    project_z(1)
            pe.wait_ge(s["n2_read"], 1)
            for lv in range(1, LEVELS):
                bs = 2 ** lv
                for b in range(2):
                    if lv == 1:
                        pe.wait_ge(s["x_init"], b + 1)
                    else:
                        pe.wait_ge(x_done[b], lv - 1)
                    for k in range(4):
                        h = 4 * b + k
                        o = bank[0 if b == 0 else 7][:, k * 64:(k + 1) * 64]
                        if lv < BLOCK_LEVEL:
                            last = nc.tensor.matmul(o.rearrange("p (n w) -> p n w", w=bs), AW[:, h, 0, :],
                                                    X[:, h, :].rearrange("p (n z w) -> p n z w", z=2, w=bs)[:, :, 0, :], start=True, stop=True)
                        else:
                            for i, (one, two) in enumerate(block_pairs(bs)):
                                last = nc.tensor.matmul(o[two, i * bs:(i + 1) * bs], AW[:, h, 0, two], X[:, h, one], start=True, stop=True)
                    last.then_inc(s["t_mm"], 1)
                for b in range(2):
                    pe.wait_ge(s["t_done"], 2 * (lv - 1) + b + 1)
                    st = steps[lv % 2]
                    for k in range(4):
                        h = 4 * b + k
                        o = bank[1 + b][:, k * 64:(k + 1) * 64]
                        if lv < BLOCK_LEVEL:
                            last = nc.tensor.matmul(o.rearrange("p (n w) -> p n w", w=bs), st[:, h, :],
                                                    Y[:, h, :].rearrange("p (n z w) -> p n z w", z=2, w=bs)[:, :, 1, :], start=True, stop=True)
                        else:
                            for i, (one, two) in enumerate(block_pairs(bs)):
                                last = nc.tensor.matmul(o[one, i * bs:(i + 1) * bs], st[:, h, one], Y[:, h, two], start=True, stop=True)
                    last.then_inc(s["ty_mm"], 1)
                if lv < LEVELS - 1:
                    for b in range(2):
                        pe.wait_ge(s["y_done"], 2 * (lv - 1) + b + 1)
                        transposes([(bank[3 + b][:, k * P:(k + 1) * P], Y[:, 4 * b + k, :]) for k in range(4)], s["x_T"])
                        if lv in V_LEVELS:
                            pe.wait_ge(s["zs_done"], 2)
                            pe.wait_ge(s["silu_done"], 4)
                            half_bank = 2 * V_LEVELS.index(lv) + b
                            for h in (2 * half_bank, 2 * half_bank + 1):
                                last = nc.tensor.transpose(bank[5 + h // 4][:, (h % 4) * P:(h % 4 + 1) * P], qkvT[:, 2 * HK + h, :], ident)
                            last.then_inc(s["vT_done"], 1)
            for b in range(2):
                pe.wait_ge(s["y_done"], 2 * (LEVELS - 2) + b + 1)
                pe.wait_ge(s["bv_done"], 2)
                for k in range(4):
                    last = nc.tensor.matmul(bank[3 + b][:, k * P:(k + 1) * P], Y[:, 4 * b + k, :], Bv[:, 4 * b + k, :], start=True, stop=True)
                last.then_inc(s["delta_mm"], 1)
            for b in range(2):
                pe.wait_ge(s["delta_done"], b + 1)
                for k in range(4):
                    last = nc.tensor.matmul(bank[5 + b][:, k * P:(k + 1) * P], AW[:, 4 * b + k, 1, :], delta[:, 4 * b + k, :], start=True, stop=True)
                last.then_inc(s["o_mm"], 1)
            keep_warm(10)
            def core_transposes(b):
                pe.wait_ge(s["core_dve"], b + 1)
                pe.wait_ge(s["core_act"], b + 1)
                transposes([(bank[3 + b][:, k * P:(k + 1) * P], core[:, 4 * b + k, :]) for k in range(4)], s["core_T"])

            def project_out(heads):
                pe.wait_ge(s["coreT_done"], heads[0] // 4 + 1)
                for h in heads:
                    last = nc.tensor.matmul(bank[0][:, 0:D], coreT[:, h, :], w_out[:, h, :], start=(h == 0), stop=(h == HV - 1))
                return last

            core_transposes(0)
            keep_warm(4)
            core_transposes(1)
            project_out(range(0, 4))
            last = project_out(range(4, HV))
            last.then_inc(s["out_mm"], 1)

            pe.wait_ge(s["h_done"], 1)
            transposes([(bank[1 + c][:, 0:P], half(hh, c)) for c in range(DC)], s["x2_T"])
            keep_warm(3)
            pe.wait_ge(s["x2_copied_dve"], 1)
            pe.wait_ge(s["x2_copied_act"], 1)
            wide(bank[1][:, D:D + E], lambda c: half(xT, c), lambda c: w_router[:, c, :]).then_inc(s["lg_mm"], 1)
            def gate_up(b, o, w):
                wide(bank[o + b][:, :], lambda c: half(xT, c), lambda c: w[:, c, 512 * b:512 * (b + 1)]).then_inc(s["gu_mm"], 1)

            def products(b):
                pe.wait_ge(s["prod_done"], 4 * b + 4)
                transposes([(bank[3 + b][:, k * P:(k + 1) * P], prod[:, 4 * b + k, :]) for k in range(4)], s["prod_T"])

            def downs(experts):
                pe.wait_ge(s["prodT_done"], experts[0] // 4 + 1)
                for e in experts:
                    last = nc.tensor.matmul(bank[0][:, 0:D], prodT[:, e, :], w_down[:, e, :], start=(e == 0), stop=(e == E - 1))
                return last

            gate_up(0, 3, w_gate)
            gate_up(0, 5, w_up)
            gate_up(1, 3, w_gate)
            products(0)
            gate_up(1, 5, w_up)
            downs(range(0, 3))
            products(1)
            downs(range(3, 4))
            last = downs(range(4, E))
            last.then_inc(s["moe_mm"], 1)

            keep_warm(9)
            pe.wait_ge(s["xf_done"], 1)
            transposes([(half(bank[1], c), half(xn, c)) for c in range(DC)], s["xf_T"])
            keep_warm(2)
            pe.wait_ge(s["xf_copied"], 1)
            for n in range(FC):
                last = wide(half(bank[3 + n // 2], n % 2), lambda c: rw1[:, c, n * P:(n + 1) * P], lambda c: half(xT, c))
                if n % 2:
                    last.then_inc(s["r1_mm"], 1)
            for n in range(FC):
                if n % 4 == 0:
                    pe.wait_ge(s["rel_dve"], n // 4 + 1)
                if n % 4 == 2:
                    pe.wait_ge(s["rel_act"], n // 4 + 1)
                last = nc.tensor.matmul(bank[0][:, D:D + E], relT[:, n, :], rw2[:, n, :], start=(n == 0), stop=(n == FC - 1))
            last.then_inc(s["sc_mm"], 1)

            def hidden(i, j):
                w1 = slots[j][:, 0:DC * FF].rearrange("p (c n) -> p c n", c=DC)
                pe.wait_ge(slot_in[j], slot_full(i, j))
                for b in range(2):
                    for k in range(4):
                        n = 4 * b + k
                        last = wide(bank[3 + 2 * (j % 2) + b][:, k * P:(k + 1) * P], lambda c: w1[:, c, n * P:(n + 1) * P], lambda c: half(xT, c))
                    last.then_inc(s["h_mm"], 1)

            def output(i, j):
                e = i * SLOTS + j
                pe.wait_ge(s["y_free"], e + 1)
                pe.wait_ge(s["w2_lo_pool"], e + 1)
                pe.wait_ge(s["w2_lo_dve"], e + 1)
                terms = [(n, a, b) for chunks in (range(4), range(4, FC)) for a, b in ((0, 0), (1, 0), (0, 1)) for n in chunks]
                for t, (n, a, b) in enumerate(terms):
                    if t % 12 == 0:
                        pe.wait_ge(s["h_lo_done"], e * 2 + (t // 12 + 3))
                    last = nc.tensor.matmul(bank[1 + j % 2][:, 0:D], hT[a][:, j % 2, n, :], w2[b][:, j % 2, n, :],
                                            start=(t == 0), stop=(t == len(terms) - 1))
                last.then_inc(s["y_mm"], 1)

            with pe.Fori(0, E // SLOTS) as i:
                hidden(i, 0)
                for j in range(SLOTS):
                    if j < SLOTS - 1:
                        hidden(i, j + 1)
                    output(i, j)
            pe.wait_ge(s["gate_done"], 1)
            nc.tensor.transpose(bank[7][0:E, 0:P], s_("gate"), ident).then_inc(s["gate_T"], 1)
            pe.wait_ge(s["gateT_done"], 1)
            nc.tensor.matmul(bank[0][:, 0:D], gateT[:, :], b2_sb[:, :], start=True, stop=True).then_inc(s["b2_mm"], 1)

        @block.scalar
        def _(act):
            chain = [0]

            def link(ins):
                chain[0] += 1
                ins.then_inc(s["act_chain"], 1)
                act.wait_ge(s["act_chain"], chain[0])

            act.wait_ge(s["eps_set"], 4)
            nc.scalar.activation(s_("spare", 0, 1), s_("eps", 3, 4), ACT.Sqrt).then_inc(s["act_chain"], 1)
            chain[0] += 1
            act.wait_ge(s["early_in"], 16)
            act.wait_ge(s["ln_var"], 1)
            nc.scalar.activation(s_("sd", 0, 1), s_("mv", 1, 2), ACT.Sqrt, bias=s_("eps", 0, 1)).then_inc(s["ln_sd"], 1)
            nc.scalar.activation(s_("negA"), early_at("A_log"), ACT.Exp)
            act.wait_ge(s["q_ready"], 1)
            a = EARLY["bq"][0]
            for m in range(DC):
                nc.scalar.activation(QT[:, m * P:(m + 1) * P], bank[5][:, m * P:(m + 1) * P], ACT.Identity,
                                     bias=E_sb[:, a + m:a + m + 1]).then_inc(s["q_done"], 1)

            def hi_parts(g, quads, first=False):
                if not first:
                    act.wait_ge(s["scores_ready"], g)
                for q in quads:
                    act.wait_ge(s["ctx_transposed"], g * 4 + (q + 1))
                    n = min(512, NC * P - 512 * q)
                    nc.scalar.activation(ctxT[0][:, 512 * q:512 * q + n], bank[CTX_BANKS[q]][:, 0:n], ACT.Copy).then_inc(s["ctxT_hi"], 1)

            def exps(g, b, first=False):
                act.wait_ge(s["max_ready"], g + 1)
                if not first:
                    act.wait_ge(s["probs_transposed"], g * 2)
                    act.wait_ge(s["acc_done"], g)
                nc.scalar.activation(probs[:, :].rearrange("p (z k) -> p z k", z=2), psum[:, 2:4, 0:HALF], ACT.Exp,
                                     bias=s_("nb"), accum_out=s_("rowsum", b, b + 1)).then_inc(s["exp_done"], 1)
                nc.scalar.activation(s_("al", b, b + 1), s_("dm", b, b + 1), ACT.Exp).then_inc(s["alpha_done"], 1)

            def ctx_hi_parts(g, r, first=False):
                if not first:
                    act.wait_ge(s["pv_done"], g - 1)
                nc.scalar.activation(ctxNv[0][:, r % 2], ring[:, r], ACT.Copy).then_inc(s["ctx_hi"], 1)

            def probs_hi_parts(g, first=False):
                if not first:
                    act.wait_ge(s["pv_done"], g)
                for q, tiles in ((0, 4), (1, 3)):
                    act.wait_ge(s["probs_transposed"], g * 2 + (q + 1))
                    nc.scalar.activation(probsT[0][:, 4 * q:4 * q + tiles, :], bank[4 + q][:, 0:tiles * P].rearrange("p (t q) -> p t q", q=T),
                                         ACT.Copy).then_inc(s["probsT_hi"], 1)

            hi_parts(0, range(4), first=True)
            ctx_hi_parts(0, 0, first=True)
            hi_parts(1, range(3))
            exps(0, 0, first=True)
            hi_parts(1, [3])
            probs_hi_parts(0, first=True)
            ctx_hi_parts(1, 1, first=True)
            with act.Fori(0, 3) as i:
                for j in range(RING):
                    g = i * RING + (j + 1)
                    hi_parts(g + 1, range(3))
                    exps(g, (j + 1) % 2)
                    hi_parts(g + 1, [3])
                    probs_hi_parts(g)
                    ctx_hi_parts(g + 1, (j + 2) % RING)
            exps(NG - 1, (NG - 1) % 2)
            probs_hi_parts(NG - 1)

            act.wait_ge(s["o_T"], 1)
            nc.scalar.activation(OT[:, :], bank[0][:, 0:D], ACT.Copy).then_inc(s["o_copied"], 1)
            act.wait_ge(s["var1_done"], 1)
            nc.scalar.activation(s_("sd", 1, 2), s_("mv", 1, 2), ACT.Sqrt, bias=s_("eps", 1, 2), scale=1.0 + RMS_EPS).then_inc(s["sd1_done"], 1)
            nc.scalar.activation(s_("sd", 0, 1), s_("mv", 1, 2), ACT.Sqrt, bias=s_("eps", 0, 1)).then_inc(s["sd1_done"], 1)
            act.wait_ge(s["xz_T"], 1)
            nc.scalar.activation(half(xT, 1), bank[6][:, 0:P], ACT.Copy, scale=s_("w1p", 1, 2)).then_inc(s["xz_copied_act"], 1)
            link(nc.scalar.activation(s_("spare", 1, 2), s_("eps", 3, 4), ACT.Exp))
            act.wait_ge(s["tables_in"], 16)
            act.wait_ge(s["u_ready"], 1)
            link(nc.scalar.activation(s_("au"), s_("u"), ACT.Abs))
            link(nc.scalar.activation(s_("sp"), s_("au"), ACT.Exp, scale=-1.0))
            nc.scalar.activation(s_("au"), s_("sp"), ACT.Ln, bias=s_("eps", 3, 4)).then_inc(s["ln1p_done"], 1)
            for i in range(2):
                act.wait_ge(s["proj_bank"], i + 1)
                for k in range(4):
                    n = 4 * CHANNELS[i] + k
                    last = nc.scalar.activation(qkvT[:, n, :], bank[1 + i][:, k * P:(k + 1) * P], ACT.Copy, scale=conv_w[:, n, 3:4])
                last.then_inc(s["tap0_done"], 1)
            for b in range(2):
                act.wait_ge(s["decay_done"], b + 1)
                nc.scalar.activation(DT[:, 4 * b:4 * b + 4, :], bank[0 if b == 0 else 7][:, :].rearrange("p (h t) -> p h t", h=4),
                                     ACT.Exp).then_inc(s["exp_decay"], 1)
            for i in range(2):
                act.wait_ge(s["conv_done"], i + 1)
                at = slice(4 * CHANNELS[i], 4 * CHANNELS[i] + 4)
                nc.scalar.activation(qkvT[:, at, :], qkvT[:, at, :], ACT.Silu).then_inc(s["silu_done"], 1)
                act.wait_ge(s["silu_done"], i + 1)
                nc.scalar.activation(squares[:, at, :], qkvT[:, at, :], ACT.Square).then_inc(s["sq_done"], 1)
                if i == 0:
                    nc.scalar.activation(s_("beta"), s_("ba", 0, HV), ACT.Tanh, scale=0.5).then_inc(s["beta_done"], 1)
                act.wait_ge(s["proj_bank"], 3 + i)
                nc.scalar.activation(rawv[:, 4 * i:4 * i + 4, :], bank[3 + i][:, :].rearrange("p (h t) -> p h t", h=4), ACT.Copy).then_inc(s["raw_v"], 1)
            for b in range(2):
                act.wait_ge(s["x_T"], b + 1)
                nc.scalar.activation(X[:, 4 * b:4 * b + 4, :], bank[3 + b][:, :].rearrange("p (h t) -> p h t", h=4), ACT.Copy).then_inc(s["x_init"], 1)

            def silu_v(b):
                act.wait_ge(s["conv_v"], b + 1)
                at = slice(2 * HK + 4 * b, 2 * HK + 4 * b + 4)
                nc.scalar.activation(qkvT[:, at, :], qkvT[:, at, :], ACT.Silu).then_inc(s["silu_done"], 1)

            def copy_x(lv):
                act.wait_ge(s["x_T"], 2 * lv + 1)
                nc.scalar.activation(X[:, 0:4, :], bank[3][:, :].rearrange("p (h t) -> p h t", h=4), ACT.Copy).then_inc(x_done[0], 1)

            silu_v(0)
            for lv in (1, 2, 3):
                copy_x(lv)
            silu_v(1)
            for b in range(2):
                act.wait_ge(s["z_done"], b + 1)
                nc.scalar.activation(zs[:, 4 * b:4 * b + 4, :], bank[5 + b][:, :].rearrange("p (h t) -> p h t", h=4), ACT.Silu).then_inc(s["zs_done"], 1)
            act.wait_ge(s["kn_in"], 1)
            link(nc.scalar.activation(s_("kn"), s_("n2", HK, 2 * HK), ACT.Sqrt, bias=s_("eps", 2, 3)))
            for lv in (4, 5):
                copy_x(lv)
            for b in range(2):
                act.wait_ge(s["vT_done"], 2 * b + 2)
                for k in range(4):
                    h = 4 * b + k
                    last = nc.scalar.activation(Bv[:, h, :], bank[5 + b][:, k * P:(k + 1) * P], ACT.Copy, scale=s_("kn", h // 2, h // 2 + 1))
                last.then_inc(s["bv_done"], 1)
            for b in range(2):
                act.wait_ge(s["delta_mm"], b + 1)
                nc.scalar.activation(delta[:, 4 * b:4 * b + 4, :], bank[3 + b][:, :].rearrange("p (h t) -> p h t", h=4), ACT.Copy).then_inc(s["delta_done"], 1)
            act.wait_ge(s["o_mm"], 1)
            nc.scalar.activation(squares[:, 0:4, :], bank[5][:, :].rearrange("p (h t) -> p h t", h=4), ACT.Square).then_inc(s["osq_done"], 1)
            act.wait_ge(s["o_mm"], 2)
            for k in range(4):
                last = nc.scalar.activation(squares[:, 4 + k, :], bank[6][:, k * P:(k + 1) * P], ACT.Square, accum_out=s_("ms", 4 + k, 5 + k))
            last.then_inc(s["osq_done"], 1)
            for b in range(2):
                act.wait_ge(s["ms_done"], b + 1)
                nc.scalar.activation(s_("f", 4 * b, 4 * b + 4), s_("ms", 4 * b, 4 * b + 4), ACT.Sqrt).then_inc(s["f_sd"], 1)
                act.wait_ge(s["f_done"], b + 1)
                for k in (2, 3):
                    h = 4 * b + k
                    last = nc.scalar.activation(core[:, h, :], core[:, h, :], ACT.Copy, scale=s_("f", h, h + 1))
                last.then_inc(s["core_act"], 1)
            for b in range(2):
                act.wait_ge(s["core_T"], b + 1)
                nc.scalar.activation(coreT[:, 4 * b:4 * b + 4, :], bank[3 + b][:, :].rearrange("p (h t) -> p h t", h=4), ACT.Copy,
                                     scale=early_at("gate_norm")).then_inc(s["coreT_done"], 1)
            act.wait_ge(s["h_done"], 1)
            act.wait_ge(s["x2_T"], 1)
            nc.scalar.activation(half(xT, 1), bank[2][:, 0:P], ACT.Copy, scale=s_("w2p", 1, 2)).then_inc(s["x2_copied_act"], 1)
            link(nc.scalar.activation(scratch[:, :], hh[:, :], ACT.Square, accum_out=s_("sd", 0, 1)))
            nc.scalar.activation(s_("sd", 1, 2), s_("sd", 0, 1), ACT.Sqrt, scale=1.0 / D, bias=s_("eps", 2, 3)).then_inc(s["hsd_done"], 1)
            act.wait_ge(s["th_in"], 1)
            nc.scalar.activation(s_("th"), s_("dm", 0, 1), ACT.Tanh, scale=0.5).then_inc(s["th_done"], 1)
            for b in range(2):
                act.wait_ge(s["x2_done"], 1)
                act.wait_ge(s["gu_mm"], 2 * b + 1)
                nc.scalar.activation(gact[:, 4 * b:4 * b + 4, :], bank[3 + b][:, :].rearrange("p (h t) -> p h t", h=4), ACT.Silu,
                                     scale=s_("rs", 0, 1)).then_inc(s["gact_done"], 1)
            for b in range(2):
                act.wait_ge(s["prod_T"], b + 1)
                nc.scalar.activation(prodT[:, 4 * b:4 * b + 4, :], bank[3 + b][:, :].rearrange("p (h t) -> p h t", h=4), ACT.Copy).then_inc(s["prodT_done"], 1)
            act.wait_ge(s["x3_done"], 1)
            nc.scalar.activation(s_("sd", 0, 1), s_("mv", 1, 2), ACT.Sqrt, bias=s_("eps", 0, 1)).then_inc(s["ln3_sd"], 1)
            a = EARLY["rb1"][0]
            for i in (1, 3):
                act.wait_ge(s["r1_mm"], i + 1)
                for n in (2 * i, 2 * i + 1):
                    last = nc.scalar.activation(relT[:, n, :], half(bank[3 + i], n % 2), ACT.Relu, bias=E_sb[:, a + n:a + n + 1])
                last.then_inc(s["rel_act"], 1)
            act.wait_ge(s["sc_in"], 1)
            nc.scalar.activation(s_("th"), s_("dm", 0, 1), ACT.Tanh, scale=0.5).then_inc(s["sc_th"], 1)
            a = EARLY["b1"][0]
            act.wait_ge(s["moe_mm"], 1)
            with act.Fori(0, E // SLOTS) as i:
                for j in range(SLOTS):
                    e = i * SLOTS + j
                    act.wait_ge(slot_in[j], slot_full(i, j))
                    act.wait_ge(s["y_mm"], e + 1)
                    nc.scalar.activation(w2[0][:, j % 2], slot_w2(j), ACT.Copy).then_inc(s["w2_hi_done"], 1)
                    act.wait_ge(s["h_mm"], e * 2 + 1)
                    act.wait_ge(s["h_lo_done"], e * 2 + 1)
                    for k in range(4):
                        last = nc.scalar.activation(h32[:, k, :], bank[3 + 2 * (j % 2)][:, k * P:(k + 1) * P], ACT.Relu,
                                                    bias=E_sb[:, bass.ds(i * (SLOTS * FC) + (a + j * FC + k), 1)])
                    last.then_inc(s["h_act"], 1)
                    act.wait_ge(s["h_act"], e + 1)
                    nc.scalar.activation(hT[0][:, j % 2, 0:4, :], h32[:, 0:4, :], ACT.Copy).then_inc(s["h_hi_done"], 1)
                    act.wait_ge(s["h_dve"], e + 1)
                    nc.scalar.activation(hT[0][:, j % 2, 4:8, :], h32[:, 4:8, :], ACT.Copy).then_inc(s["h_hi_done"], 1)
            act.wait_ge(s["gate_T"], 1)
            nc.scalar.activation(gateT[:, :], bank[7][0:E, 0:P], ACT.Copy).then_inc(s["gateT_done"], 1)

        @block.vector
        def _(dve):
            V = nc.vector
            chain = [0]

            def link(ins):
                chain[0] += 1
                ins.then_inc(s["dve_chain"], 1)
                dve.wait_ge(s["dve_chain"], chain[0])

            def moments(t):
                link(V.bn_stats(s_("stats"), t))
                return V.bn_aggr(s_("mv"), s_("stats"))

            def lo_parts(g, quads):
                for q in quads:
                    dve.wait_ge(s["ctxT_hi"], g * 4 + (q + 1))
                    n = min(512, NC * P - 512 * q)
                    at = slice(512 * q, 512 * q + n)
                    V.tensor_tensor(ctxT[1][:, at], bank[CTX_BANKS[q]][:, 0:n], ctxT[0][:, at], ALU.subtract).then_inc(s["ctxT_lo"], 1)

            V.memset(s_("marks", 0, 1), 0.0).then_inc(s["y_free"], 2)
            V.memset(s_("marks", 1, 2), 0.0).then_inc(s["y_mm"], 2)
            V.memset(s_("marks", 5, 6), 0.0).then_inc(s["h_lo_done"], 2)
            V.memset(s_("marks", 2, 3), 0.0).then_inc(s["acc_done"], 1)
            for j in range(EARLY_SLOTS):
                V.memset(s_("marks", 3 + j, 4 + j), 0.0).then_inc(slot_in[j], 1)
            dve.wait_ge(s["early_in"], 16)
            moments(x).then_inc(s["ln_var"], 1)
            dve.wait_ge(s["ln_sd"], 1)
            link(V.reciprocal(s_("rs", 0, 1), s_("sd", 0, 1)))
            V.tensor_scalar(xn[:, :], x, s_("mv", 0, 1), s_("rs", 0, 1), ALU.subtract, ALU.mult).then_inc(s["ln_xn"], 1)
            V.tensor_scalar(s_("w1p"), early_at("w_ln1"), 1.0, None, ALU.add).then_inc(s["dve_chain"], 1)
            V.tensor_scalar(s_("w2p"), early_at("w_ln2"), 1.0, None, ALU.add).then_inc(s["dve_chain"], 1)
            chain[0] += 2
            dve.wait_ge(s["ln_T"], 1)
            V.tensor_copy(xT[:, :], bank[4][:, 0:D]).then_inc(s["ln_xT"], 1)
            dve.wait_ge(s["bv_ready"], 1)
            V.tensor_tensor(xb[:, :], bank[3][:, 0:D], x, ALU.add).then_inc(s["g_done"], 1)
            lo_parts(0, range(2))
            dve.wait_ge(s["g_ready"], 1)
            V.tensor_copy(s_("qb"), bank[6][:, D:D + 1]).then_inc(s["g_done"], 1)
            link(V.tensor_copy(G[0][:, :], bank[6][:, 0:D]))
            V.tensor_tensor(G[1][:, :], bank[6][:, 0:D], G[0][:, :], ALU.subtract).then_inc(s["g_done"], 1)
            dve.wait_ge(s["g_done"], 3)
            dve.wait_ge(s["consts_set"], 4)

            def maxima(g, b):
                dve.wait_ge(s["scores_ready"], g + 1)
                V.tensor_reduce(s_("mx"), psum[:, 2:4, 0:HALF], mybir.AxisListType.XY, ALU.max).then_inc(s["mx_done"], 1)
                dve.wait_ge(s["mx_done"], g * 2 + 1)
                V.tensor_scalar(s_("M", 1 - b, 2 - b), s_("mx"), s_("qb"), s_("M", b, b + 1), ALU.add, ALU.max).then_inc(s["mx_done"], 1)
                dve.wait_ge(s["mx_done"], g * 2 + 2)
                V.tensor_tensor(s_("dm", b, b + 1), s_("M", b, b + 1), s_("M", 1 - b, 2 - b), ALU.subtract)
                V.tensor_tensor(s_("nb"), s_("qb"), s_("M", 1 - b, 2 - b), ALU.subtract).then_inc(s["max_ready"], 1)

            def accumulate(g, b):
                dve.wait_ge(s["pv_done"], g + 1)
                dve.wait_ge(s["acc_done"], g + 1)
                V.scalar_tensor_tensor(O[:, :], O[:, :], s_("al", b, b + 1), bank[6][:, 0:D], ALU.mult, ALU.add).then_inc(s["acc_done"], 1)

            def sums(g, b, first=False):
                dve.wait_ge(s["exp_done"], g + 1)
                dve.wait_ge(s["alpha_done"], g + 1)
                if not first:
                    dve.wait_ge(s["l_done"], g)
                V.scalar_tensor_tensor(s_("l"), s_("l"), s_("al", b, b + 1), s_("rowsum", b, b + 1), ALU.mult, ALU.add).then_inc(s["l_done"], 1)

            def probs_lo_parts(g):
                for q, tiles in ((0, 4), (1, 3)):
                    dve.wait_ge(s["probsT_hi"], g * 2 + (q + 1))
                    V.tensor_tensor(probsT[1][:, 4 * q:4 * q + tiles, :], bank[4 + q][:, 0:tiles * P].rearrange("p (t q) -> p t q", q=T),
                                    probsT[0][:, 4 * q:4 * q + tiles, :], ALU.subtract).then_inc(s["probsT_lo"], 1)

            lo_parts(0, [2, 3])
            maxima(0, 0)
            lo_parts(1, range(3))
            sums(0, 0, first=True)
            lo_parts(1, [3])
            probs_lo_parts(0)
            with dve.Fori(0, 3) as i:
                for j in range(RING):
                    g = i * RING + (j + 1)
                    maxima(g, (j + 1) % 2)
                    lo_parts(g + 1, range(3))
                    sums(g, (j + 1) % 2)
                    accumulate(i * RING + j, j % 2)
                    lo_parts(g + 1, [3])
                    probs_lo_parts(g)
            g = NG - 1
            maxima(g, g % 2)
            accumulate(g - 1, (g - 1) % 2)
            sums(g, g % 2)
            probs_lo_parts(g)
            accumulate(g, g % 2)

            dve.wait_ge(s["l_done"], NG)
            link(V.reciprocal(s_("rl"), s_("l")))
            link(V.tensor_scalar(s_("rl"), s_("rl"), NORM, None, ALU.mult))
            dve.wait_ge(s["att_ready"], 1)
            link(V.scalar_tensor_tensor(x1[:, :], bank[1][:, 0:D], s_("rl"), xb[:, :], ALU.mult, ALU.add))
            moments(x1[:, :]).then_inc(s["var1_done"], 1)
            dve.wait_ge(s["sd1_done"], 1)
            link(V.reciprocal(s_("rs", 1, 2), s_("sd", 1, 2)))
            V.tensor_scalar(xn[:, :], x1[:, :], s_("mv", 0, 1), s_("rs", 1, 2), ALU.subtract, ALU.mult).then_inc(s["xz_done"], 1)
            dve.wait_ge(s["sd1_done"], 2)
            link(V.reciprocal(s_("rs", 0, 1), s_("sd", 0, 1)))
            V.tensor_scalar(h0[:, :], x1[:, :], s_("mv", 0, 1), s_("rs", 0, 1), ALU.subtract, ALU.mult).then_inc(s["h0_done"], 1)
            dve.wait_ge(s["xz_T"], 1)
            V.tensor_scalar(half(xT, 0), bank[5][:, 0:P], s_("w1p", 0, 1), None, ALU.mult).then_inc(s["xz_copied_dve"], 1)
            dve.wait_ge(s["ba_done"], 1)
            V.tensor_copy(s_("ba"), bank[7][:, 0:2 * HV]).then_inc(s["ba_read"], 1)
            dve.wait_ge(s["ba_read"], 1)
            dve.wait_ge(s["tables_in"], 16)
            V.tensor_tensor(s_("u"), s_("ba", HV, 2 * HV), early_at("dt_bias"), ALU.add).then_inc(s["u_ready"], 1)

            dve.wait_ge(s["ln1p_done"], 1)
            link(V.scalar_tensor_tensor(s_("sp"), s_("u"), 0.0, s_("au"), ALU.max, ALU.add))
            V.scalar_tensor_tensor(s_("g"), s_("sp"), -1.0, s_("negA"), ALU.mult, ALU.mult).then_inc(s["rates_done"], 1)

            def taps(i):
                dve.wait_ge(s["tap0_done"], i + 1)
                for d in (1, 2, 3):
                    for k in range(4):
                        n = 4 * CHANNELS[i] + k
                        last = V.scalar_tensor_tensor(qkvT[:, n, d:T], bank[1 + i][:, k * P:(k + 1) * P - d], conv_w[:, n, 3 - d:4 - d],
                                                      qkvT[:, n, d:T], ALU.mult, ALU.add)
                        last.then_inc(s["conv_done" if d == 3 and k == 3 else "dve_chain"], 1)
                    chain[0] += 4 if d < 3 else 3
                    dve.wait_ge(s["dve_chain"], chain[0])

            taps(0)
            taps(1)
            dve.wait_ge(s["beta_done"], 1)
            link(V.tensor_scalar(s_("beta"), s_("beta"), 0.5, 0.5, ALU.mult, ALU.add))
            dve.wait_ge(s["n2_done"], 1)
            V.tensor_copy(s_("n2", HK, 2 * HK), bank[0][:, HK:2 * HK]).then_inc(s["kn_in"], 1)
            dve.wait_ge(s["kn_in"], 1)
            link(V.tensor_scalar(s_("ki"), s_("n2", HK, 2 * HK), RMS_EPS, None, ALU.add))
            link(V.reciprocal(s_("ki"), s_("ki")))
            link(V.tensor_tensor(s_("kap").rearrange("p (k r) -> p k r", r=2), s_("beta").rearrange("p (k r) -> p k r", r=2),
                                 s_("ki").rearrange("p (k r) -> p k r", r=1).to_broadcast([P, HK, 2]), ALU.mult))
            dve.wait_ge(s["y_ident"], 1)
            for b in range(2):
                dve.wait_ge(s["dt_done"], b + 1)
                dve.wait_ge(s["gram_done"], b + 1)
                for k in range(4):
                    h = 4 * b + k
                    kh = h // 2
                    last = V.scalar_tensor_tensor(AW[:, h, :, :],
                                                  bank[1 + kh // 2][:, (kh % 2) * 256:(kh % 2) * 256 + 256].rearrange("p (a t) -> p a t", a=2),
                                                  s_("kap", h, h + 1), DT[:, h:h + 1, :].to_broadcast([P, 2, P]), ALU.mult, ALU.mult)
                    last.then_inc(s["aw_done"], 1)
                dve.wait_ge(s["aw_done"], 4 * b + 4)
                odd = AW[:, 4 * b:4 * b + 4, 0, :].rearrange("p h (n z) -> p h n z", z=2)[:, :, :, 1]
                tmp = delta[:, 4 * b:4 * b + 4, 0:64]
                link(V.scalar_tensor_tensor(tmp, odd, -1.0, m0.rearrange("p (a t) -> p a t", a=1).to_broadcast([P, 4, 64]), ALU.mult, ALU.mult))
                yo = Y[:, 4 * b:4 * b + 4, :].rearrange("p h (n z) -> p h n z", z=2)[:, :, :, 1]
                V.tensor_tensor(yo, yo, tmp, ALU.add).then_inc(s["y_init"], 1)

            dve.wait_ge(s["n2_done"], 2)
            V.tensor_scalar(s_("eq"), bank[0][:, 0:HK], P * RMS_EPS, P * RMS_EPS * RMS_EPS, ALU.mult, ALU.add).then_inc(s["n2_read"], 1)
            dve.wait_ge(s["n2_read"], 1)
            dve.wait_ge(s["y_init"], 2)
            dve.wait_ge(s["x_init"], 2)
            for lv in range(1, LEVELS):
                bs = 2 ** lv
                st = steps[lv % 2]

                def first(t, b, z):
                    return t[:, 4 * b:4 * b + 4, :].rearrange("p h (n z w) -> p h n z w", z=2, w=bs)[:, :, :, z, :]

                def four(t):
                    return t.rearrange("p (h n w) -> p h n w", h=4, w=bs)

                for b in range(2):
                    dve.wait_ge(s["t_mm"], 2 * (lv - 1) + b + 1)
                    dve.wait_ge(s["steps_zeroed"], max(2, lv))
                    t = bank[0 if b == 0 else 7][:, 0:256]
                    if lv < BLOCK_LEVEL:
                        m = masks[:, lv - 1:lv, :].to_broadcast([P, 4, 64]).rearrange("p h (n w) -> p h n w", w=bs)
                        last = V.tensor_tensor(first(st, b, 0), four(t), m, ALU.mult)
                    else:
                        for i, (one, two) in enumerate(block_pairs(bs)):
                            last = V.tensor_copy(st[two, 4 * b:4 * b + 4, one], t.rearrange("p (h c) -> p h c", h=4)[two, :, i * bs:(i + 1) * bs])
                    last.then_inc(s["t_done"], 1)
                for b in range(2):
                    dve.wait_ge(s["ty_mm"], 2 * (lv - 1) + b + 1)
                    t = bank[1 + b][:, 0:256]
                    if lv < BLOCK_LEVEL:
                        last = V.tensor_tensor(first(Y, b, 1), first(Y, b, 1), four(t), ALU.subtract)
                    else:
                        for i, (one, two) in enumerate(block_pairs(bs)):
                            y = Y[one, 4 * b:4 * b + 4, two]
                            last = V.tensor_tensor(y, y, t.rearrange("p (h c) -> p h c", h=4)[one, :, i * bs:(i + 1) * bs], ALU.subtract)
                    last.then_inc(s["y_done"], 1)
                if lv < LEVELS - 1:
                    dve.wait_ge(s["x_T"], 2 * lv + 2)
                    V.tensor_copy(X[:, 4:8, :], bank[4][:, :].rearrange("p (h t) -> p h t", h=4)).then_inc(x_done[1], 1)

            dve.wait_ge(s["zs_done"], 2)
            for b in range(2):
                dve.wait_ge(s["osq_done"], b + 1)
                if b == 0:
                    link(V.tensor_reduce(s_("ms", 0, 4), squares[:, 0:4, :], AX, ALU.add))
                ms = s_("ms", 4 * b, 4 * b + 4).rearrange("p (k r) -> p k r", r=2)
                V.scalar_tensor_tensor(ms, ms, 1.0 / P, s_("eq", 2 * b, 2 * b + 2).rearrange("p (k r) -> p k r", r=1).to_broadcast([P, 2, 2]),
                                       ALU.mult, ALU.add).then_inc(s["ms_done"], 1)
                V.tensor_tensor(core[:, 4 * b:4 * b + 4, :], bank[5 + b][:, :].rearrange("p (h t) -> p h t", h=4), zs[:, 4 * b:4 * b + 4, :],
                                ALU.mult).then_inc(s["zo_done"], 1)
                dve.wait_ge(s["f_sd"], b + 1)
                dve.wait_ge(s["zo_done"], b + 1)
                V.reciprocal(s_("f", 4 * b, 4 * b + 4), s_("f", 4 * b, 4 * b + 4)).then_inc(s["f_done"], 1)
                dve.wait_ge(s["f_done"], b + 1)
                for k in range(2):
                    h = 4 * b + k
                    last = V.tensor_scalar(core[:, h, :], core[:, h, :], s_("f", h, h + 1), None, ALU.mult)
                    if k == 0:
                        last.then_inc(s["dve_chain"], 1)
                last.then_inc(s["core_dve"], 1)
                chain[0] += 1
            dve.wait_ge(s["h0_done"], 1)
            dve.wait_ge(s["out_mm"], 1)
            V.tensor_tensor(hh[:, :], bank[0][:, 0:D], h0[:, :], ALU.add).then_inc(s["h_done"], 1)
            dve.wait_ge(s["h_done"], 1)
            dve.wait_ge(s["x2_T"], 1)
            V.tensor_scalar(half(xT, 0), bank[1][:, 0:P], s_("w2p", 0, 1), None, ALU.mult).then_inc(s["x2_copied_dve"], 1)
            dve.wait_ge(s["hsd_done"], 1)
            V.reciprocal(s_("rs", 0, 1), s_("sd", 1, 2)).then_inc(s["x2_done"], 1)
            dve.wait_ge(s["x2_done"], 1)
            link(V.tensor_tensor(xh[:, :], x1[:, :], hh[:, :], ALU.add))

            def gates(out, half_tanh, tanh_done, scale):
                link(V.max(s_("top"), s_("lg")))
                link(V.max_index(topi[:, :], s_("top"), s_("lg")))
                V.tensor_scalar(s_("dm", 0, 1), s_("top", 0, 1), s_("top", 1, 2), scale, ALU.subtract, ALU.mult).then_inc(s[half_tanh], 1)
                link(V.tensor_copy(s_("idf"), topi[:, :]))
                link(V.tensor_scalar(s_("e1"), early_at("iota"), s_("idf", 0, 1), None, ALU.is_equal))
                link(V.tensor_scalar(s_("e2"), early_at("iota"), s_("idf", 1, 2), None, ALU.is_equal))
                dve.wait_ge(s[tanh_done], 1)
                link(V.tensor_scalar(s_("w", 0, 1), s_("th"), 0.5, 0.5, ALU.mult, ALU.add))
                link(V.tensor_scalar(s_("w", 1, 2), s_("th"), -0.5, 0.5, ALU.mult, ALU.add))
                link(V.tensor_scalar(s_("e1"), s_("e1"), s_("w", 0, 1), None, ALU.mult))
                return V.scalar_tensor_tensor(out, s_("e2"), s_("w", 1, 2), s_("e1"), ALU.mult, ALU.add)

            dve.wait_ge(s["lg_mm"], 1)
            link(V.tensor_copy(s_("lg"), bank[1][:, D:D + E]))
            link(gates(s_("route"), "th_in", "th_done", s_("rs", 0, 1)))
            link(V.tensor_scalar(s_("route"), s_("route"), s_("rs", 0, 1), None, ALU.mult))
            for b in range(2):
                dve.wait_ge(s["gact_done"], b + 1)
                dve.wait_ge(s["gu_mm"], 2 * b + 2)
                for k in range(4):
                    e = 4 * b + k
                    V.scalar_tensor_tensor(prod[:, e, :], gact[:, e, :], s_("route", e, e + 1), bank[5 + b][:, k * P:(k + 1) * P], ALU.mult, ALU.mult)\
                        .then_inc(s["prod_done"], 1)
            dve.wait_ge(s["moe_mm"], 1)
            link(V.tensor_tensor(O[:, :], bank[0][:, 0:D], xh[:, :], ALU.add))
            moments(O[:, :]).then_inc(s["x3_done"], 1)
            dve.wait_ge(s["ln3_sd"], 1)
            link(V.reciprocal(s_("rs", 0, 1), s_("sd", 0, 1)))
            V.tensor_scalar(xn[:, :], O[:, :], s_("mv", 0, 1), s_("rs", 0, 1), ALU.subtract, ALU.mult).then_inc(s["xf_done"], 1)
            dve.wait_ge(s["xf_T"], 1)
            V.tensor_copy(xT[:, :], bank[1][:, 0:D]).then_inc(s["xf_copied"], 1)
            a = EARLY["rb1"][0]
            for i in (0, 2):
                dve.wait_ge(s["r1_mm"], i + 1)
                for n in (2 * i, 2 * i + 1):
                    last = V.tensor_scalar(relT[:, n, :], half(bank[3 + i], n % 2), E_sb[:, a + n:a + n + 1], 0.0, ALU.add, ALU.max)
                last.then_inc(s["rel_dve"], 1)
            dve.wait_ge(s["sc_mm"], 1)
            link(V.tensor_tensor(s_("lg"), bank[0][:, D:D + E], early_at("rb2"), ALU.add))
            gates(s_("gate"), "sc_in", "sc_th", 1.0).then_inc(s["gate_done"], 1)
            dve.wait_ge(s["gate_done"], 1)
            a = EARLY["b1"][0]
            gcol = smalls["gate"][0]

            def add_output(i, j):
                e = i * SLOTS + j
                dve.wait_ge(s["y_mm"], e + 3)
                dve.wait_ge(s["y_free"], e + 2)
                V.scalar_tensor_tensor(O[:, :], bank[1 + j % 2][:, 0:D], sm[:, bass.ds(i * SLOTS + (gcol + j), 1)], O[:, :], ALU.mult, ALU.add)\
                    .then_inc(s["y_free"], 1)

            with dve.Fori(0, E // SLOTS) as i:
                for j in range(SLOTS):
                    e = i * SLOTS + j
                    at = slice(POOL_CHUNKS, FC)
                    dve.wait_ge(s["w2_hi_done"], e + 1)
                    V.tensor_tensor(w2[1][:, j % 2, at], slot_w2(j)[:, at], w2[0][:, j % 2, at], ALU.subtract).then_inc(s["w2_lo_dve"], 1)
                    dve.wait_ge(s["h_mm"], e * 2 + 2)
                    dve.wait_ge(s["h_lo_done"], e * 2 + 2)
                    for k in range(4, FC):
                        last = V.tensor_scalar(h32[:, k, :], bank[4 + 2 * (j % 2)][:, (k - 4) * P:(k - 3) * P],
                                               E_sb[:, bass.ds(i * (SLOTS * FC) + (a + j * FC + k), 1)], 0.0, ALU.add, ALU.max)
                    last.then_inc(s["h_dve"], 1)
                    for b in range(2):
                        at = slice(4 * b, 4 * b + 4)
                        dve.wait_ge(s["h_hi_done"], e * 2 + (b + 1))
                        V.tensor_tensor(hT[1][:, j % 2, at, :], h32[:, at, :], hT[0][:, j % 2, at, :], ALU.subtract).then_inc(s["h_lo_done"], 1)
                    if j > 0:
                        add_output(i, j - 1)
                add_output(i, SLOTS - 1)
            dve.wait_ge(s["y_free"], E + 2)
            dve.wait_ge(s["b2_mm"], 1)
            V.tensor_tensor(O[:, :], bank[0][:, 0:D], O[:, :], ALU.add).then_inc(s["out_ready"], 1)


def _chunks(w):
    k, n = w.shape
    return w.reshape(k // P, P, n).transpose(1, 0, 2).reshape(P, -1)


def _constants():
    import numpy as np
    s, t = np.arange(P)[:, None], np.arange(P)[None, :]
    out = {
        "ident": (s == t), "tri": (s <= t), "strict": (s > t),
        "m0": (s == 2 * np.arange(P // 2)[None, :]),
        "iota": np.broadcast_to(np.arange(E), (P, E)), "ones": np.ones((P, 1)),
    }
    masks = []
    for lv in range(1, BLOCK_LEVEL):
        b = 2 ** lv
        col = np.arange(64)[None, :]
        masks.append((s // (2 * b) == col // b) & (s % (2 * b) >= b))
    out["masks"] = np.concatenate(masks, axis=1)
    return {k: v.astype(np.float32) for k, v in out.items()}


def kernel(**inputs):
    import numpy as np
    import concourse.bacc as bacc
    from concourse.bass_utils import run_bass_kernel_spmd

    a = {k: np.asarray(v) for k, v in inputs.items()}
    c = _constants()

    def rows(v):
        return np.broadcast_to(v[None, :], (P, v.shape[0]))

    def cols(v):
        return v.reshape(-1, P).T

    e = dict(c)
    e.update({
        "x": a["x"][0],
        "conv_w": a["L0_attn_conv_w"].reshape(NCH, P, 4).transpose(1, 0, 2).reshape(P, -1),
        "w_ln1": cols(a["L0_attn_w_ln1"]), "w_ln2": cols(a["L0_attn_w_ln2"]), "gate_norm": cols(a["L0_attn_gate_norm_w"]),
        "bq": cols(a["L0_xattn_bq"]), "bk": cols(a["L0_xattn_bk"]), "rb1": cols(a["L0_ffn_rb1"]),
        "b1": a["L0_ffn_b1"].reshape(E * FC, P).T,
        "dt_bias": rows(a["L0_attn_dt_bias"]), "A_log": rows(a["L0_attn_A_log"]), "rb2": rows(a["L0_ffn_rb2"]),
        "wq": _chunks(a["L0_xattn_Wq"]), "wkT": _chunks(a["L0_xattn_Wk"].T), "wv": _chunks(a["L0_xattn_Wv"]),
    })
    early = np.concatenate([e[name] for name in EARLY], axis=1)

    def by_input(w):
        return w.transpose(1, 0, 2).reshape(w.shape[1], -1)

    w1, w2 = a["L0_ffn_W1"], a["L0_ffn_W2"]
    experts = np.stack([np.concatenate([_chunks(w1[k]), _chunks(w2[k])], axis=1) for k in range(E)])
    late = {
        "qkvz": _chunks(a["L0_attn_W_qkvz"]), "ba": _chunks(a["L0_attn_W_ba"]), "out": _chunks(a["L0_attn_W_out"]),
        "gate": _chunks(by_input(a["L0_attn_W_gate_e"])), "up": _chunks(by_input(a["L0_attn_W_up_e"])),
        "down": a["L0_attn_W_down_e"].transpose(1, 0, 2).reshape(P, -1), "router": _chunks(a["L0_attn_W_router"]),
        "rw1": _chunks(a["L0_ffn_rw1"]), "rw2": _chunks(a["L0_ffn_rw2"]),
    }
    late = np.concatenate([late[name] for name in LATE] + [experts[k] for k in range(EARLY_SLOTS)], axis=1)
    late = np.pad(late, ((0, 0), (0, LATE_N - late.shape[1])))
    late = late.reshape(P, LATE_PARTS, PART_N).transpose(1, 0, 2)

    nc = bacc.Bacc("TRN2", target_bir_lowering=False, num_devices=1)
    arrays = {"early": early, "late": late, "experts": experts[EARLY_SLOTS:], "ctx": a["ctx_1024"][0],
              "bv": a["L0_xattn_bv"].reshape(1, D), "b2": a["L0_ffn_b2"]}
    arrays = {f"in_{k}": np.ascontiguousarray(v) for k, v in arrays.items()}
    args = [nc.dram_tensor(k, v.shape, mybir.dt.from_np(v.dtype), kind="ExternalInput").ap() for k, v in arrays.items()]
    args.append(nc.dram_tensor("out_0", (1, T, D), F32, kind="ExternalOutput").ap().rearrange("b t d -> (b t) d"))
    perceiver(nc, *args)
    r = run_bass_kernel_spmd(nc, [arrays], core_ids=[0])
    return r.results[0]["out_0"]
```
